# Optimizing a Trainium2 kernel written in Bass

```python
import numpy as np
import jax
import jax.numpy as jnp

def _softmax(x, axis=-1):
    return jax.nn.softmax(x, axis=axis)

def _gelu(x):
    return jax.nn.gelu(x, approximate=True)

def _silu(x):
    return jax.nn.silu(x)

def _sigmoid(x):
    return jax.nn.sigmoid(x)

def _layernorm(x, axis=-1, eps=1e-05):
    m = jnp.mean(x, axis=axis, keepdims=True)
    v = jnp.var(x, axis=axis, keepdims=True)
    return (x - m) / jnp.sqrt(v + eps)

def _scatter_add(tgt, idx, src, axis=0):
    return tgt.at[idx].add(src)

def _segment_sum(src, seg, n):
    return jax.ops.segment_sum(src, seg, n)
kernel_name = 'mk_seq_postln_d1_jaxref_r8_0b10b1'

def setup_inputs(seed: int=0):
    np.random.seed(seed)
    _w = jnp.asarray

    def _L0_attn_setup():
        import jax, jax.numpy as jnp
        import numpy as np
        DIM = 128
        HEADS = 16
        DIM_HEAD = 64
        key = jax.random.key(seed)
        ks = jax.random.split(key, 6)
        inner = HEADS * DIM_HEAD
        s = lambda fan_in: 1.0 / np.sqrt(fan_in)
        return {'x': jax.random.normal(ks[0], (4, 512, DIM), dtype=jnp.float32), 'W_qkv': jax.random.normal(ks[1], (DIM, inner * 3), dtype=jnp.float32) * s(DIM), 'W_f': jax.random.normal(ks[2], (DIM_HEAD, DIM_HEAD), dtype=jnp.float32) * s(DIM_HEAD), 'b_f': jax.random.normal(ks[3], (DIM_HEAD,), dtype=jnp.float32) * 0.01, 'W_out': jax.random.normal(ks[4], (inner, DIM), dtype=jnp.float32) * s(inner), 'b_out': jax.random.normal(ks[5], (DIM,), dtype=jnp.float32) * 0.01}
    _L0_attn_in = _L0_attn_setup()

    def _L0_ffn_setup():
        import jax, jax.numpy as jnp
        import numpy as np
        D_MODEL = 128
        EXPANSION = 4
        D_HIDDEN = D_MODEL * EXPANSION
        NUM_STAGES = int(np.log2(D_HIDDEN))

        def butterfly(y, weights, dim):
            lead = y.shape[:-1]
            for stage in range(weights.shape[0]):
                s = 2 ** stage
                nb = dim // (2 * s)
                yr = y.reshape(*lead, nb, 2, s)
                a = yr[..., 0, :]
                b = yr[..., 1, :]
                w = weights[stage].reshape(nb, s, 2, 2)
                na = w[..., 0, 0] * a + w[..., 0, 1] * b
                nb2 = w[..., 1, 0] * a + w[..., 1, 1] * b
                y = jnp.stack([na, nb2], axis=-2).reshape(*lead, dim)
            return y
        key = jax.random.key(seed)
        ks = jax.random.split(key, 6)
        B, S = (4, 256)
        x = jax.random.normal(ks[0], (B, S, D_MODEL), jnp.float32)
        W_exp = jax.random.normal(ks[1], (D_MODEL, D_HIDDEN), jnp.float32) * 0.02
        b_exp = jnp.zeros((D_HIDDEN,), jnp.float32)
        up_weights = jax.random.normal(ks[2], (NUM_STAGES, D_HIDDEN // 2, 2, 2), jnp.float32) * 0.02
        up_bias = jnp.zeros((D_HIDDEN,), jnp.float32)
        down_weights = jax.random.normal(ks[3], (NUM_STAGES, D_HIDDEN // 2, 2, 2), jnp.float32) * 0.02
        W_con = jax.random.normal(ks[4], (D_HIDDEN, D_MODEL), jnp.float32) * 0.02
        b_con = jnp.zeros((D_MODEL,), jnp.float32)
        down_bias = jnp.zeros((D_MODEL,), jnp.float32)
        return dict(x=x, W_exp=W_exp, b_exp=b_exp, up_weights=up_weights, up_bias=up_bias, down_weights=down_weights, W_con=W_con, b_con=b_con, down_bias=down_bias)
    _L0_ffn_in = _L0_ffn_setup()
    _d = {'L0_attn_x': _L0_attn_in['x'], 'L0_attn_W_qkv': _L0_attn_in['W_qkv'], 'L0_attn_W_f': _L0_attn_in['W_f'], 'L0_attn_b_f': _L0_attn_in['b_f'], 'L0_attn_W_out': _L0_attn_in['W_out'], 'L0_attn_b_out': _L0_attn_in['b_out'], 'L0_ffn_W_exp': _L0_ffn_in['W_exp'], 'L0_ffn_b_exp': _L0_ffn_in['b_exp'], 'L0_ffn_up_weights': _L0_ffn_in['up_weights'], 'L0_ffn_up_bias': _L0_ffn_in['up_bias'], 'L0_ffn_down_weights': _L0_ffn_in['down_weights'], 'L0_ffn_W_con': _L0_ffn_in['W_con'], 'L0_ffn_b_con': _L0_ffn_in['b_con'], 'L0_ffn_down_bias': _L0_ffn_in['down_bias']}
    _x0 = _d['L0_attn_x']
    _d['L0_attn_x'] = jax.random.normal(jax.random.fold_in(jax.random.key(seed), 1), (4, 1024, 128), dtype=_x0.dtype)
    del _x0
    return _d

def reference(L0_attn_x, L0_attn_W_qkv, L0_attn_W_f, L0_attn_b_f, L0_attn_W_out, L0_attn_b_out, L0_ffn_W_exp, L0_ffn_b_exp, L0_ffn_up_weights, L0_ffn_up_bias, L0_ffn_down_weights, L0_ffn_W_con, L0_ffn_b_con, L0_ffn_down_bias):

    def _L0_attn_ref(x, W_qkv, W_f, b_f, W_out, b_out):
        import jax, jax.numpy as jnp
        import numpy as np
        DIM = 128
        HEADS = 16
        DIM_HEAD = 64
        B, N, C = x.shape
        H, D = (HEADS, DIM_HEAD)
        qkv = x @ W_qkv
        q, k, v = jnp.split(qkv, 3, axis=-1)
        reshape = lambda t: t.reshape(B, N, H, D).transpose(0, 2, 1, 3)
        q, k, v = (reshape(q), reshape(k), reshape(v))
        fmap = lambda t: jax.nn.relu(t @ W_f + b_f)
        q = fmap(q)
        k = fmap(k)
        kv = jnp.einsum('bhnd,bhne->bhde', k, v)
        out = jnp.einsum('bhnd,bhde->bhne', q, kv)
        k_sum = k.sum(axis=2)
        normalizer = jnp.einsum('bhnd,bhd->bhn', q, k_sum)
        out = out / (normalizer[..., None] + 1e-06)
        out = out.transpose(0, 2, 1, 3).reshape(B, N, H * D)
        return out @ W_out + b_out

    def _L0_ffn_ref(x, W_exp, b_exp, up_weights, up_bias, down_weights, W_con, b_con, down_bias):
        import jax, jax.numpy as jnp
        import numpy as np
        D_MODEL = 128
        EXPANSION = 4
        D_HIDDEN = D_MODEL * EXPANSION
        NUM_STAGES = int(np.log2(D_HIDDEN))

        def butterfly(y, weights, dim):
            lead = y.shape[:-1]
            for stage in range(weights.shape[0]):
                s = 2 ** stage
                nb = dim // (2 * s)
                yr = y.reshape(*lead, nb, 2, s)
                a = yr[..., 0, :]
                b = yr[..., 1, :]
                w = weights[stage].reshape(nb, s, 2, 2)
                na = w[..., 0, 0] * a + w[..., 0, 1] * b
                nb2 = w[..., 1, 0] * a + w[..., 1, 1] * b
                y = jnp.stack([na, nb2], axis=-2).reshape(*lead, dim)
            return y
        h = jnp.einsum('bsd,dh->bsh', x, W_exp) + b_exp
        h = butterfly(h, up_weights, D_HIDDEN)
        h = jax.nn.gelu(h + up_bias, approximate=False)
        h = butterfly(h, down_weights, D_HIDDEN)
        y = jnp.einsum('bsh,hd->bsd', h, W_con) + b_con
        return y + down_bias
    x = L0_attn_x
    x = _layernorm(x + _L0_attn_ref(x, L0_attn_W_qkv, L0_attn_W_f, L0_attn_b_f, L0_attn_W_out, L0_attn_b_out), axis=-1)
    x = _layernorm(x + _L0_ffn_ref(x, L0_ffn_W_exp, L0_ffn_b_exp, L0_ffn_up_weights, L0_ffn_up_bias, L0_ffn_down_weights, L0_ffn_W_con, L0_ffn_b_con, L0_ffn_down_bias), axis=-1)
    return x

_drawn_inputs = setup_inputs


def setup_inputs(seed=0):
    import zlib

    import numpy as np

    out = dict(_drawn_inputs(seed))
    spreads = {'L0_ffn_b_exp': (0.0, 0.1),
     'L0_ffn_up_bias': (0.0, 0.1),
     'L0_ffn_b_con': (0.0, 0.1),
     'L0_ffn_down_bias': (0.0, 0.1)}
    factors = {'L0_attn_b_f': 8.0, 'L0_attn_b_out': 4.83}
    for name, (base, spread) in spreads.items():
        noise = np.random.default_rng([zlib.crc32(name.encode()), seed]).standard_normal(out[name].shape)
        drawn = base * np.exp(spread * noise) if base else spread * noise
        out[name] = jnp.asarray(drawn.astype(out[name].dtype))
    for name, factor in factors.items():
        out[name] = (out[name] * factor).astype(out[name].dtype)
    return out
```

```python
import concourse.bass as bass
from concourse import mybir
from contextlib import ExitStack


def postln_linear_attention_butterfly_ffn_kernel(
    nc: bass.Bass,
    x: bass.AP,
    W_qkv: bass.AP,
    W_f: bass.AP,
    b_f: bass.AP,
    W_out: bass.AP,
    b_out: bass.AP,
    W_exp: bass.AP,
    b_exp: bass.AP,
    up_weights: bass.AP,
    up_bias: bass.AP,
    down_weights: bass.AP,
    W_con: bass.AP,
    b_con: bass.AP,
    down_bias: bass.AP,
    out: bass.AP,
):
    fp32 = mybir.dt.float32
    fp32r = mybir.dt.float32r
    ALU = mybir.AluOpType
    ACT = mybir.ActivationFunctionType

    BATCH, N, C = x.shape
    D = W_f.shape[0]
    HD = W_out.shape[0]
    HID = W_exp.shape[1]
    STAGES = up_weights.shape[0]
    PAIRS = HD // 128
    TILES = N // 128
    CH = 512
    CHUNKS = N // CH
    STEPS = CHUNKS * PAIRS
    QUADS = CH // 128
    HT = HID // 128
    ALLCH = BATCH * CHUNKS
    SUMS = TILES - 1
    NORM_EPS = 1e-6
    LN_EPS = 1e-5

    xs_view = x.rearrange("b (t p) c -> b p t c", p=128)
    out_view = out.rearrange("b (h t p) c -> (b h) p t c", p=128, h=CHUNKS)

    ctx = ExitStack()
    with ctx:
        def sb(name, shape, dt=fp32):
            return ctx.enter_context(nc.sbuf_tensor(name, shape, dt))

        def pb(name, shape):
            return ctx.enter_context(nc.psum_tensor(name, shape, fp32))

        def sem(name):
            return ctx.enter_context(nc.semaphore(name))

        wq_h = sb("wq_h", [128, PAIRS, 128], fp32r)
        wq_l = sb("wq_l", [128, PAIRS, 128], fp32r)
        wk_h = sb("wk_h", [128, HD], fp32r)
        wk_l = sb("wk_l", [128, HD], fp32r)
        vo = sb("vo", [128, 2 * PAIRS, 128])
        wup_h = sb("wup_h", [128, HID], fp32r)
        wup_l = sb("wup_l", [128, HID], fp32r)
        wdn_h = sb("wdn_h", [128, HT, 128], fp32r)
        wdn_l = sb("wdn_l", [128, HT, 128], fp32r)
        wf_diag = sb("wf_diag", [128, 128])
        ident = sb("ident", [128, 128])
        ones = sb("ones", [128, 1])
        head_mask = sb("head_mask", [128, PAIRS, 32])
        select = sb("select", [128, 4, 8, 64], fp32r)
        part_b = sb("part_b", [128, 1])
        bf_col = sb("bf_col", [128, 1])
        bf_row = sb("bf_row", [128, D])
        bout_col = sb("bout_col", [128, 1])
        bup_raw = sb("bup_raw", [128, HT])
        bup_col = sb("bup_col", [128, HT])
        bcon_col = sb("bcon_col", [128, 1])
        bdn_raw = sb("bdn_raw", [128, 1])
        bdn_col = sb("bdn_col", [128, 1])
        ln_eps = sb("ln_eps", [128, 1])
        scratch = sb("scratch", [128, 1])
        minus_half = sb("minus_half", [128, 1])
        xs = sb("xs", [128, TILES, C])
        x_res = sb("x_res", [128, TILES, C])
        x_h = sb("x_h", [128, TILES, C], fp32r)
        x_l = sb("x_l", [128, TILES, C], fp32r)
        xT_h = sb("xT_h", [128, N], fp32r)
        xT_l = sb("xT_l", [128, N], fp32r)
        q = sb("q", [128, PAIRS, N])
        k = sb("k", [128, 2, HD])
        k_h = sb("k_h", [128, 2, HD], fp32r)
        k_l = sb("k_l", [128, 2, HD], fp32r)
        k_total = sb("k_total", [128, HD])
        kx = sb("kx", [128, HD])
        ksum_cols = sb("ksum_cols", [128, PAIRS, 32])
        m_h = sb("m_h", [128, PAIRS, C], fp32r)
        m_l = sb("m_l", [128, PAIRS, C], fp32r)
        norm = sb("norm", [128, CH])
        recip = sb("recip", [128, CH])
        recip_h = sb("recip_h", [128, CH], fp32r)
        recip_parts = sb("recip_parts", [128, CH], fp32r)
        qn = sb("qn", [128, 2, CH])
        qn_h = sb("qn_h", [128, 4, CH], fp32r)
        qn_l = sb("qn_l", [128, 4, CH], fp32r)
        attnT = sb("attnT", [128, CH])
        x1_pre = sb("x1_pre", [128, QUADS, C])
        x1 = sb("x1", [128, QUADS, C])
        x1T = sb("x1T", [128, BATCH * N])
        stats = sb("stats", [128, QUADS, 6])
        mean_var = sb("mean_var", [128, QUADS, 2])
        var_eps = sb("var_eps", [128, QUADS])
        rstd = sb("rstd", [128, QUADS])
        y_up = sb("y_up", [128, HID])
        y_bias = sb("y_bias", [1, HID])
        y_dn = sb("y_dn", [128, HID])
        stats2 = sb("stats2", [128, 2, QUADS, 6])
        mean_var2 = sb("mean_var2", [128, 2, QUADS, 2])
        var_eps2 = sb("var_eps2", [128, 2, QUADS])
        rstd2 = sb("rstd2", [128, 2, QUADS])

        q_flat = q[:, :, :].rearrange("p a n -> p (a n)")
        wqkv_raw = q_flat[:, 0:3 * HD]
        wout_diag = q_flat[:, 3 * HD:5 * HD].rearrange("p (a h c) -> p a h c", a=PAIRS, h=2)
        wT = q_flat[:, 5 * HD:8 * HD]
        select_raw = k[:, :, :].rearrange("p a (b h m) -> p (a b) h m", h=8, m=64)
        wcon_raw = attnT[:, :].rearrange("p (a c) -> p a c", a=HT)
        COEF = 4 * (HID // 2)
        COEFS = 2
        coef = x1T[:, 0:COEFS * COEF].rearrange("p (r n) -> p r n", r=COEFS)
        up_term = [x1T[:, COEFS * COEF + i * HID:COEFS * COEF + (i + 1) * HID] for i in range(2)]
        dve_term = [x1T[:, COEFS * COEF + (2 + i) * HID:COEFS * COEF + (3 + i) * HID] for i in range(2)]
        hid = q_flat[:, 0:2 * HT * CH].rearrange("p (r i n) -> p r i n", r=2, i=HT)
        hid_h = [k_h[:, :, :].rearrange("p a (b n) -> p (a b) n", n=CH), qn_h[:, :, :]]
        hid_l = [k_l[:, :, :].rearrange("p a (b n) -> p (a b) n", n=CH), qn_l[:, :, :]]
        yT = [kx[:, 0:CH], kx[:, CH:2 * CH]]
        y_out = k_total[:, :].rearrange("p (r t c) -> p r t c", r=2, t=QUADS)

        pz = pb("pz", [128, 2 * CH])
        pa = pb("pa", [128, 2 * CH])
        pq = pb("pq", [128, 2 * CH])
        pc = pb("pc", [128, CH])
        pd = pb("pd", [128, CH])
        ring = [pz[:, 0:CH], pz[:, CH:2 * CH], pq[:, 0:CH], pq[:, CH:2 * CH]]

        s_wqkv = [sem(f"{n}_weights_loaded") for n in ("q", "k", "v")]
        s_wf = sem("wf_loaded")
        s_wout = sem("wout_loaded")
        s_bias = sem("biases_loaded")
        s_xs = sem("xs_loaded")
        s_xres = sem("xres_loaded")
        s_wffn = sem("ffn_weights_loaded")
        s_coef = [sem(f"coef_loaded{r}") for r in range(COEFS)]
        s_zero = sem("zeroed")
        s_wfz = sem("wf_zeroed")
        s_const = sem("constants_made")
        s_sel = sem("select_rounded")
        s_wT = sem("wT_transposed")
        s_wTa = sem("wT_copied_act")
        s_wTd = sem("wT_copied_dve")
        s_fold = sem("folded")
        s_wh = sem("folded_hi")
        s_wl = sem("folded_lo")
        s_voa = sem("vo_copied_act")
        s_vod = sem("vo_copied_dve")
        s_xTp = sem("xT_transposed")
        s_xTh = sem("xT_hi")
        s_xTl = sem("xT_lo")
        s_xh = sem("x_hi")
        s_xl = sem("x_lo")
        s_kp = sem("k_projected")
        s_kb = sem("k_biased")
        s_k = sem("k_relu")
        s_kh = sem("k_hi")
        s_kl = sem("k_lo")
        s_ks = sem("k_summed")
        s_kxt = sem("kx_tile_added")
        s_kx = sem("kx_copied")
        s_qp = sem("q_projected")
        s_q = sem("q_relu")
        s_kcol = sem("ksum_columns")
        s_kcm = sem("ksum_masked")
        s_m = sem("m_done")
        s_mh = sem("m_hi")
        s_ml = sem("m_lo")
        s_np = sem("norm_done")
        s_ne = sem("norm_plus_eps")
        s_r = sem("recip_done")
        s_rh = sem("recip_hi")
        s_rp = sem("recip_parts_done")
        s_rb = sem("recip_spread")
        s_qn = sem("qn_done")
        s_qnh = sem("qn_hi")
        s_qnlp = sem("qn_lo_pool")
        s_qnld = sem("qn_lo_dve")
        s_at = sem("attn_step_added")
        s_atc = sem("attn_copied")
        s_att = sem("attn_transposed")
        s_x1p = sem("x1_pre_done")
        s_st = sem("stats_done")
        s_mv = sem("mean_var_done")
        s_ve = sem("var_eps_done")
        s_rs = sem("rstd_done")
        s_x1 = sem("x1_done")
        s_x1t = sem("x1_transposed")
        s_x1c = sem("x1T_copied")
        s_up = sem("up_butterfly_pool")
        s_ub = sem("up_bias_butterfly_dve")
        s_dn = sem("down_butterfly_dve")
        s_wct = sem("wcon_transposed")
        s_wcc = sem("wconT_copied")
        s_bT = sem("b_up_transposed")
        s_bc = sem("ffn_biases_done")
        s_wdt = sem("wdn_transposed")
        s_wuh = sem("wup_hi")
        s_wul = sem("wup_lo")
        s_wdh = sem("wdn_hi")
        s_wdl = sem("wdn_lo")
        s_fxh = sem("ffn_x_hi")
        s_fxl = sem("ffn_x_lo")
        s_h = sem("hidden_projected")
        s_g = sem("hidden_gelu")
        s_gh = sem("hidden_hi")
        s_gl = sem("hidden_lo")
        s_dp = sem("down_projected")
        s_y = sem("yT_done")
        s_yt = sem("y_transposed")
        s_st2 = sem("stats2_done")
        s_mv2 = sem("mean_var2_done")
        s_ve2 = sem("var_eps2_done")
        s_rs2 = sem("rstd2_done")
        s_yo = sem("y_normalised")
        s_out = [sem(f"out_stored{r}") for r in range(2)]

        def lo_on_dve(a):
            return a % 4 == 3

        LO_DVE = sum(lo_on_dve(a) for a in range(STEPS))
        LO_POOL = STEPS - LO_DVE

        def wait_qn_lo(eng, b, a):
            if lo_on_dve(a):
                eng.wait_ge(s_qnld, b * LO_DVE + sum(lo_on_dve(i) for i in range(a + 1)))
            else:
                eng.wait_ge(s_qnlp, b * LO_POOL + sum(not lo_on_dve(i) for i in range(a + 1)))

        SLOTS = TILES + 3

        block = ctx.enter_context(nc.Block())

        @block.sync
        def _(sp):
            for part in (1, 0):
                cols = slice(part * HD, (part + 1) * HD)
                sp.dma_start(wqkv_raw[:, cols], W_qkv[:, cols]).then_inc(s_wqkv[part], 16)
            sp.dma_start(xs[:, :, :], xs_view[0, :, :, :]).then_inc(s_xs, 16)
            sp.dma_start(wqkv_raw[:, 2 * HD:3 * HD], W_qkv[:, 2 * HD:3 * HD]).then_inc(s_wqkv[2], 16)
            sp.wait_ge(s_zero, 1)
            wo = W_out.rearrange("(a h e) c -> h e a c", h=2, e=D)
            for h in range(2):
                sp.dma_start(wout_diag[h * D:(h + 1) * D, :, h, :], wo[h, :, :, :]).then_inc(s_wout, 16)
            sp.dma_start(x_res[:, :, :], xs_view[0, :, :, :]).then_inc(s_xres, 16)
            n = 0
            sp.dma_start(y_up[:, :], W_exp).then_inc(s_wffn, 16)
            sp.dma_start(y_bias[:, :], b_exp.rearrange("(a n) -> a n", a=1)).then_inc(s_wffn, 16)
            sp.dma_start(wcon_raw, W_con.rearrange("(a p) c -> p a c", p=128)).then_inc(s_wffn, 16)

            def load_coef(n):
                if n >= COEFS:
                    m = n - COEFS
                    if m < STAGES:
                        sp.wait_ge(s_up, 3 * (m + 1))
                        sp.wait_ge(s_ub, 3 * (m + 1))
                    else:
                        sp.wait_ge(s_dn, 3 * (m - STAGES + 1))
                w, stage = (up_weights, n) if n < STAGES else (down_weights, 2 * STAGES - 1 - n)
                row = w[stage, :, :, :].rearrange("(o k) i j -> o (k i j)", o=1)
                sp.dma_start(coef[:, n % COEFS, :], row.to_broadcast([128, COEF])).then_inc(s_coef[n % COEFS], 16)

            load_coef(0)
            load_coef(1)
            sp.wait_ge(s_xTp, 2)
            sp.wait_ge(s_xh, 1)
            sp.wait_ge(s_xl, 1)
            sp.dma_start(xs[:, :, :], xs_view[1, :, :, :]).then_inc(s_xs, 16)
            for n in range(2, 2 * STAGES):
                load_coef(n)
            for b in range(1, BATCH - 1):
                sp.wait_ge(s_xTp, 2 * b + 2)
                sp.wait_ge(s_xh, b + 1)
                sp.wait_ge(s_xl, b + 1)
                sp.dma_start(xs[:, :, :], xs_view[b + 1, :, :, :]).then_inc(s_xs, 16)
                sp.wait_ge(s_x1p, CHUNKS * b)
                sp.dma_start(x_res[:, :, :], xs_view[b, :, :, :]).then_inc(s_xres, 16)
            sp.wait_ge(s_x1p, CHUNKS * (BATCH - 1))
            sp.dma_start(x_res[:, :, :], xs_view[BATCH - 1, :, :, :]).then_inc(s_xres, 16)
            for c in range(ALLCH):
                sp.wait_ge(s_yo, c + 1)
                sp.dma_start(out_view[c, :, :, :], y_out[:, c % 2, :, :]).then_inc(s_out[c % 2], 16)
            for r in range(2):
                sp.wait_ge(s_out[r], 16 * (ALLCH // 2))

        @block.gpsimd
        def _(pool):
            g = nc.gpsimd
            g.memset(wf_diag[:, :], 0.0).then_inc(s_wfz, 1)
            g.memset(ident[:, :], 0.0).then_inc(s_const, 1)
            pool.wait_ge(s_const, 1)
            g.affine_select(out=ident[:, :], in_=ident[:, :], compare_op=ALU.not_equal, fill=1.0, base=0,
                            pattern=[[-1, 128]], channel_multiplier=1).then_inc(s_const, 1)
            g.memset(ones[:, :], 1.0)
            g.memset(ln_eps[:, :], LN_EPS)
            g.memset(minus_half[:, :], -0.5)
            g.memset(head_mask[:, :, :], 0.0).then_inc(s_const, 1)
            g.memset(part_b[:, :], 0.0).then_inc(s_const, 1)
            g.memset(select_raw, 0.0).then_inc(s_const, 1)
            pool.wait_ge(s_const, 5)
            n = 5
            for half in range(2):
                for part in range(2):
                    v = head_mask[half * D:(half + 1) * D, :, :].rearrange("p (s a) c -> p s a c", s=2)
                    g.affine_select(out=v, in_=v, compare_op=ALU.not_equal, fill=1.0, base=-half - 8 * part,
                                    pattern=[[0, 2], [-2, 4], [1, 32]], channel_multiplier=0).then_inc(s_const, 1)
                    n += 1
                    pool.wait_ge(s_const, n)
            for part in range(2):
                g.affine_select(out=select_raw, in_=select_raw, compare_op=ALU.not_equal, fill=1.0,
                                base=-8 * part, pattern=[[-32, 4], [-1, 8], [0, 64]],
                                channel_multiplier=1).then_inc(s_const, 1)
                n += 1
                pool.wait_ge(s_const, n)
            for j in range(4):
                for i in range(8):
                    g.affine_select(out=part_b[:, :], in_=part_b[:, :], compare_op=ALU.not_equal, fill=-1.0,
                                    base=-32 * j - 8 - i, pattern=[[0, 1]], channel_multiplier=1).then_inc(s_const, 1)
                    n += 1
                    pool.wait_ge(s_const, n)

            def up_stage(st):
                s = 1 << st
                w = coef[:, st % COEFS, :].rearrange("p (k s i j) -> p k i s j", s=s, i=2, j=2)
                y = y_up[:, :].rearrange("p (k i s) -> p k i s", i=2, s=s)
                pool.wait_ge(s_coef[st % COEFS], 16 * (st // COEFS + 1))
                if st:
                    pool.wait_ge(s_up, 3 * st)
                for j in range(2):
                    src = y[:, :, j:j + 1, :].to_broadcast([128, HID // (2 * s), 2, s])
                    dst = up_term[j].rearrange("p (k i s) -> p k i s", i=2, s=s)
                    g.tensor_tensor(dst, w[:, :, :, :, j], src, ALU.mult).then_inc(s_up, 1)
                pool.wait_ge(s_up, 3 * st + 2)
                g.tensor_tensor(y_up[:, :], up_term[0], up_term[1], ALU.add).then_inc(s_up, 1)

            def k_sum(b, s):
                if s == 0:
                    return
                pool.wait_ge(s_k, b * TILES + s + 1)
                if s == 1:
                    if not isinstance(b, int):
                        pool.wait_ge(s_kcol, b)
                    g.tensor_tensor(k_total[:, :], k[:, 0, :], k[:, 1, :], ALU.add).then_inc(s_ks, 1)
                else:
                    pool.wait_ge(s_ks, b * SUMS + s - 1)
                    g.tensor_tensor(k_total[:, :], k_total[:, :], k[:, s % 2, :], ALU.add).then_inc(s_ks, 1)

            def qn_lo(b, a):
                if lo_on_dve(a):
                    return
                pool.wait_ge(s_qnh, b * STEPS + a + 1)
                if a >= 4:
                    pool.wait_ge(s_at, b * STEPS + a - 3)
                g.tensor_tensor(qn_l[:, a % 4, :], qn[:, a % 2, :], qn_h[:, a % 4, :].bitcast(fp32),
                                ALU.subtract).then_inc(s_qnlp, 1)

            def ln_rstd(c, ve, rs, mv, s_in, s_mid, s_done):
                pool.wait_ge(s_in, QUADS * (c + 1))
                g.tensor_tensor(ve, mv, ln_eps[:, :].to_broadcast([128, QUADS]), ALU.add).then_inc(s_mid, 1)
                pool.wait_ge(s_mid, c + 1)
                g.tensor_tensor(rs, ve, minus_half[:, :].to_broadcast([128, QUADS]), ALU.pow).then_inc(s_done, 1)

            def slots(b, more):
                for s in range(SLOTS):
                    if more and s < TILES:
                        k_sum(b + 1, s)
                    if 2 <= s < TILES + 2:
                        qn_lo(b, 2 * (s - 2))
                        qn_lo(b, 2 * (s - 2) + 1)
                    if s == 9:
                        ln_rstd(CHUNKS * b, var_eps[:, :], rstd[:, :], mean_var[:, :, 1], s_mv, s_ve, s_rs)
                ln_rstd(CHUNKS * b + 1, var_eps[:, :], rstd[:, :], mean_var[:, :, 1], s_mv, s_ve, s_rs)

            pool.wait_ge(s_wffn, 48)
            for st in range(3):
                up_stage(st)
            for s in range(TILES):
                k_sum(0, s)
            for st in range(3, STAGES):
                up_stage(st)
            with pool.Fori(0, BATCH - 1) as b:
                slots(b, True)
            slots(BATCH - 1, False)

            def hidden_lo(c, r):
                for i in range(0, HT, 2):
                    pool.wait_ge(s_gh, 2 * c + i // 2 + 1)
                    g.tensor_tensor(hid_l[r][:, i:i + 2, :], hid[:, r, i:i + 2, :],
                                    hid_h[r][:, i:i + 2, :].bitcast(fp32), ALU.subtract).then_inc(s_gl, 1)

            def rstd_out(c, r):
                ln_rstd(c, var_eps2[:, r, :], rstd2[:, r, :], mean_var2[:, r, :, 1], s_mv2, s_ve2, s_rs2)

            hidden_lo(0, 0)
            with pool.Fori(0, ALLCH // 2 - 1) as i:
                for r in range(2):
                    hidden_lo(2 * i + r + 1, 1 - r)
                    rstd_out(2 * i + r, r)
            hidden_lo(ALLCH - 1, 1)
            rstd_out(ALLCH - 2, 0)
            rstd_out(ALLCH - 1, 1)

        @block.tensor
        def _(pe):
            t = nc.tensor

            def product(dst, pairs, start, stop):
                for n, (lhsT, rhs) in enumerate(pairs):
                    last = t.matmul(dst, lhsT, rhs, start=start and n == 0, stop=stop and n == len(pairs) - 1)
                return last

            def split(dst, lhs, rhs, start=True, stop=True):
                (lh, ll), (rh, rl) = lhs, rhs
                return product(dst, [(lh, rh), (lh, rl), (ll, rh)], start, stop)

            banks = [pz[:, 0:CH], pz[:, CH:], pa[:, 0:CH], pa[:, CH:], pq[:, 0:CH], pq[:, CH:]]
            ORDER = [2, 3, 0, 1, 4, 5]
            pe.wait_ge(s_const, 2)
            for n, grp in enumerate(ORDER):
                pe.wait_ge(s_wqkv[grp // 2], 16)
                for i in range(4):
                    col = (grp * 4 + i) * 128
                    last = t.transpose(banks[n][:, i * 128:(i + 1) * 128], wqkv_raw[:, col:col + 128], ident[:, :])
                last.then_inc(s_wT, 1)
            pe.wait_ge(s_wf, 32)
            for n, (grp, dst) in enumerate([(2, pc[:, :]), (3, pd[:, :]), (0, pz[:, 0:CH]), (1, pz[:, CH:])]):
                if n % 2 == 0:
                    pe.wait_ge(s_wTa, n // 2 + 1)
                else:
                    pe.wait_ge(s_wTd, n // 2 + 1)
                for i in range(4):
                    col = (grp * 4 + i) * 128
                    last = t.matmul(dst[:, i * 128:(i + 1) * 128], wT[:, col:col + 128], wf_diag[:, :],
                                    start=True, stop=True)
                last.then_inc(s_fold, 1)

            def transpose_x(n):
                pe.wait_ge(s_xs, 16 * (n + 1))
                for half in range(2):
                    for i in range(4):
                        last = t.transpose(pa[:, half * CH + i * 128:half * CH + (i + 1) * 128],
                                           xs[:, 4 * half + i, :], ident[:, :])
                    last.then_inc(s_xTp, 1)

            transpose_x(0)
            pe.wait_ge(s_wTa, 3)
            pe.wait_ge(s_wTd, 3)
            pe.wait_ge(s_wout, 32)
            pe.wait_ge(s_wh, 2)
            pe.wait_ge(s_wl, 2)
            for n, dst in enumerate([pq[:, 0:CH], pq[:, CH:], pc[:, :], pd[:, :]]):
                for i in range(2):
                    pair = 2 * n + i
                    col = 2 * HD + pair * 128
                    last = t.matmul(dst[:, i * 256:(i + 1) * 256], wT[:, col:col + 128],
                                    wout_diag[:, pair, :, :].rearrange("p h c -> p (h c)"), start=True, stop=True)
                last.then_inc(s_fold, 1)

            def project_k(b, s, half):
                if s == 0:
                    pe.wait_ge(s_xTh, b + 1)
                    pe.wait_ge(s_xTl, b + 1)
                else:
                    pe.wait_ge(s_kb, b * 2 * TILES + 2 * (s - 1) + half + 1)
                tok = slice(s * 128, (s + 1) * 128)
                cols = slice(half * CH, (half + 1) * CH)
                split(pz[:, cols], (xT_h[:, tok], xT_l[:, tok]), (wk_h[:, cols], wk_l[:, cols])).then_inc(s_kp, 1)

            def add_kx(b, s):
                pe.wait_ge(s_kh, b * TILES + s + 1)
                pe.wait_ge(s_kl, b * TILES + s + 1)
                if s == 0:
                    pe.wait_ge(s_xh, b + 1)
                    pe.wait_ge(s_xl, b + 1)
                for half in range(2):
                    cols = slice(half * CH, (half + 1) * CH)
                    last = split(pa[:, cols], (x_h[:, s, :], x_l[:, s, :]),
                                 (k_h[:, s % 2, cols], k_l[:, s % 2, cols]), s == 0, s == TILES - 1)
                last.then_inc(s_kxt, 1)

            def project_q(b, i):
                p, c = i // CHUNKS, i % CHUNKS
                if i >= 4:
                    pe.wait_ge(s_q, b * STEPS + i - 3)
                cols = slice(c * CH, (c + 1) * CH)
                split(ring[i % 4], (wq_h[:, p, :], wq_l[:, p, :]), (xT_h[:, cols], xT_l[:, cols])).then_inc(s_qp, 1)

            def ksum(b):
                pe.wait_ge(s_ks, SUMS * (b + 1))
                for p in range(PAIRS):
                    last = t.matmul(pc[:, p:p + 1], k_total[:, p * 128:(p + 1) * 128], ones[:, :],
                                    start=True, stop=True)
                last.then_inc(s_kcol, 1)

            def head_maps(b):
                pe.wait_ge(s_kx, b + 1)
                pe.wait_ge(s_q, STEPS * (b + 1))
                for p in range(PAIRS):
                    for h in range(2):
                        last = t.matmul(pq[h * D:(h + 1) * D, p * 128:(p + 1) * 128],
                                        kx[:, (2 * p + h) * D:(2 * p + h + 1) * D], vo[:, 2 * p + h, :],
                                        start=True, stop=True)
                last.then_inc(s_m, 1)

            def norms(b):
                pe.wait_ge(s_kcm, b + 1)
                pe.wait_ge(s_q, STEPS * (b + 1))
                for n in range(4):
                    for c in range(CHUNKS):
                        for s in range(2):
                            j = 2 * c + s
                            last = t.matmul(pd[32 * j:32 * j + 32, :], ksum_cols[:, 4 * s + n, :],
                                            q[:, 4 * s + n, c * CH:(c + 1) * CH], start=n == 0, stop=n == 3)
                last.then_inc(s_np, 1)

            def spread(b, a):
                c, p = a // PAIRS, a % PAIRS
                if a < 2:
                    pe.wait_ge(s_rp, b + 1)
                    pe.wait_ge(s_ml, b + 1)
                else:
                    pe.wait_ge(s_qn, b * STEPS + a - 1)
                j, n = 2 * c + p // 4, p % 4
                sel = select[:, j, 2 * n:2 * n + 2, :].rearrange("p h m -> p (h m)")
                t.matmul(pq[:, (a % 2) * CH:(a % 2 + 1) * CH], sel, recip_parts[:, :],
                         start=True, stop=True).then_inc(s_rb, 1)

            def add_attn(b, a):
                c, p = a // PAIRS, a % PAIRS
                if p == 0:
                    pe.wait_ge(s_kcm, b + 1)
                    if c:
                        pe.wait_ge(s_atc, CHUNKS * b + c)
                pe.wait_ge(s_qnh, b * STEPS + a + 1)
                wait_qn_lo(pe, b, a)
                split(pc[:, :], (m_h[:, p, :], m_l[:, p, :]), (qn_h[:, a % 4, :], qn_l[:, a % 4, :]),
                      p == 0, p == PAIRS - 1).then_inc(s_at, 1)

            def transpose_attn(c):
                pe.wait_ge(s_atc, c + 1)
                for i in range(QUADS):
                    last = t.transpose(pd[:, i * 128:(i + 1) * 128], attnT[:, i * 128:(i + 1) * 128], ident[:, :])
                last.then_inc(s_att, 1)

            def transpose_x1(c):
                pe.wait_ge(s_x1, c + 1)
                for i in range(QUADS):
                    last = t.transpose(pd[:, i * 128:(i + 1) * 128], x1[:, i, :], ident[:, :])
                last.then_inc(s_x1t, 1)

            def slots(b, more):
                for s in range(SLOTS):
                    if more and 2 <= s < TILES + 2:
                        add_kx(b + 1, s - 2)
                    if more and s < TILES:
                        project_k(b + 1, s, 0)
                    if 2 <= s < TILES + 2:
                        spread(b, 2 * (s - 2))
                    if more and s < TILES:
                        project_k(b + 1, s, 1)
                    if 3 <= s:
                        add_attn(b, 2 * (s - 3))
                    if 2 <= s < TILES + 2:
                        spread(b, 2 * (s - 2) + 1)
                    if 3 <= s:
                        add_attn(b, 2 * (s - 3) + 1)
                    if s == 8:
                        transpose_attn(CHUNKS * b)

            pe.wait_ge(s_wh, 4)
            pe.wait_ge(s_wl, 4)
            for s in range(TILES + 2):
                if 2 <= s:
                    add_kx(0, s - 2)
                if s < TILES:
                    project_k(0, s, 0)
                    project_k(0, s, 1)
            pe.wait_ge(s_voa, 2)
            pe.wait_ge(s_vod, 2)
            pe.wait_ge(s_kb, 2 * TILES)
            for i in range(STEPS):
                project_q(0, i)
            pe.wait_ge(s_wffn, 48)
            for i in range(HT):
                last = t.transpose(pd[:, i * 128:(i + 1) * 128], wcon_raw[:, i, :], ident[:, :])
            last.then_inc(s_wct, 1)
            pe.wait_ge(s_wcc, 1)
            with t.Fori(0, BATCH - 1) as b:
                pe.wait_ge(s_kx, b + 1)
                transpose_x(b + 1)
                ksum(b)
                head_maps(b)
                norms(b)
                slots(b, True)
                pe.wait_ge(s_kb, (b + 2) * 2 * TILES)
                pe.wait_ge(s_qn, (b + 1) * STEPS)
                for i in range(STEPS):
                    project_q(b + 1, i)
                    if i == 0:
                        transpose_x1(CHUNKS * b)
                    if i == 4:
                        pe.wait_ge(s_x1c, CHUNKS * b + 1)
                        transpose_attn(CHUNKS * b + 1)
                    if i == 14:
                        transpose_x1(CHUNKS * b + 1)
                pe.wait_ge(s_x1c, CHUNKS * b + 2)
            last_b = BATCH - 1
            ksum(last_b)
            head_maps(last_b)
            norms(last_b)
            slots(last_b, False)
            transpose_x1(CHUNKS * last_b)
            pe.wait_ge(s_x1c, CHUNKS * last_b + 1)
            transpose_attn(CHUNKS * last_b + 1)

            pe.wait_ge(s_ub, 3 * STAGES)
            for i in range(HT):
                last = t.matmul(pz[:, i:i + 1], y_bias[:, i * 128:(i + 1) * 128], ones[0:1, :],
                                start=True, stop=True)
            last.then_inc(s_bT, 1)
            pe.wait_ge(s_dn, 3 * STAGES)
            for i in range(HT):
                last = t.transpose(pz[:, CH + i * 128:CH + (i + 1) * 128], y_dn[:, i * 128:(i + 1) * 128], ident[:, :])
            last.then_inc(s_wdt, 1)
            transpose_x1(CHUNKS * last_b + 1)
            pe.wait_ge(s_bc, 2)
            pe.wait_ge(s_wdl, 1)
            pe.wait_ge(s_wuh, 1)
            pe.wait_ge(s_wul, 1)

            def up(c, r, first=False):
                pe.wait_ge(s_fxh, c + 1)
                pe.wait_ge(s_fxl, c + 1)
                for i in range(HT):
                    if not first:
                        pe.wait_ge(s_g, HT * (c - 1) + i + 1)
                    cols = slice(i * 128, (i + 1) * 128)
                    tok = slice(r * CH, (r + 1) * CH)
                    split(ring[i], (wup_h[:, cols], wup_l[:, cols]), (xT_h[:, tok], xT_l[:, tok])).then_inc(s_h, 1)

            def down(c, r, first=False):
                if not first:
                    pe.wait_ge(s_y, c - 1)
                for i in range(HT):
                    if i % 2 == 0:
                        pe.wait_ge(s_gl, 2 * c + i // 2 + 1)
                    last = split(pa[:, r * CH:(r + 1) * CH], (wdn_h[:, i, :], wdn_l[:, i, :]),
                                 (hid_h[r][:, i, :], hid_l[r][:, i, :]), i == 0, i == HT - 1)
                last.then_inc(s_dp, 1)

            def transpose_y(c, r, first=False):
                pe.wait_ge(s_y, c + 1)
                if not first:
                    pe.wait_ge(s_yo, c - 1)
                for i in range(QUADS):
                    last = t.transpose([pc, pd][r][:, i * 128:(i + 1) * 128], yT[r][:, i * 128:(i + 1) * 128],
                                       ident[:, :])
                last.then_inc(s_yt, 1)

            up(0, 0, first=True)
            pe.wait_ge(s_x1c, ALLCH)
            up(1, 1)
            down(0, 0, first=True)
            up(2, 0)
            transpose_y(0, 0, first=True)
            down(1, 1, first=True)
            up(3, 1)
            transpose_y(1, 1, first=True)
            down(2, 0)
            with t.Fori(1, ALLCH // 2 - 1) as i:
                for n in range(2):
                    c, r = 2 * i + 1 + n, 1 - n
                    up(c + 1, 1 - r)
                    transpose_y(c - 1, 1 - r)
                    down(c, r)
            transpose_y(ALLCH - 2, 0)
            down(ALLCH - 1, 1)
            transpose_y(ALLCH - 1, 1)

        @block.scalar
        def _(act):
            a_ = nc.scalar
            act.wait_ge(s_wfz, 1)
            for h in range(2):
                act.dma_start(wf_diag[h * D:(h + 1) * D, h * D:(h + 1) * D], W_f).then_inc(s_wf, 16)
                act.dma_start(bf_col[h * D:(h + 1) * D, :], b_f.rearrange("(p o) -> p o", o=1)).then_inc(s_bias, 16)
            act.dma_start(bf_row[:, :], b_f.rearrange("(o n) -> o n", o=1).to_broadcast([128, D])).then_inc(s_bias, 16)
            act.dma_start(bout_col[:, :], b_out.rearrange("(p o) -> p o", o=1)).then_inc(s_bias, 16)
            act.dma_start(bcon_col[:, :], b_con.rearrange("(p o) -> p o", o=1)).then_inc(s_bias, 16)
            act.dma_start(bdn_raw[:, :], down_bias.rearrange("(p o) -> p o", o=1)).then_inc(s_bias, 16)
            for i in range(HT):
                act.dma_start(bup_raw[:, i:i + 1],
                              up_bias[i * 128:(i + 1) * 128].rearrange("(p o) -> p o", o=1)).then_inc(s_bias, 16)

            def hi(dst, src, done):
                a_.activation(dst, src, ACT.Copy).then_inc(done, 1)

            for n, grp in [(0, 2), (2, 0), (4, 4)]:
                act.wait_ge(s_wT, n + 1)
                bank = [pz[:, 0:CH], None, pa[:, 0:CH], None, pq[:, 0:CH]][n]
                a_.activation(wT[:, grp * CH:(grp + 1) * CH], bank, ACT.Copy).then_inc(s_wTa, 1)
            act.wait_ge(s_fold, 1)
            hi(wk_h[:, 0:CH], pc[:, :], s_wh)
            act.wait_ge(s_fold, 2)
            hi(wk_h[:, CH:], pd[:, :], s_wh)

            def x_hi(b):
                act.wait_ge(s_xTp, 2 * (b + 1))
                hi(xT_h[:, :], pa[:, :], s_xTh)
                hi(x_h[:, :, :], xs[:, :, :], s_xh)

            x_hi(0)
            act.wait_ge(s_fold, 4)
            wq_flat = wq_h[:, :, :].rearrange("p a m -> p (a m)")
            for half in range(2):
                hi(wq_flat[:, half * CH:(half + 1) * CH], pz[:, half * CH:(half + 1) * CH], s_wh)
            vo_flat = vo[:, :, :].rearrange("p a m -> p (a m)")
            for n, bank in [(0, pq[:, 0:CH]), (2, pc[:, :])]:
                act.wait_ge(s_fold, 5 + n)
                a_.activation(vo_flat[:, n * CH:(n + 1) * CH], bank, ACT.Copy).then_inc(s_voa, 1)
            act.wait_ge(s_const, 11)
            hi(select[:, :, :, :].rearrange("p a h m -> p (a h m)"),
               select_raw.rearrange("p a h m -> p (a h m)"), s_sel)
            act.wait_ge(s_bias, 16 * (6 + HT))

            def k_relu(b, s):
                act.wait_ge(s_kb, b * 2 * TILES + 2 * s + 2)
                kt = k[:, s % 2, :]
                if s >= 2:
                    act.wait_ge(s_kxt, b * TILES + s - 1)
                a_.activation(k_h[:, s % 2, :], kt, ACT.Relu).then_inc(s_kh, 1)
                act.wait_ge(s_kh, b * TILES + s + 1)
                a_.activation(kt, kt, ACT.Relu).then_inc(s_k, 1)

            def kx_copy(b):
                act.wait_ge(s_kxt, TILES * (b + 1))
                a_.activation(kx[:, :], pa[:, :], ACT.Copy).then_inc(s_kx, 1)

            def q_relu(b, i):
                p, c = i // CHUNKS, i % CHUNKS
                act.wait_ge(s_qp, b * STEPS + i + 1)
                a_.activation(q[:, p, c * CH:(c + 1) * CH], ring[i % 4], ACT.Relu,
                              bias=bf_col[:, :]).then_inc(s_q, 1)

            def qn_hi(b, a):
                act.wait_ge(s_qn, b * STEPS + a + 1)
                if a >= 4:
                    act.wait_ge(s_at, b * STEPS + a - 3)
                hi(qn_h[:, a % 4, :], qn[:, a % 2, :], s_qnh)

            def attn_copy(c):
                act.wait_ge(s_at, PAIRS * (c + 1))
                a_.activation(attnT[:, :], pc[:, :], ACT.Identity, bias=bout_col[:, :]).then_inc(s_atc, 1)

            def x1T_copy(c):
                act.wait_ge(s_x1t, c + 1)
                act.wait_ge(s_up, 3 * STAGES)
                act.wait_ge(s_ub, 3 * STAGES)
                act.wait_ge(s_dn, 3 * STAGES)
                a_.activation(x1T[:, c * CH:(c + 1) * CH] if isinstance(c, int) else x1T[:, bass.ds(c * CH, CH)],
                              pd[:, :], ACT.Copy).then_inc(s_x1c, 1)

            def slots(b, more):
                for s in range(SLOTS):
                    if 2 <= s < TILES + 2:
                        qn_hi(b, 2 * (s - 2))
                    if s == 7:
                        attn_copy(CHUNKS * b)
                    if more and s < TILES:
                        k_relu(b + 1, s)
                    if 2 <= s < TILES + 2:
                        qn_hi(b, 2 * (s - 2) + 1)
                    if s == 1:
                        act.wait_ge(s_r, b + 1)
                        hi(recip_h[:, :], recip[:, :], s_rh)

            for s in range(TILES):
                k_relu(0, s)
            kx_copy(0)
            act.wait_ge(s_fold, 8)
            for i in range(STEPS):
                q_relu(0, i)
            act.wait_ge(s_wct, 1)
            a_.activation(y_dn[:, :], pd[:, :], ACT.Copy).then_inc(s_wcc, 1)
            with a_.Fori(0, BATCH - 1) as b:
                x_hi(b + 1)
                act.wait_ge(s_m, b + 1)
                hi(m_h[:, :, :].rearrange("p a c -> p (a c)"), pq[:, :], s_mh)
                slots(b, True)
                attn_copy(CHUNKS * b + 1)
                kx_copy(b + 1)
                for i in range(STEPS):
                    q_relu(b + 1, i)
                    if i == 4:
                        x1T_copy(CHUNKS * b)
                x1T_copy(CHUNKS * b + 1)
            last_b = BATCH - 1
            act.wait_ge(s_m, last_b + 1)
            hi(m_h[:, :, :].rearrange("p a c -> p (a c)"), pq[:, :], s_mh)
            slots(last_b, False)
            act.wait_ge(s_up, 3 * STAGES)
            hi(wup_h[:, :], y_up[:, :], s_wuh)
            x1T_copy(CHUNKS * last_b)
            attn_copy(CHUNKS * last_b + 1)

            def ffn_x_hi(c, r, first=False):
                if not first:
                    act.wait_ge(s_h, HT * (c - 1))
                hi(xT_h[:, r * CH:(r + 1) * CH],
                   x1T[:, c * CH:(c + 1) * CH] if isinstance(c, int) else x1T[:, bass.ds(c * CH, CH)], s_fxh)

            ffn_x_hi(0, 0, first=True)
            ffn_x_hi(1, 1, first=True)
            act.wait_ge(s_wdt, 1)
            hi(wdn_h[:, :, :].rearrange("p a c -> p (a c)"), pz[:, CH:], s_wdh)
            x1T_copy(CHUNKS * last_b + 1)
            act.wait_ge(s_bc, 2)

            def gelu(c, r, first=False):
                for i in range(HT):
                    act.wait_ge(s_h, HT * c + i + 1)
                    if i == 0 and not first:
                        act.wait_ge(s_gl, 2 * (c - 1))
                    a_.activation(hid[:, r, i, :], ring[i], ACT.Gelu, bias=bup_col[:, i:i + 1]).then_inc(s_g, 1)
                    if i % 2:
                        act.wait_ge(s_g, HT * c + i + 1)
                        if i == 1 and not first:
                            act.wait_ge(s_dp, c - 1)
                        hi(hid_h[r][:, i - 1:i + 1, :], hid[:, r, i - 1:i + 1, :], s_gh)

            gelu(0, 0, first=True)
            ffn_x_hi(2, 0)
            gelu(1, 1, first=True)
            ffn_x_hi(3, 1)
            gelu(2, 0)
            with a_.Fori(1, ALLCH // 2 - 1) as i:
                for n in range(2):
                    c, r = 2 * i + 1 + n, 1 - n
                    ffn_x_hi(c + 1, 1 - r)
                    gelu(c, r)
            gelu(ALLCH - 1, 1)

        @block.vector
        def _(dve):
            v = nc.vector

            def lo(dst, src, high, done):
                v.tensor_tensor(dst, src, high.bitcast(fp32), ALU.subtract).then_inc(done, 1)

            v.memset(wout_diag, 0.0).then_inc(s_zero, 1)
            for n, grp in [(1, 3), (3, 1), (5, 5)]:
                dve.wait_ge(s_wT, n + 1)
                bank = {1: pz[:, CH:], 3: pa[:, CH:], 5: pq[:, CH:]}[n]
                v.tensor_copy(wT[:, grp * CH:(grp + 1) * CH], bank).then_inc(s_wTd, 1)
            dve.wait_ge(s_wh, 1)
            lo(wk_l[:, 0:CH], pc[:, :], wk_h[:, 0:CH], s_wl)
            dve.wait_ge(s_wh, 2)
            lo(wk_l[:, CH:], pd[:, :], wk_h[:, CH:], s_wl)

            def x_lo(b):
                dve.wait_ge(s_xTh, b + 1)
                lo(xT_l[:, :], pa[:, :], xT_h[:, :], s_xTl)
                dve.wait_ge(s_xh, b + 1)
                lo(x_l[:, :, :], xs[:, :, :], x_h[:, :, :], s_xl)

            x_lo(0)
            wq_lf = wq_l[:, :, :].rearrange("p a m -> p (a m)")
            wq_hf = wq_h[:, :, :].rearrange("p a m -> p (a m)")
            for half in range(2):
                cols = slice(half * CH, (half + 1) * CH)
                dve.wait_ge(s_wh, 3 + half)
                lo(wq_lf[:, cols], pz[:, cols], wq_hf[:, cols], s_wl)
            vo_flat = vo[:, :, :].rearrange("p a m -> p (a m)")
            for n, bank in [(1, pq[:, CH:]), (3, pd[:, :])]:
                dve.wait_ge(s_fold, 5 + n)
                v.tensor_copy(vo_flat[:, n * CH:(n + 1) * CH], bank).then_inc(s_vod, 1)
            dve.wait_ge(s_bias, 16 * (6 + HT))
            dve.wait_ge(s_sel, 1)

            def k_bias(b, s):
                for half in range(2):
                    dve.wait_ge(s_kp, b * 2 * TILES + 2 * s + half + 1)
                    if half == 0 and s >= 2:
                        dve.wait_ge(s_ks, b * SUMS + max(1, s - 2))
                    if half == 0 and s < 2 and not isinstance(b, int):
                        dve.wait_ge(s_ks, b * SUMS)
                    cols = slice(half * CH, (half + 1) * CH)
                    v.tensor_tensor(k[:, s % 2, cols].rearrange("p (h d) -> p h d", d=D),
                                    pz[:, cols].rearrange("p (h d) -> p h d", d=D),
                                    bf_row[:, :].rearrange("p (o d) -> p o d", o=1).to_broadcast([128, CH // D, D]),
                                    ALU.add).then_inc(s_kb, 1)

            def k_lo(b, s):
                dve.wait_ge(s_k, b * TILES + s + 1)
                lo(k_l[:, s % 2, :], k[:, s % 2, :], k_h[:, s % 2, :], s_kl)

            def normalise_q(b, a):
                c, p = a // PAIRS, a % PAIRS
                dve.wait_ge(s_rb, b * STEPS + a + 1)
                if a >= 2:
                    wait_qn_lo(dve, b, a - 2)
                v.tensor_tensor(qn[:, a % 2, :], q[:, p, c * CH:(c + 1) * CH], pq[:, (a % 2) * CH:(a % 2 + 1) * CH],
                                ALU.mult).then_inc(s_qn, 1)

            def qn_lo(b, a):
                if not lo_on_dve(a):
                    return
                dve.wait_ge(s_qnh, b * STEPS + a + 1)
                lo(qn_l[:, a % 4, :], qn[:, a % 2, :], qn_h[:, a % 4, :], s_qnld)

            def layer_norm_1(c, token):
                dve.wait_ge(s_att, c + 1)
                dve.wait_ge(s_xres, 16 * token[0] + 16)
                v.tensor_tensor(x1_pre[:, :, :], pd[:, :].rearrange("p (t c) -> p t c", t=QUADS),
                                x_res[:, token[1]:token[1] + QUADS, :], ALU.add).then_inc(s_x1p, 1)
                dve.wait_ge(s_x1p, c + 1)
                for i in range(QUADS):
                    v.bn_stats(stats[:, i, :], x1_pre[:, i, :]).then_inc(s_st, 1)
                dve.wait_ge(s_st, QUADS * (c + 1))
                v.memset(scratch[:, :], 0.0)
                for i in range(QUADS):
                    v.bn_aggr(mean_var[:, i, :], stats[:, i, :]).then_inc(s_mv, 1)

            def layer_norm_1_end(c):
                dve.wait_ge(s_rs, c + 1)
                for i in range(QUADS):
                    ins = v.tensor_scalar(x1[:, i, :], x1_pre[:, i, :], mean_var[:, i, 0:1], rstd[:, i:i + 1],
                                          ALU.subtract, ALU.mult)
                ins.then_inc(s_x1, 1)

            def row_stage(y, part, n, st, done, base, transposed):
                s = 1 << st
                w = coef[0:part, n % COEFS, :].rearrange("p (k s i j) -> p k i s j", s=s, i=2, j=2)
                yv = y.rearrange("p (k i s) -> p k i s", i=2, s=s)
                dve.wait_ge(s_coef[n % COEFS], 16 * (n // COEFS + 1))
                if base:
                    dve.wait_ge(done, base)
                for j in range(2):
                    src = yv[:, :, j:j + 1, :].to_broadcast([part, HID // (2 * s), 2, s])
                    dst = dve_term[j][0:part, :].rearrange("p (k i s) -> p k i s", i=2, s=s)
                    wj = w[:, :, j, :, :].rearrange("p k s i -> p k i s") if transposed else w[:, :, :, :, j]
                    v.tensor_tensor(dst, wj, src, ALU.mult).then_inc(done, 1)
                dve.wait_ge(done, base + 2)
                v.tensor_tensor(y, dve_term[0][0:part, :], dve_term[1][0:part, :], ALU.add).then_inc(done, 1)

            def bias_stage(st):
                row_stage(y_bias[:, :], 1, st, st, s_ub, 3 * st, False)

            def down_stage(m):
                row_stage(y_dn[:, :], 128, STAGES + m, STAGES - 1 - m, s_dn, 3 * m, True)

            def head(b):
                dve.wait_ge(s_kcol, b + 1)
                v.tensor_tensor(ksum_cols[:, :, :], head_mask[:, :, :],
                                pc[:, 0:PAIRS].rearrange("p (a o) -> p a o", o=1).to_broadcast([128, PAIRS, 32]),
                                ALU.mult).then_inc(s_kcm, 1)
                dve.wait_ge(s_mh, b + 1)
                lo(m_l[:, :, :].rearrange("p a c -> p (a c)"), pq[:, :],
                   m_h[:, :, :].rearrange("p a c -> p (a c)"), s_ml)
                dve.wait_ge(s_np, b + 1)
                v.tensor_scalar(norm[:, :], pd[:, :], NORM_EPS, None, ALU.add).then_inc(s_ne, 1)
                dve.wait_ge(s_ne, b + 1)
                v.reciprocal(recip[:, :], norm[:, :]).then_inc(s_r, 1)

            def recip_split(b):
                dve.wait_ge(s_rh, b + 1)
                dve.wait_ge(s_r, b + 1)
                v.scalar_tensor_tensor(recip_parts[:, :], recip_h[:, :].bitcast(fp32), part_b[:, :], recip[:, :],
                                       ALU.mult, ALU.add).then_inc(s_rp, 1)

            def slots(b, more):
                for s in range(SLOTS):
                    if more and s < TILES:
                        k_bias(b + 1, s)
                    if s == 1:
                        recip_split(b)
                    if 2 <= s < TILES + 2:
                        normalise_q(b, 2 * (s - 2))
                    if more and 1 <= s <= TILES:
                        k_lo(b + 1, s - 1)
                    if 2 <= s < TILES + 2:
                        normalise_q(b, 2 * (s - 2) + 1)
                    if 2 <= s < TILES + 2:
                        qn_lo(b, 2 * (s - 2) + 1)
                    if s == 9:
                        layer_norm_1(CHUNKS * b, (b, 0))
                layer_norm_1_end(CHUNKS * b)

            dve.wait_ge(s_wffn, 48)
            for st in range(3):
                bias_stage(st)
            for s in range(TILES + 1):
                if s < TILES:
                    k_bias(0, s)
                if s:
                    k_lo(0, s - 1)
            for st in range(3, STAGES):
                bias_stage(st)
            dve.wait_ge(s_wcc, 1)
            dve.wait_ge(s_const, 11 + 32)
            dve.wait_ge(s_ub, 3 * STAGES)
            for m in range(STAGES):
                down_stage(m)
            with v.Fori(0, BATCH - 1) as b:
                x_lo(b + 1)
                head(b)
                slots(b, True)
                layer_norm_1(CHUNKS * b + 1, (b, QUADS))
                layer_norm_1_end(CHUNKS * b + 1)
            last_b = BATCH - 1
            head(last_b)
            slots(last_b, False)
            dve.wait_ge(s_wuh, 1)
            lo(wup_l[:, :], y_up[:, :], wup_h[:, :], s_wul)
            dve.wait_ge(s_bT, 1)
            v.tensor_tensor(bup_col[:, :], bup_raw[:, :], pz[:, 0:HT], ALU.add).then_inc(s_bc, 1)
            v.tensor_tensor(bdn_col[:, :], bcon_col[:, :], bdn_raw[:, :], ALU.add).then_inc(s_bc, 1)
            layer_norm_1(CHUNKS * last_b + 1, (last_b, QUADS))
            layer_norm_1_end(CHUNKS * last_b + 1)

            def tokens(c):
                return x1T[:, c * CH:(c + 1) * CH] if isinstance(c, int) else x1T[:, bass.ds(c * CH, CH)]

            def ffn_x_lo(c, r):
                dve.wait_ge(s_fxh, c + 1)
                lo(xT_l[:, r * CH:(r + 1) * CH], tokens(c), xT_h[:, r * CH:(r + 1) * CH], s_fxl)

            ffn_x_lo(0, 0)
            ffn_x_lo(1, 1)
            dve.wait_ge(s_wdh, 1)
            lo(wdn_l[:, :, :].rearrange("p a c -> p (a c)"), pz[:, CH:],
               wdn_h[:, :, :].rearrange("p a c -> p (a c)"), s_wdl)
            dve.wait_ge(s_bc, 2)

            def residual(c, r):
                dve.wait_ge(s_dp, c + 1)
                v.scalar_tensor_tensor(yT[r], pa[:, r * CH:(r + 1) * CH], bdn_col[:, :], tokens(c),
                                       ALU.add, ALU.add).then_inc(s_y, 1)

            def layer_norm_2(c, r):
                bank = [pc, pd][r]
                dve.wait_ge(s_yt, c + 1)
                for i in range(QUADS):
                    v.bn_stats(stats2[:, r, i, :], bank[:, i * 128:(i + 1) * 128]).then_inc(s_st2, 1)
                dve.wait_ge(s_st2, QUADS * (c + 1))
                v.memset(scratch[:, :], 0.0)
                for i in range(QUADS):
                    v.bn_aggr(mean_var2[:, r, i, :], stats2[:, r, i, :]).then_inc(s_mv2, 1)

            def layer_norm_2_end(c, r, stored):
                bank = [pc, pd][r]
                dve.wait_ge(s_rs2, c + 1)
                if stored is not None:
                    dve.wait_ge(s_out[r], 16 * stored)
                for i in range(QUADS):
                    ins = v.tensor_scalar(y_out[:, r, i, :], bank[:, i * 128:(i + 1) * 128],
                                          mean_var2[:, r, i, 0:1], rstd2[:, r, i:i + 1], ALU.subtract, ALU.mult)
                ins.then_inc(s_yo, 1)

            residual(0, 0)
            for c, r in [(1, 1), (2, 0)]:
                ffn_x_lo(c + 1, 1 - r)
                layer_norm_2(c - 1, 1 - r)
                residual(c, r)
                layer_norm_2_end(c - 1, 1 - r, None)
            with v.Fori(1, ALLCH // 2 - 1) as i:
                for n in range(2):
                    c, r = 2 * i + 1 + n, 1 - n
                    ffn_x_lo(c + 1, 1 - r)
                    layer_norm_2(c - 1, 1 - r)
                    residual(c, r)
                    layer_norm_2_end(c - 1, 1 - r, i)
            layer_norm_2(ALLCH - 2, 0)
            residual(ALLCH - 1, 1)
            layer_norm_2_end(ALLCH - 2, 0, ALLCH // 2 - 1)
            layer_norm_2(ALLCH - 1, 1)
            layer_norm_2_end(ALLCH - 1, 1, ALLCH // 2 - 1)


_INS = ['L0_attn_x', 'L0_attn_W_qkv', 'L0_attn_W_f', 'L0_attn_b_f', 'L0_attn_W_out', 'L0_attn_b_out',
        'L0_ffn_W_exp', 'L0_ffn_b_exp', 'L0_ffn_up_weights', 'L0_ffn_up_bias', 'L0_ffn_down_weights',
        'L0_ffn_W_con', 'L0_ffn_b_con', 'L0_ffn_down_bias']


def kernel(**inputs):
    import numpy as _np
    import concourse.bacc as _bacc
    from concourse import mybir as _mybir
    from concourse.bass_utils import run_bass_kernel_spmd as _run

    nc = _bacc.Bacc("TRN2", target_bir_lowering=False, num_devices=1)
    arrays, args = {}, []
    for name in _INS:
        a = _np.ascontiguousarray(inputs[name])
        arrays[f"in_{name}_dram"] = a
        args.append(nc.dram_tensor(f"in_{name}_dram", a.shape, _mybir.dt.from_np(a.dtype), kind="ExternalInput").ap())
    shape = inputs['L0_attn_x'].shape
    args.append(nc.dram_tensor("out_0_dram", shape, _mybir.dt.from_np(_np.dtype('float32')), kind="ExternalOutput").ap())
    postln_linear_attention_butterfly_ffn_kernel(nc, *args)
    r = _run(nc, [arrays], core_ids=[0])
    return r.results[0]["out_0_dram"]
```

```python
import concourse.bass as bass
from concourse import mybir
from contextlib import ExitStack


def postln_linear_attention_butterfly_ffn_kernel(
    nc: bass.Bass,
    x: bass.AP,
    W_qkv: bass.AP,
    W_f: bass.AP,
    b_f: bass.AP,
    W_out: bass.AP,
    b_out: bass.AP,
    W_exp: bass.AP,
    b_exp: bass.AP,
    up_weights: bass.AP,
    up_bias: bass.AP,
    down_weights: bass.AP,
    W_con: bass.AP,
    b_con: bass.AP,
    down_bias: bass.AP,
    out: bass.AP,
):
    fp32 = mybir.dt.float32
    fp32r = mybir.dt.float32r
    ALU = mybir.AluOpType
    ACT = mybir.ActivationFunctionType

    BATCH, N, C = x.shape
    D = W_f.shape[0]
    HD = W_out.shape[0]
    HID = W_exp.shape[1]
    STAGES = up_weights.shape[0]
    PAIRS = HD // 128
    TILES = N // 128
    CH = 512
    CHUNKS = N // CH
    STEPS = CHUNKS * PAIRS
    QUADS = CH // 128
    QT = N // 4
    HT = HID // 128
    ALLCH = BATCH * CHUNKS
    SUMS = TILES - 1
    NORM_EPS = 1e-6
    LN_EPS = 1e-5

    xs_view = x.rearrange("b (t p) c -> b p t c", p=128)
    out_view = out.rearrange("b (h t p) c -> (b h) p t c", p=128, h=CHUNKS)

    ctx = ExitStack()
    with ctx:
        def sb(name, shape, dt=fp32):
            return ctx.enter_context(nc.sbuf_tensor(name, shape, dt))

        def pb(name, shape):
            return ctx.enter_context(nc.psum_tensor(name, shape, fp32))

        def sem(name):
            return ctx.enter_context(nc.semaphore(name))

        wq_h = sb("wq_h", [128, PAIRS, 128], fp32r)
        wq_l = sb("wq_l", [128, PAIRS, 128], fp32r)
        wk_h = sb("wk_h", [128, HD], fp32r)
        wk_l = sb("wk_l", [128, HD], fp32r)
        vo = sb("vo", [128, 2 * PAIRS, 128])
        wup_h = sb("wup_h", [128, HID], fp32r)
        wup_l = sb("wup_l", [128, HID], fp32r)
        wdn_h = sb("wdn_h", [128, HT, 128], fp32r)
        wdn_l = sb("wdn_l", [128, HT, 128], fp32r)
        wf_diag = sb("wf_diag", [128, 128])
        ident = sb("ident", [128, 128])
        ones = sb("ones", [128, 1])
        head_mask = sb("head_mask", [128, PAIRS, 32])
        row_head = sb("row_head", [128, 16])
        row_part = sb("row_part", [128, 1])
        select = sb("select", [128, 16, D], fp32r)
        part_b = sb("part_b", [128, 1])
        bf_col = sb("bf_col", [128, 1])
        bf_row = sb("bf_row", [128, D])
        bout_col = sb("bout_col", [128, 1])
        bup_raw = sb("bup_raw", [128, HT])
        bup_col = sb("bup_col", [128, HT])
        bcon_col = sb("bcon_col", [128, 1])
        bdn_raw = sb("bdn_raw", [128, 1])
        bdn_col = sb("bdn_col", [128, 1])
        ln_eps = sb("ln_eps", [128, 1])
        scratch = sb("scratch", [128, 1])
        warm = sb("warm", [128, 1])
        minus_half = sb("minus_half", [128, 1])
        xs = sb("xs", [128, TILES, C])
        x_res = sb("x_res", [128, TILES, C])
        x_h = sb("x_h", [128, TILES, C], fp32r)
        x_l = sb("x_l", [128, TILES, C], fp32r)
        xT_h = sb("xT_h", [128, N], fp32r)
        xT_l = sb("xT_l", [128, N], fp32r)
        q = sb("q", [128, PAIRS, N])
        k = sb("k", [128, 2, HD])
        k_h = sb("k_h", [128, 2, HD], fp32r)
        k_l = sb("k_l", [128, 2, HD], fp32r)
        k_total = sb("k_total", [128, HD])
        kx = sb("kx", [128, HD])
        ksum_cols = sb("ksum_cols", [128, PAIRS, 32])
        m_h = sb("m_h", [128, PAIRS, C], fp32r)
        m_l = sb("m_l", [128, PAIRS, C], fp32r)
        recip = sb("recip", [128, QT])
        recip_h = sb("recip_h", [128, QT], fp32r)
        recip_parts = sb("recip_parts", [128, N], fp32r)
        qn = sb("qn", [128, 2, CH])
        qn_h = sb("qn_h", [128, 4, CH], fp32r)
        qn_l = sb("qn_l", [128, 4, CH], fp32r)
        attnT = sb("attnT", [128, CH])
        x1 = sb("x1", [128, QUADS, C])
        x1T = sb("x1T", [128, BATCH * N])
        stats = sb("stats", [128, QUADS, 6])
        mean_var = sb("mean_var", [128, QUADS, 2])
        var_eps = sb("var_eps", [128, QUADS])
        rstd = sb("rstd", [128, QUADS])
        y_up = sb("y_up", [128, HID])
        y_bias = sb("y_bias", [1, HID])
        y_dn = sb("y_dn", [128, HID])
        coef_up = sb("coef_up", [128, 2 * HID])
        coef_dn = sb("coef_dn", [128, 2 * HID])
        term = sb("term", [128, 2, HID])
        bias_term = sb("bias_term", [1, 2, HID])
        coef_scratch = nc.dram_tensor("coef_scratch", [2, STAGES, 2 * HID], fp32, kind="Internal").ap()
        stats2 = sb("stats2", [128, QUADS, 6])
        mean_var2 = sb("mean_var2", [128, QUADS, 2])
        var_eps2 = sb("var_eps2", [128, QUADS])
        rstd2 = sb("rstd2", [128, QUADS])

        q_flat = q[:, :, :].rearrange("p a n -> p (a n)")
        wqkv_raw = q_flat[:, 0:3 * HD]
        wout_diag = q_flat[:, 3 * HD:5 * HD].rearrange("p (a h c) -> p a h c", a=PAIRS, h=2)
        wT = q_flat[:, 5 * HD:8 * HD]
        wcon_raw = attnT[:, :].rearrange("p (a c) -> p a c", a=HT)
        term_dve = [attnT[:, :], x1[:, :, :].rearrange("p t c -> p (t c)")]
        hid = [[k[:, 0, :], k[:, 1, :]], [kx[:, :], k_total[:, :]]]
        hid_h = [[k_h[:, 0, :], k_h[:, 1, :]],
                 [x_h[:, :, :].rearrange("p t c -> p (t c)"), x_l[:, :, :].rearrange("p t c -> p (t c)")]]
        hid_l = [[k_l[:, 0, :], k_l[:, 1, :]],
                 [wk_h[:, :], wk_l[:, :]]]

        def tile_of(pairs, i):
            return pairs[i // 2][:, (i % 2) * CH:(i % 2 + 1) * CH]

        yT = y_up[:, :]
        y_out = y_dn[:, :].rearrange("p (t c) -> p t c", t=QUADS)

        pz = pb("pz", [128, 2 * CH])
        pa = pb("pa", [128, 2 * CH])
        pq = pb("pq", [128, 2 * CH])
        pc = pb("pc", [128, CH])
        pd = pb("pd", [128, CH])
        ring = [pz[:, 0:CH], pz[:, CH:2 * CH], pq[:, 0:CH], pq[:, CH:2 * CH]]
        early_ring = [pz[:, 0:CH], pz[:, CH:2 * CH], pa[:, CH:2 * CH]]
        xT_banks = [pz[:, 0:CH], pd[:, :]]

        s_wqkv = [sem(f"{n}_weights_loaded") for n in ("q", "k", "v")]
        s_wf = sem("wf_loaded")
        s_wout = sem("wout_loaded")
        s_bf = sem("bf_loaded")
        s_bias = sem("biases_loaded")
        s_xs = sem("xs_loaded")
        s_xres = sem("xres_loaded")
        s_wffn = sem("ffn_weights_loaded")
        s_order = sem("coefs_reordered")
        s_cu = sem("coef_up_loaded")
        s_cd = sem("coef_dn_loaded")
        s_zero = sem("zeroed")
        s_wfz = sem("wf_zeroed")
        s_const = sem("constants_made")
        s_row = sem("row_heads_done")
        s_part = sem("part_b_done")
        s_sel = sem("select_rounded")
        s_wT = sem("wT_transposed")
        s_wTa = sem("wT_copied_act")
        s_wTd = sem("wT_copied_dve")
        s_fold = sem("folded")
        s_wh = sem("folded_hi")
        s_wl = sem("folded_lo")
        s_voa = sem("vo_copied_act")
        s_vod = sem("vo_copied_dve")
        s_xTp = sem("xT_transposed")
        s_xTh = sem("xT_hi")
        s_xTl = sem("xT_lo")
        s_xh = sem("x_hi")
        s_xl = sem("x_lo")
        s_kp = sem("k_projected")
        s_kb = sem("k_biased")
        s_k = sem("k_relu")
        s_kh = sem("k_hi")
        s_kl = sem("k_lo")
        s_ks = sem("k_summed")
        s_kxt = sem("kx_tile_added")
        s_kx = sem("kx_copied")
        s_qp = sem("q_projected")
        s_q = sem("q_relu")
        s_kcol = sem("ksum_columns")
        s_kcm = sem("ksum_masked")
        s_m = sem("m_done")
        s_mh = sem("m_hi")
        s_ml = sem("m_lo")
        s_np = sem("norm_done")
        s_ne = sem("norm_plus_eps")
        s_r = sem("recip_done")
        s_rh = sem("recip_hi")
        s_rp = sem("recip_parts_done")
        s_rb = sem("recip_spread")
        s_qn = sem("qn_done")
        s_qnh = sem("qn_hi")
        s_qnlp = sem("qn_lo_pool")
        s_qnld = sem("qn_lo_dve")
        s_at = sem("attn_step_added")
        s_atc = sem("attn_copied")
        s_att = sem("attn_transposed")
        s_x1p = sem("x1_pre_done")
        s_st = sem("stats_done")
        s_mv = sem("mean_var_done")
        s_ve = sem("var_eps_done")
        s_rs = sem("rstd_done")
        s_x1 = sem("x1_done")
        s_x1t = sem("x1_transposed")
        s_x1c = sem("x1T_copied")
        s_up = sem("up_butterfly")
        s_ub = sem("up_bias_butterfly")
        s_dn = sem("down_butterfly")
        s_wct = sem("wcon_transposed")
        s_wcc = sem("wconT_copied")
        s_bT = sem("b_up_transposed")
        s_bc = sem("ffn_biases_done")
        s_wdt = sem("wdn_transposed")
        s_wuh = sem("wup_hi")
        s_wul = sem("wup_lo")
        s_wdh = sem("wdn_hi")
        s_wdl = sem("wdn_lo")
        s_fxh = sem("ffn_x_hi")
        s_fxl = sem("ffn_x_lo")
        s_h = sem("hidden_projected")
        s_g = sem("hidden_gelu")
        s_gh = sem("hidden_hi")
        s_glp = sem("hidden_lo_pool")
        s_gld = sem("hidden_lo_dve")
        s_dp = sem("down_projected")
        s_y = sem("yT_done")
        s_yt = sem("y_transposed")
        s_st2 = sem("stats2_done")
        s_mv2 = sem("mean_var2_done")
        s_ve2 = sem("var_eps2_done")
        s_rs2 = sem("rstd2_done")
        s_yo = sem("y_normalised")
        s_out = sem("out_stored")

        HALF_STEPS = STEPS // 2
        HID_POOL = HT - 1

        def wait_qn_lo(eng, b, a):
            eng.wait_ge(s_qnld if a % 2 else s_qnlp, b * HALF_STEPS + a // 2 + 1)

        FIRST = 1
        SLOTS = FIRST + PAIRS + 1
        PER_SLOT = 3
        EARLY_Q = PER_SLOT * (SLOTS - TILES)

        def spreads(s):
            return [2 * (s - FIRST), 2 * (s - FIRST) + 1] if FIRST <= s < FIRST + PAIRS else []

        def adds(s):
            return [2 * (s - FIRST - 1), 2 * (s - FIRST - 1) + 1] if FIRST < s <= FIRST + PAIRS else []

        def early_q(s):
            return range(PER_SLOT * (s - TILES), PER_SLOT * (s - TILES + 1)) if s >= TILES else []

        COPY_SLOT = FIRST + 5
        TURN_SLOT = TILES
        PART_SLOT = FIRST + 2
        PRE = 3
        PER_TURN = (STAGES - PRE) // (BATCH - 1)

        def q_bank(b, i):
            if isinstance(b, int):
                return ring[2 + i % 2]
            return ring[i % 2] if i < EARLY_Q else ring[i % 4]

        def first_q(s):
            return [2 * (s - 2), 2 * (s - 2) + 1] if s < TILES else [2 * (TILES - 2) + s - TILES]

        LAST_UP = {1: [0, 1], 2: [2, 3], 3: [4, 5], 4: [6], 5: [7], 8: [8], 9: [9]}
        LAST_DOWN = {6: [0, 1], 7: [2, 3]}

        block = ctx.enter_context(nc.Block())

        @block.sync
        def _(sp):
            def column(dst, src):
                sp.dma_start(dst, src.rearrange("(p o) -> p o", o=1)).then_inc(s_bias, 16)

            def weights(part):
                cols = slice(part * HD, (part + 1) * HD)
                sp.dma_start(wqkv_raw[:, cols], W_qkv[:, cols]).then_inc(s_wqkv[part], 16)

            weights(1)
            sp.dma_start(xs[:, :, :], xs_view[0, :, :, :]).then_inc(s_xs, 16)
            sp.dma_start(bf_row[:, :], b_f.rearrange("(o n) -> o n", o=1).to_broadcast([128, D])).then_inc(s_bf, 16)
            weights(0)
            for h in range(2):
                sp.dma_start(bf_col[h * D:(h + 1) * D, :], b_f.rearrange("(p o) -> p o", o=1)).then_inc(s_bf, 16)
            weights(2)
            sp.wait_ge(s_zero, 1)
            wo = W_out.rearrange("(a h e) c -> h e a c", h=2, e=D)
            for h in range(2):
                sp.dma_start(wout_diag[h * D:(h + 1) * D, :, h, :], wo[h, :, :, :]).then_inc(s_wout, 16)
            sp.dma_start(y_up[:, :], W_exp).then_inc(s_wffn, 16)
            sp.dma_start(y_bias[:, :], b_exp.rearrange("(a n) -> a n", a=1)).then_inc(s_wffn, 16)
            sp.dma_start(wcon_raw, W_con.rearrange("(a p) c -> p a c", p=128)).then_inc(s_wffn, 16)

            def reorder(way, st):
                w = [up_weights, down_weights][way][st, :, :, :]
                src = w.rearrange("(hi lo) i j -> lo hi (i j)", lo=1 << st)
                dst = coef_scratch[way, st, :].rearrange("(lo hi f) -> lo hi f", lo=1 << st, f=4)
                sp.dma_start(dst, src).then_inc(s_order, 16)

            def load_up(n):
                if n:
                    sp.wait_ge(s_up, 3 * n)
                    sp.wait_ge(s_ub, 3 * n)
                row = coef_scratch[0, n, :].rearrange("(o n) -> o n", o=1)
                sp.dma_start(coef_up[:, :], row.to_broadcast([128, 2 * HID])).then_inc(s_cu, 16)

            def load_down(n):
                if n:
                    sp.wait_ge(s_dn, 3 * n)
                row = coef_scratch[1, STAGES - 1 - n, :].rearrange("(o n) -> o n", o=1)
                sp.dma_start(coef_dn[:, :], row.to_broadcast([128, 2 * HID])).then_inc(s_cd, 16)

            def reorder_steps(first, end):
                for n in range(first, end):
                    reorder(0, n)
                    reorder(1, STAGES - 1 - n)
                sp.wait_ge(s_order, 32 * end)

            reorder_steps(0, 1)
            load_up(0)
            load_down(0)
            reorder_steps(1, STAGES)
            load_up(1)
            load_down(1)
            column(bout_col[:, :], b_out)
            column(bcon_col[:, :], b_con)
            column(bdn_raw[:, :], down_bias)
            for i in range(HT):
                column(bup_raw[:, i:i + 1], up_bias[i * 128:(i + 1) * 128])
            sp.dma_start(x_res[:, :, :], xs_view[0, :, :, :]).then_inc(s_xres, 16)

            def load_xs(b):
                sp.wait_ge(s_xTp, CHUNKS * b)
                sp.wait_ge(s_xh, b)
                sp.wait_ge(s_xl, b)
                sp.dma_start(xs[:, :, :], xs_view[b, :, :, :]).then_inc(s_xs, 16)

            load_xs(1)
            for n in range(2, PRE + 1):
                load_up(n)
                load_down(n)
            for b in range(BATCH - 1):
                if b + 2 < BATCH:
                    load_xs(b + 2)
                for n in range(PRE + PER_TURN * b + 1, PRE + PER_TURN * (b + 1) + 1):
                    if n < STAGES:
                        load_down(n)
                        load_up(n)
                    if n == PRE + PER_TURN * b + 1:
                        sp.wait_ge(s_x1p, CHUNKS * (b + 1))
                        sp.dma_start(x_res[:, :, :], xs_view[b + 1, :, :, :]).then_inc(s_xres, 16)
            for c in range(ALLCH):
                sp.wait_ge(s_yo, c + 1)
                sp.dma_start(out_view[c, :, :, :], y_out).then_inc(s_out, 16)
            sp.wait_ge(s_out, 16 * ALLCH)

        @block.gpsimd
        def _(pool):
            g = nc.gpsimd
            g.memset(wf_diag[:, :], 0.0).then_inc(s_wfz, 1)
            g.memset(ident[:, :], 0.0).then_inc(s_const, 1)
            pool.wait_ge(s_const, 1)
            g.affine_select(out=ident[:, :], in_=ident[:, :], compare_op=ALU.not_equal, fill=1.0, base=0,
                            pattern=[[-1, 128]], channel_multiplier=1).then_inc(s_const, 1)
            g.memset(ones[:, :], 1.0)
            g.memset(ln_eps[:, :], LN_EPS)
            g.memset(minus_half[:, :], -0.5)
            g.memset(head_mask[:, :, :], 0.0).then_inc(s_const, 1)
            pool.wait_ge(s_const, 3)
            for part in range(2):
                for half in range(2):
                    rows = head_mask[half * D:(half + 1) * D, :, :]
                    g.affine_select(out=rows, in_=rows, compare_op=ALU.not_equal, fill=1.0,
                                    base=-half - 16 * part, pattern=[[-2, PAIRS], [1, 32]],
                                    channel_multiplier=0).then_inc(s_const, 1)
                    pool.wait_ge(s_const, 4 + 2 * part + half)

            def up_part(n, j):
                w = coef_up[:, :].rearrange("p (j i f) -> p i j f", i=2, f=2)
                y = y_up[:, :].rearrange("p (o j f) -> p o j f", o=1, f=2)
                if j < 2:
                    if j == 0:
                        pool.wait_ge(s_cu, 16 * (n + 1))
                    g.tensor_tensor(term[:, j, :].rearrange("p (i j) -> p i j", i=2), w[:, :, :, j],
                                    y[:, :, :, j].to_broadcast([128, 2, HID // 2]), ALU.mult).then_inc(s_up, 1)
                else:
                    pool.wait_ge(s_up, 3 * n + 2)
                    g.tensor_tensor(y_up[:, :], term[:, 0, :], term[:, 1, :], ALU.add).then_inc(s_up, 1)
                    pool.wait_ge(s_up, 3 * n + 3)

            def up_step(n):
                for j in range(3):
                    up_part(n, j)

            def down_step(n):
                w = coef_dn[:, :].rearrange("p (j i f) -> p i j f", i=2, f=2)
                y = y_dn[:, :].rearrange("p (i j o) -> p i j o", i=2, o=1)
                pool.wait_ge(s_cd, 16 * (n + 1))
                pool.wait_ge(s_dn, 3 * n)
                for i in range(2):
                    g.tensor_tensor(term[:, i, :].rearrange("p (j f) -> p j f", f=2), w[:, i, :, :],
                                    y[:, i, :, :].to_broadcast([128, HID // 2, 2]), ALU.mult).then_inc(s_dn, 1)
                pool.wait_ge(s_dn, 3 * n + 2)
                g.tensor_tensor(y_dn[:, :], term[:, 0, :], term[:, 1, :], ALU.add).then_inc(s_dn, 1)
                pool.wait_ge(s_dn, 3 * n + 3)

            def x_lo(b):
                pool.wait_ge(s_xh, b + 1)
                g.tensor_tensor(x_l[:, :, :], xs[:, :, :], x_h[:, :, :].bitcast(fp32), ALU.subtract).then_inc(s_xl, 1)

            def k_sum(b, s):
                if s == 0:
                    return
                pool.wait_ge(s_k, b * TILES + s + 1)
                if s == 1:
                    if not isinstance(b, int):
                        pool.wait_ge(s_kcol, b)
                    g.tensor_tensor(k_total[:, :], k[:, 0, :], k[:, 1, :], ALU.add).then_inc(s_ks, 1)
                else:
                    pool.wait_ge(s_ks, b * SUMS + s - 1)
                    g.tensor_tensor(k_total[:, :], k_total[:, :], k[:, s % 2, :], ALU.add).then_inc(s_ks, 1)

            def qn_lo(b, a):
                if a % 2:
                    return
                pool.wait_ge(s_qnh, b * STEPS + a + 1)
                g.tensor_tensor(qn_l[:, a % 4, :], qn[:, a % 2, :], qn_h[:, a % 4, :].bitcast(fp32),
                                ALU.subtract).then_inc(s_qnlp, 1)

            def ln_rstd(c, ve, rs, mv, s_in, s_mid, s_done):
                pool.wait_ge(s_in, QUADS * (c + 1))
                g.tensor_tensor(ve, mv, ln_eps[:, :].to_broadcast([128, QUADS]), ALU.add).then_inc(s_mid, 1)
                pool.wait_ge(s_mid, c + 1)
                g.tensor_tensor(rs, ve, minus_half[:, :].to_broadcast([128, QUADS]), ALU.pow).then_inc(s_done, 1)

            def rstd_1(c):
                ln_rstd(c, var_eps[:, :], rstd[:, :], mean_var[:, :, 1], s_mv, s_ve, s_rs)

            def rstd_2(c):
                ln_rstd(c, var_eps2[:, :], rstd2[:, :], mean_var2[:, :, 1], s_mv2, s_ve2, s_rs2)

            def hidden_lo(c, r, tiles):
                for i in tiles:
                    pool.wait_ge(s_gh, 2 * c + i // 2 + 1)
                    g.tensor_tensor(tile_of(hid_l[r], i), tile_of(hid[r], i), tile_of(hid_h[r], i).bitcast(fp32),
                                    ALU.subtract).then_inc(s_glp, 1)

            pool.wait_ge(s_wffn, 48)
            x_lo(0)
            up_step(0)
            parts = [(n, j) for n in range(1, PRE) for j in range(3)]
            for s in range(1, TILES):
                k_sum(0, s)
                if s >= 2:
                    up_part(*parts[s - 2])
            with pool.Fori(0, BATCH - 1) as b:
                x_lo(b + 1)
                n = PRE + PER_TURN * b
                for s in range(SLOTS):
                    if s <= FIRST:
                        k_sum(b + 1, s)
                    for a in spreads(s):
                        qn_lo(b, a)
                    if FIRST < s < TILES:
                        k_sum(b + 1, s)
                    if s == TURN_SLOT:
                        down_step(n)
                rstd_1(CHUNKS * b)
                up_step(n)
                rstd_1(CHUNKS * b + 1)
                for m in range(1, PER_TURN):
                    down_step(n + m)
                    up_step(n + m)
            for s in range(FIRST, SLOTS):
                for a in spreads(s):
                    qn_lo(BATCH - 1, a)
                if s == 2:
                    hidden_lo(0, 0, [0, 1])
                if s == 3:
                    hidden_lo(0, 0, [2])
                if s == 4:
                    hidden_lo(1, 1, [0])
                if s == 5:
                    hidden_lo(1, 1, [1])
                if s == 6:
                    hidden_lo(1, 1, [2])
                if s == TURN_SLOT:
                    rstd_1(ALLCH - 2)
            hidden_lo(2, 0, [0])
            rstd_1(ALLCH - 1)
            hidden_lo(2, 0, [1])
            rstd_2(0)
            hidden_lo(2, 0, [2])

            def turn(c, r):
                hidden_lo(c + 1, 1 - r, [0])
                rstd_2(c - 1)
                hidden_lo(c + 1, 1 - r, range(1, HID_POOL))

            with pool.Fori(1, ALLCH // 2 - 1) as i:
                for r in range(2):
                    turn(2 * i + r, r)
            turn(ALLCH - 2, 0)
            rstd_2(ALLCH - 2)
            rstd_2(ALLCH - 1)

        @block.tensor
        def _(pe):
            t = nc.tensor

            def product(dst, pairs, start, stop):
                for n, (lhsT, rhs) in enumerate(pairs):
                    last = t.matmul(dst, lhsT, rhs, start=start and n == 0, stop=stop and n == len(pairs) - 1)
                return last

            def split(dst, lhs, rhs, start=True, stop=True):
                (lh, ll), (rh, rl) = lhs, rhs
                return product(dst, [(lh, rh), (lh, rl), (ll, rh)], start, stop)

            def transpose_tiles(dst, src):
                for i in range(QUADS):
                    last = t.transpose(dst[:, i * 128:(i + 1) * 128], src(i), ident[:, :])
                return last

            def transpose_weights(grp, dst):
                pe.wait_ge(s_wqkv[grp // 2], 16)
                transpose_tiles(dst, lambda i: wqkv_raw[:, (grp * 4 + i) * 128:(grp * 4 + i + 1) * 128])\
                    .then_inc(s_wT, 1)

            def fold_wf(grp, dst):
                for i in range(4):
                    col = (grp * 4 + i) * 128
                    last = t.matmul(dst[:, i * 128:(i + 1) * 128], wT[:, col:col + 128], wf_diag[:, :],
                                    start=True, stop=True)
                last.then_inc(s_fold, 1)

            def transpose_x(n, banks):
                pe.wait_ge(s_xs, 16 * (n + 1))
                for half in range(2):
                    transpose_tiles(banks[half], lambda i: xs[:, 4 * half + i, :]).then_inc(s_xTp, 1)

            def project_k(b, s):
                if s % QUADS == 0:
                    pe.wait_ge(s_xTh, CHUNKS * b + s // QUADS + 1)
                    pe.wait_ge(s_xTl, CHUNKS * b + s // QUADS + 1)
                tok = slice(s * 128, (s + 1) * 128)
                for half in range(2):
                    if s:
                        pe.wait_ge(s_kb, b * 2 * TILES + 2 * (s - 1) + half + 1)
                    cols = slice(half * CH, (half + 1) * CH)
                    split(pz[:, cols], (xT_h[:, tok], xT_l[:, tok]), (wk_h[:, cols], wk_l[:, cols])).then_inc(s_kp, 1)

            def add_kx(b, s):
                pe.wait_ge(s_kh, b * TILES + s + 1)
                pe.wait_ge(s_kl, b * TILES + s + 1)
                if s == 0:
                    pe.wait_ge(s_xh, b + 1)
                    pe.wait_ge(s_xl, b + 1)
                    if not isinstance(b, int):
                        pe.wait_ge(s_ml, b)
                for half in range(2):
                    cols = slice(half * CH, (half + 1) * CH)
                    last = split(pa[:, cols], (x_h[:, s, :], x_l[:, s, :]),
                                 (k_h[:, s % 2, cols], k_l[:, s % 2, cols]), s == 0, s == TILES - 1)
                last.then_inc(s_kxt, 1)

            def project_q(b, i):
                p, c = i // CHUNKS, i % CHUNKS
                if isinstance(b, int):
                    if i == 0:
                        pe.wait_ge(s_voa, 2)
                        pe.wait_ge(s_vod, 2)
                    elif i >= 2:
                        pe.wait_ge(s_q, i - 1)
                elif i == 0:
                    pe.wait_ge(s_kb, (b + 1) * 2 * TILES)
                elif i == EARLY_Q:
                    pe.wait_ge(s_qn, b * STEPS)
                elif 2 <= i < EARLY_Q:
                    pe.wait_ge(s_q, b * STEPS + i - 1)
                elif i >= EARLY_Q + 2:
                    pe.wait_ge(s_q, b * STEPS + i - 3)
                cols = slice(c * CH, (c + 1) * CH)
                split(q_bank(b, i), (wq_h[:, p, :], wq_l[:, p, :]), (xT_h[:, cols], xT_l[:, cols])).then_inc(s_qp, 1)

            def ksum(b):
                pe.wait_ge(s_kx, b + 1)
                pe.wait_ge(s_ks, SUMS * (b + 1))
                for p in range(PAIRS):
                    last = t.matmul(pa[:, p:p + 1], k_total[:, p * 128:(p + 1) * 128], ones[:, :],
                                    start=True, stop=True)
                last.then_inc(s_kcol, 1)

            def add_norm(b, p):
                if p == 0:
                    pe.wait_ge(s_kcm, b + 1)
                    if not isinstance(b, int):
                        pe.wait_ge(s_atc, CHUNKS * b)
                pe.wait_ge(s_q, b * STEPS + CHUNKS * (p + 1))
                for j in range(4):
                    last = t.matmul(pc[32 * j:32 * j + 32, 0:QT], ksum_cols[:, p, :],
                                    q[:, p, j * QT:(j + 1) * QT], start=p == 0, stop=p == PAIRS - 1)
                if p == PAIRS - 1:
                    last.then_inc(s_np, 1)

            def head_maps(b):
                pe.wait_ge(s_kx, b + 1)
                for p in range(PAIRS):
                    for h in range(2):
                        last = t.matmul(pa[h * D:(h + 1) * D, p * 128:(p + 1) * 128],
                                        kx[:, (2 * p + h) * D:(2 * p + h + 1) * D], vo[:, 2 * p + h, :],
                                        start=True, stop=True)
                last.then_inc(s_m, 1)

            def spread(b, a):
                c, p = a // PAIRS, a % PAIRS
                if p == 0:
                    pe.wait_ge(s_rp, 4 * b + 2 * c + 2)
                if a >= 2:
                    pe.wait_ge(s_qn, b * STEPS + a - 1)
                sel = select[:, 2 * p:2 * p + 2, :].rearrange("p h m -> p (h m)")
                t.matmul(pq[:, (a % 2) * CH:(a % 2 + 1) * CH], sel, recip_parts[:, c * CH:(c + 1) * CH],
                         start=True, stop=True).then_inc(s_rb, 1)

            def add_attn(b, a):
                c, p = a // PAIRS, a % PAIRS
                if a == 0:
                    pe.wait_ge(s_ml, b + 1)
                if a == PAIRS:
                    pe.wait_ge(s_atc, CHUNKS * b + 1)
                pe.wait_ge(s_qnh, b * STEPS + a + 1)
                wait_qn_lo(pe, b, a)
                split(pc[:, :], (m_h[:, p, :], m_l[:, p, :]), (qn_h[:, a % 4, :], qn_l[:, a % 4, :]),
                      p == 0, p == PAIRS - 1).then_inc(s_at, 1)

            def transpose_attn(c, dst):
                pe.wait_ge(s_atc, c + 1)
                transpose_tiles(dst, lambda i: attnT[:, i * 128:(i + 1) * 128]).then_inc(s_att, 1)

            def transpose_x1(c, dst):
                pe.wait_ge(s_x1, c + 1)
                transpose_tiles(dst, lambda i: x1[:, i, :]).then_inc(s_x1t, 1)

            pe.wait_ge(s_const, 2)
            transpose_weights(2, pz[:, 0:CH])
            transpose_weights(3, pz[:, CH:])
            transpose_x(0, [pa[:, 0:CH], pa[:, CH:]])
            pe.wait_ge(s_wf, 32)
            pe.wait_ge(s_wTa, 1)
            fold_wf(2, pc[:, :])
            pe.wait_ge(s_wTd, 1)
            fold_wf(3, pd[:, :])
            transpose_weights(0, pq[:, 0:CH])
            transpose_weights(1, pq[:, CH:])
            pe.wait_ge(s_wh, 2)
            pe.wait_ge(s_wl, 2)
            project_k(0, 0)
            pe.wait_ge(s_wTa, 2)
            fold_wf(0, pc[:, :])
            pe.wait_ge(s_wTd, 2)
            fold_wf(1, pd[:, :])
            transpose_weights(4, pq[:, 0:CH])
            transpose_weights(5, pq[:, CH:])
            project_k(0, 1)
            pe.wait_ge(s_wTa, 3)
            pe.wait_ge(s_wTd, 3)
            pe.wait_ge(s_wout, 32)
            pe.wait_ge(s_wh, 4)
            pe.wait_ge(s_wl, 4)
            for n, dst in enumerate([pq[:, 0:CH], pq[:, CH:], pc[:, :], pd[:, :]]):
                for i in range(2):
                    pair = 2 * n + i
                    col = 2 * HD + pair * 128
                    last = t.matmul(dst[:, i * 256:(i + 1) * 256], wT[:, col:col + 128],
                                    wout_diag[:, pair, :, :].rearrange("p h c -> p (h c)"), start=True, stop=True)
                last.then_inc(s_fold, 1)
            for s in range(2, TILES + 2):
                if s < TILES:
                    project_k(0, s)
                project_q(0, first_q(s)[0])
                add_kx(0, s - 2)
                if s == 2:
                    pe.wait_ge(s_wffn, 48)
                    transpose_tiles(pd, lambda i: wcon_raw[:, i, :]).then_inc(s_wct, 1)
                for i in first_q(s)[1:]:
                    project_q(0, i)
            project_q(0, STEPS - 2)
            ksum(0)
            project_q(0, STEPS - 1)
            for p in range(PAIRS - 1):
                add_norm(0, p)
            pe.wait_ge(s_wcc, 1)

            with t.Fori(0, BATCH - 1) as b:
                pe.wait_ge(s_q, b * STEPS + STEPS - 2)
                transpose_x(b + 1, xT_banks)
                add_norm(b, PAIRS - 1)
                head_maps(b)
                for s in range(SLOTS):
                    if s < TILES:
                        project_k(b + 1, s)
                    if s == TURN_SLOT:
                        transpose_attn(CHUNKS * b, pd)
                    for a in spreads(s)[:1]:
                        spread(b, a)
                    if s >= 2:
                        add_kx(b + 1, s - 2)
                    for a in spreads(s)[1:]:
                        spread(b, a)
                    if s <= TILES:
                        for a in adds(s):
                            add_attn(b, a)
                    for i in early_q(s)[:1]:
                        project_q(b + 1, i)
                    if s > TILES:
                        for a in adds(s)[:1]:
                            add_attn(b, a)
                    for i in early_q(s)[1:2]:
                        project_q(b + 1, i)
                    if s > TILES:
                        for a in adds(s)[1:]:
                            add_attn(b, a)
                    for i in early_q(s)[2:]:
                        project_q(b + 1, i)
                for i in range(EARLY_Q, STEPS):
                    project_q(b + 1, i)
                    n = i - EARLY_Q
                    if n == 0:
                        transpose_x1(CHUNKS * b, pd)
                    if n == 1:
                        ksum(b + 1)
                    if n == 2:
                        pe.wait_ge(s_x1c, CHUNKS * b + 1)
                        transpose_attn(CHUNKS * b + 1, pd)
                    if n >= 3:
                        add_norm(b + 1, n - 3)
                    if i == STEPS - 2:
                        transpose_x1(CHUNKS * b + 1, pd)
                pe.wait_ge(s_x1c, CHUNKS * (b + 1))
            last_b = BATCH - 1
            pe.wait_ge(s_q, last_b * STEPS + STEPS - 2)
            pe.wait_ge(s_ub, 3 * STAGES)
            for i in range(HT):
                last = t.matmul(pz[:, i:i + 1], y_bias[:, i * 128:(i + 1) * 128], ones[0:1, :],
                                start=True, stop=True)
            last.then_inc(s_bT, 1)
            add_norm(last_b, PAIRS - 1)
            head_maps(last_b)
            pe.wait_ge(s_dn, 3 * STAGES)
            transpose_tiles(pz[:, CH:], lambda i: y_dn[:, i * 128:(i + 1) * 128]).then_inc(s_wdt, 1)

            def up_tile(c, r, i, bank):
                if i == 0:
                    pe.wait_ge(s_fxh, c + 1)
                    pe.wait_ge(s_fxl, c + 1)
                cols = slice(i * 128, (i + 1) * 128)
                tok = slice(r * CH, (r + 1) * CH)
                split(bank, (wup_h[:, cols], wup_l[:, cols]), (xT_h[:, tok], xT_l[:, tok])).then_inc(s_h, 1)

            def up(c, r):
                for i in range(HT):
                    pe.wait_ge(s_g, HT * (c - 1) + i + 1)
                    up_tile(c, r, i, ring[i])

            def early_up(u):
                n = len(early_ring)
                if u == 0:
                    pe.wait_ge(s_bc, 2)
                    pe.wait_ge(s_wuh, 1)
                    pe.wait_ge(s_wul, 1)
                if u == 1:
                    pe.wait_ge(s_wdh, 1)
                    pe.wait_ge(s_wdl, 1)
                if u == 2:
                    pe.wait_ge(s_mh, BATCH)
                    pe.wait_ge(s_ml, BATCH)
                if u >= n:
                    pe.wait_ge(s_g, u - n + 1)
                up_tile(u // HT, u // HT % 2, u % HT, early_ring[u % n])

            def down_tile(c, r, i):
                if i == 0 and (not isinstance(c, int) or c):
                    pe.wait_ge(s_y, c)
                if i < HID_POOL:
                    pe.wait_ge(s_glp, HID_POOL * c + i + 1)
                else:
                    pe.wait_ge(s_gld, c + 1)
                last = split(pa[:, 0:CH], (wdn_h[:, i, :], wdn_l[:, i, :]),
                             (tile_of(hid_h[r], i), tile_of(hid_l[r], i)), i == 0, i == HT - 1)
                if i == HT - 1:
                    last.then_inc(s_dp, 1)

            def down(c, r):
                for i in range(HT):
                    down_tile(c, r, i)

            def transpose_y(c):
                pe.wait_ge(s_y, c + 1)
                if not isinstance(c, int) or c:
                    pe.wait_ge(s_yo, c)
                transpose_tiles(pd, lambda i: yT[:, i * 128:(i + 1) * 128]).then_inc(s_yt, 1)

            for s in range(FIRST, SLOTS):
                ups = LAST_UP.get(s, [])
                for a in spreads(s):
                    spread(last_b, a)
                if s == COPY_SLOT:
                    transpose_attn(ALLCH - 2, pd)
                for u in ups[:1]:
                    early_up(u)
                for a in adds(s)[:1]:
                    add_attn(last_b, a)
                for u in ups[1:]:
                    early_up(u)
                for i in LAST_DOWN.get(s, []):
                    down_tile(0, 0, i)
                for a in adds(s)[1:]:
                    add_attn(last_b, a)
            early_up(10)
            pe.wait_ge(s_qn, BATCH * STEPS)
            transpose_attn(ALLCH - 1, pq[:, 0:CH])
            transpose_x1(ALLCH - 2, pc)
            early_up(11)
            down_tile(1, 1, 0)
            down_tile(1, 1, 1)
            transpose_y(0)
            down_tile(1, 1, 2)
            down_tile(1, 1, 3)
            transpose_x1(ALLCH - 1, pq[:, CH:])
            pe.wait_ge(s_x1c, ALLCH)
            pe.wait_ge(s_g, HT * 3 - 2)
            with t.Fori(1, ALLCH // 2 - 1) as i:
                for r in range(2):
                    c = 2 * i + r
                    up(c + 1, 1 - r)
                    transpose_y(c - 1)
                    down(c, r)
            up(ALLCH - 1, 1)
            transpose_y(ALLCH - 3)
            down(ALLCH - 2, 0)
            transpose_y(ALLCH - 2)
            down(ALLCH - 1, 1)
            transpose_y(ALLCH - 1)

        @block.scalar
        def _(act):
            a_ = nc.scalar
            act.wait_ge(s_wfz, 1)
            for h in range(2):
                act.dma_start(wf_diag[h * D:(h + 1) * D, h * D:(h + 1) * D], W_f).then_inc(s_wf, 16)
            a_.activation(warm[0:D, :], wf_diag[0:D, D:D + 1], ACT.Copy)

            def hi(dst, src, done):
                a_.activation(dst, src, ACT.Copy).then_inc(done, 1)

            def wT_copy(n, grp, bank):
                act.wait_ge(s_wT, n)
                a_.activation(wT[:, grp * CH:(grp + 1) * CH], bank, ACT.Copy).then_inc(s_wTa, 1)

            def xT_hi(b, c, bank):
                act.wait_ge(s_xTp, CHUNKS * b + c + 1)
                hi(xT_h[:, c * CH:(c + 1) * CH], bank, s_xTh)

            def x_hi(b):
                hi(x_h[:, :, :], xs[:, :, :], s_xh)

            def k_relu(b, s):
                act.wait_ge(s_kb, b * 2 * TILES + 2 * s + 2)
                kt = k[:, s % 2, :]
                a_.activation(kt, kt, ACT.Relu).then_inc(s_k, 1)

            def k_hi(b, s):
                if s >= 2:
                    act.wait_ge(s_kxt, b * TILES + s - 1)
                act.wait_ge(s_k, b * TILES + s + 1)
                hi(k_h[:, s % 2, :], k[:, s % 2, :], s_kh)

            def kx_copy(b):
                act.wait_ge(s_kxt, TILES * (b + 1))
                a_.activation(kx[:, :], pa[:, :], ACT.Copy).then_inc(s_kx, 1)

            def q_relu(b, i):
                p, c = i // CHUNKS, i % CHUNKS
                act.wait_ge(s_qp, b * STEPS + i + 1)
                if not isinstance(b, int):
                    act.wait_ge(s_qn, (b - 1) * STEPS + c * PAIRS + p + 1)
                a_.activation(q[:, p, c * CH:(c + 1) * CH], q_bank(b, i), ACT.Relu, bias=bf_col[:, :])\
                    .then_inc(s_q, 1)

            def qn_hi(b, a):
                act.wait_ge(s_qn, b * STEPS + a + 1)
                if a >= 4:
                    act.wait_ge(s_at, b * STEPS + a - 3)
                hi(qn_h[:, a % 4, :], qn[:, a % 2, :], s_qnh)

            def attn_copy(c):
                act.wait_ge(s_at, PAIRS * (c + 1))
                a_.activation(attnT[:, :], pc[:, :], ACT.Identity, bias=bout_col[:, :]).then_inc(s_atc, 1)

            def tokens(c):
                return x1T[:, c * CH:(c + 1) * CH] if isinstance(c, int) else x1T[:, bass.ds(c * CH, CH)]

            def x1T_copy(c, bank):
                act.wait_ge(s_x1t, c + 1)
                a_.activation(tokens(c), bank, ACT.Copy).then_inc(s_x1c, 1)

            def m_hi(b):
                act.wait_ge(s_m, b + 1)
                hi(m_h[:, :, :].rearrange("p a c -> p (a c)"), pa[:, :], s_mh)

            def norm_eps(b):
                act.wait_ge(s_np, b + 1)
                a_.activation(recip[:, :], pc[:, 0:QT], ACT.Copy, bias=NORM_EPS).then_inc(s_ne, 1)

            def recip_hi(b):
                act.wait_ge(s_r, b + 1)
                hi(recip_h[:, :], recip[:, :], s_rh)

            wT_copy(1, 2, pz[:, 0:CH])
            xT_hi(0, 0, pa[:, 0:CH])
            xT_hi(0, 1, pa[:, CH:])
            for half, bank in enumerate([pc, pd]):
                act.wait_ge(s_fold, half + 1)
                hi(wk_h[:, half * CH:(half + 1) * CH], bank[:, :], s_wh)
            wT_copy(3, 0, pq[:, 0:CH])
            x_hi(0)
            act.wait_ge(s_bf, 48)
            k_relu(0, 0)
            wq_flat = wq_h[:, :, :].rearrange("p a m -> p (a m)")
            for half, bank in enumerate([pc, pd]):
                act.wait_ge(s_fold, half + 3)
                hi(wq_flat[:, half * CH:(half + 1) * CH], bank[:, :], s_wh)
            wT_copy(5, 4, pq[:, 0:CH])
            k_hi(0, 0)
            k_relu(0, 1)
            vo_flat = vo[:, :, :].rearrange("p a m -> p (a m)")
            for n, bank in [(0, pq[:, 0:CH]), (2, pc[:, :])]:
                act.wait_ge(s_fold, 5 + n)
                a_.activation(vo_flat[:, n * CH:(n + 1) * CH], bank, ACT.Copy).then_inc(s_voa, 1)
            k_hi(0, 1)
            act.wait_ge(s_fold, 8)
            for s in range(2, TILES + 2):
                if s < TILES:
                    k_relu(0, s)
                q_relu(0, first_q(s)[0])
                if s < TILES:
                    k_hi(0, s)
                if s == 2:
                    act.wait_ge(s_wct, 1)
                    a_.activation(y_dn[:, :], pd[:, :], ACT.Copy).then_inc(s_wcc, 1)
                for i in first_q(s)[1:]:
                    q_relu(0, i)
                if s == 4:
                    act.wait_ge(s_row, 2)
                    hi(select[:, :, :], row_head[:, :].rearrange("p (h o) -> p h o", o=1)
                       .to_broadcast([128, 16, D]), s_sel)
                    a_.activation(part_b[:, :], row_part[:, :], ACT.Copy, scale=-1.0).then_inc(s_part, 1)
                    a_.activation(recip_parts[:, :].rearrange("p (a c) -> p a c", c=128),
                                  ident[:, :].rearrange("p (o c) -> p o c", o=1).to_broadcast([128, N // 128, 128]),
                                  ACT.Copy, scale=0.0).then_inc(s_part, 1)
            kx_copy(0)
            q_relu(0, STEPS - 2)
            q_relu(0, STEPS - 1)
            act.wait_ge(s_bias, 16 * (3 + HT))
            with a_.Fori(0, BATCH - 1) as b:
                xT_hi(b + 1, 0, xT_banks[0])
                norm_eps(b)
                xT_hi(b + 1, 1, xT_banks[1])
                x_hi(b + 1)
                m_hi(b)
                recip_hi(b)
                for s in range(SLOTS):
                    if s == COPY_SLOT:
                        attn_copy(CHUNKS * b)
                    if s < TILES:
                        k_relu(b + 1, s)
                    for a in spreads(s)[:1]:
                        qn_hi(b, a)
                    if s < TILES:
                        k_hi(b + 1, s)
                    for i in early_q(s)[:1]:
                        q_relu(b + 1, i)
                    for a in spreads(s)[1:]:
                        qn_hi(b, a)
                    for i in early_q(s)[1:]:
                        q_relu(b + 1, i)
                kx_copy(b + 1)
                attn_copy(CHUNKS * b + 1)
                for i in range(EARLY_Q, STEPS):
                    q_relu(b + 1, i)
                    if i == EARLY_Q:
                        x1T_copy(CHUNKS * b, pd[:, :])
                    if i == STEPS - 2:
                        x1T_copy(CHUNKS * b + 1, pd[:, :])
            last_b = BATCH - 1

            def ffn_x_hi(c, r):
                if not isinstance(c, int) or c >= 2:
                    act.wait_ge(s_h, HT * (c - 1))
                hi(xT_h[:, r * CH:(r + 1) * CH], tokens(c), s_fxh)

            def gelu_tile(c, r, i, bank):
                act.wait_ge(s_h, HT * c + i + 1)
                if i == 0 and (not isinstance(c, int) or c >= 2):
                    act.wait_ge(s_glp, HID_POOL * (c - 1))
                    act.wait_ge(s_gld, c - 1)
                a_.activation(tile_of(hid[r], i), bank, ACT.Gelu, bias=bup_col[:, i:i + 1]).then_inc(s_g, 1)
                if i % 2:
                    act.wait_ge(s_g, HT * c + i + 1)
                    if i == 1 and (not isinstance(c, int) or c >= 2):
                        act.wait_ge(s_dp, c - 1)
                    hi(hid_h[r][i // 2], hid[r][i // 2], s_gh)

            def gelu(c, r):
                for i in range(HT):
                    gelu_tile(c, r, i, ring[i])

            def early_gelu(u):
                gelu_tile(u // HT, u // HT % 2, u % HT, early_ring[u % len(early_ring)])

            norm_eps(last_b)
            act.wait_ge(s_up, 3 * STAGES)
            hi(wup_h[:, :], y_up[:, :], s_wuh)
            recip_hi(last_b)
            ffn_x_hi(0, 0)
            m_hi(last_b)
            act.wait_ge(s_wdt, 1)
            hi(wdn_h[:, :, :].rearrange("p a c -> p (a c)"), pz[:, CH:], s_wdh)
            ffn_x_hi(1, 1)
            a_.activation(warm[0:D, :], wf_diag[0:D, D:D + 1], ACT.Gelu)
            act.wait_ge(s_bc, 2)
            for s in range(FIRST, SLOTS):
                for a in spreads(s):
                    qn_hi(last_b, a)
                if s == COPY_SLOT - 1:
                    attn_copy(ALLCH - 2)
                for u in LAST_UP.get(s, []):
                    early_gelu(u)
                if s == 3:
                    ffn_x_hi(2, 0)
                if s == 6:
                    ffn_x_hi(3, 1)
            attn_copy(ALLCH - 1)
            early_gelu(10)
            x1T_copy(ALLCH - 2, pc[:, :])
            early_gelu(11)
            x1T_copy(ALLCH - 1, pq[:, CH:])
            with a_.Fori(1, ALLCH // 2 - 1) as i:
                for r in range(2):
                    ffn_x_hi(2 * i + r + 2, r)
                    gelu(2 * i + r + 1, 1 - r)
            gelu(ALLCH - 1, 1)

        @block.vector
        def _(dve):
            v = nc.vector

            def lo(dst, src, high, done):
                v.tensor_tensor(dst, src, high.bitcast(fp32), ALU.subtract).then_inc(done, 1)

            def wT_copy(n, grp, bank):
                dve.wait_ge(s_wT, n)
                v.tensor_copy(wT[:, grp * CH:(grp + 1) * CH], bank).then_inc(s_wTd, 1)

            def xT_lo(b, c, bank):
                dve.wait_ge(s_xTh, CHUNKS * b + c + 1)
                cols = slice(c * CH, (c + 1) * CH)
                lo(xT_l[:, cols], bank, xT_h[:, cols], s_xTl)

            def k_bias(b, s):
                for half in range(2):
                    dve.wait_ge(s_kp, b * 2 * TILES + 2 * s + half + 1)
                    if half == 0 and s >= 2:
                        dve.wait_ge(s_ks, b * SUMS + max(1, s - 2))
                        dve.wait_ge(s_kl, b * TILES + s - 1)
                    if half == 0 and s < 2 and not isinstance(b, int):
                        dve.wait_ge(s_ks, b * SUMS)
                        dve.wait_ge(s_kl, b * TILES)
                    cols = slice(half * CH, (half + 1) * CH)
                    v.tensor_tensor(k[:, s % 2, cols].rearrange("p (h d) -> p h d", d=D),
                                    pz[:, cols].rearrange("p (h d) -> p h d", d=D),
                                    bf_row[:, :].rearrange("p (o d) -> p o d", o=1).to_broadcast([128, CH // D, D]),
                                    ALU.add).then_inc(s_kb, 1)

            def k_lo(b, s):
                dve.wait_ge(s_kh, b * TILES + s + 1)
                lo(k_l[:, s % 2, :], k[:, s % 2, :], k_h[:, s % 2, :], s_kl)

            def normalise_q(b, a):
                c, p = a // PAIRS, a % PAIRS
                dve.wait_ge(s_rb, b * STEPS + a + 1)
                if a >= 2:
                    wait_qn_lo(dve, b, a - 2)
                v.tensor_tensor(qn[:, a % 2, :], q[:, p, c * CH:(c + 1) * CH], pq[:, (a % 2) * CH:(a % 2 + 1) * CH],
                                ALU.mult).then_inc(s_qn, 1)

            def qn_lo(b, a):
                dve.wait_ge(s_qnh, b * STEPS + a + 1)
                lo(qn_l[:, a % 4, :], qn[:, a % 2, :], qn_h[:, a % 4, :], s_qnld)

            def add_x(b, c, bank):
                n = CHUNKS * b + c
                dve.wait_ge(s_att, n + 1)
                dve.wait_ge(s_xres, 16 * (b + 1))
                if c:
                    dve.wait_ge(s_x1t, n)
                v.tensor_tensor(x1[:, :, :], bank.rearrange("p (t c) -> p t c", t=QUADS),
                                x_res[:, c * QUADS:(c + 1) * QUADS, :], ALU.add).then_inc(s_x1p, 1)

            def norm_stats_1(b, c):
                n = CHUNKS * b + c
                dve.wait_ge(s_x1p, n + 1)
                for i in range(QUADS):
                    v.bn_stats(stats[:, i, :], x1[:, i, :]).then_inc(s_st, 1)
                dve.wait_ge(s_st, QUADS * (n + 1))
                v.memset(scratch[:, :], 0.0)
                for i in range(QUADS):
                    v.bn_aggr(mean_var[:, i, :], stats[:, i, :]).then_inc(s_mv, 1)

            def layer_norm_1(b, c, bank):
                add_x(b, c, bank)
                norm_stats_1(b, c)

            def layer_norm_1_end(b, c):
                dve.wait_ge(s_rs, CHUNKS * b + c + 1)
                for i in range(QUADS):
                    ins = v.tensor_scalar(x1[:, i, :], x1[:, i, :], mean_var[:, i, 0:1], rstd[:, i:i + 1],
                                          ALU.subtract, ALU.mult)
                ins.then_inc(s_x1, 1)

            def bias_step(n):
                w = coef_up[0:1, :].rearrange("p (j i f) -> p i j f", i=2, f=2)
                y = y_bias[:, :].rearrange("p (o j f) -> p o j f", o=1, f=2)
                dve.wait_ge(s_cu, 16 * (n + 1))
                for f in range(2):
                    v.tensor_tensor(bias_term[:, f, :].rearrange("p (i j) -> p i j", i=2), w[:, :, :, f],
                                    y[:, :, :, f].to_broadcast([1, 2, HID // 2]), ALU.mult).then_inc(s_ub, 1)
                dve.wait_ge(s_ub, 3 * n + 2)
                v.tensor_tensor(y_bias[:, :], bias_term[:, 0, :], bias_term[:, 1, :], ALU.add).then_inc(s_ub, 1)
                dve.wait_ge(s_ub, 3 * n + 3)

            def down_step(n):
                w = coef_dn[:, :].rearrange("p (j i f) -> p i j f", i=2, f=2)
                y = y_dn[:, :].rearrange("p (i j o) -> p i j o", i=2, o=1)
                dve.wait_ge(s_wcc, 1)
                dve.wait_ge(s_cd, 16 * (n + 1))
                for i in range(2):
                    v.tensor_tensor(term_dve[i].rearrange("p (j f) -> p j f", f=2), w[:, i, :, :],
                                    y[:, i, :, :].to_broadcast([128, HID // 2, 2]), ALU.mult).then_inc(s_dn, 1)
                dve.wait_ge(s_dn, 3 * n + 2)
                v.tensor_tensor(y_dn[:, :], term_dve[0], term_dve[1], ALU.add).then_inc(s_dn, 1)
                dve.wait_ge(s_dn, 3 * n + 3)

            def m_lo(b):
                dve.wait_ge(s_mh, b + 1)
                lo(m_l[:, :, :].rearrange("p a c -> p (a c)"), pa[:, :],
                   m_h[:, :, :].rearrange("p a c -> p (a c)"), s_ml)

            def ksum_mask(b):
                dve.wait_ge(s_kcol, b + 1)
                v.tensor_tensor(ksum_cols[:, :, :], head_mask[:, :, :],
                                pa[:, 0:PAIRS].rearrange("p (a o) -> p a o", o=1).to_broadcast([128, PAIRS, 32]),
                                ALU.mult).then_inc(s_kcm, 1)

            def reciprocal(b):
                dve.wait_ge(s_ne, b + 1)
                v.reciprocal(recip[:, :], recip[:, :]).then_inc(s_r, 1)

            def recip_split(b, c):
                dve.wait_ge(s_rh, b + 1)
                for j in range(2 * c, 2 * c + 2):
                    rows = slice(32 * j, 32 * j + 32)
                    v.scalar_tensor_tensor(recip_parts[rows, j * QT:(j + 1) * QT], recip_h[rows, :].bitcast(fp32),
                                           part_b[rows, :], recip[rows, :], ALU.mult, ALU.add).then_inc(s_rp, 1)

            v.memset(wout_diag, 0.0).then_inc(s_zero, 1)
            wT_copy(2, 3, pz[:, CH:])
            xT_lo(0, 0, pa[:, 0:CH])
            for half, bank in enumerate([pc, pd]):
                cols = slice(half * CH, (half + 1) * CH)
                dve.wait_ge(s_wh, half + 1)
                lo(wk_l[:, cols], bank[:, :], wk_h[:, cols], s_wl)
            wT_copy(4, 1, pq[:, CH:])
            dve.wait_ge(s_bf, 48)
            k_bias(0, 0)
            xT_lo(0, 1, pa[:, CH:])
            wq_lf = wq_l[:, :, :].rearrange("p a m -> p (a m)")
            wq_hf = wq_h[:, :, :].rearrange("p a m -> p (a m)")
            for half, bank in enumerate([pc, pd]):
                cols = slice(half * CH, (half + 1) * CH)
                dve.wait_ge(s_wh, 3 + half)
                lo(wq_lf[:, cols], bank[:, :], wq_hf[:, cols], s_wl)
            wT_copy(6, 5, pq[:, CH:])
            k_bias(0, 1)
            vo_flat = vo[:, :, :].rearrange("p a m -> p (a m)")
            for n, bank in [(1, pq[:, CH:]), (3, pd[:, :])]:
                dve.wait_ge(s_fold, 5 + n)
                v.tensor_copy(vo_flat[:, n * CH:(n + 1) * CH], bank).then_inc(s_vod, 1)
            k_lo(0, 0)
            dve.wait_ge(s_const, 2)
            v.reduce_sum(row_head[:, :], ident[:, :].rearrange("p (k i) -> p i k", i=16),
                         axis=mybir.AxisListType.X).then_inc(s_row, 1)
            part_cols = ident[:, :].rearrange("p (k b i) -> p b k i", b=2, i=16)[:, 1, :, :]
            v.reduce_sum(row_part[:, :], part_cols, axis=mybir.AxisListType.XY).then_inc(s_row, 1)
            dve.wait_ge(s_wffn, 48)
            for s in range(2, TILES + 1):
                if s < TILES:
                    k_bias(0, s)
                k_lo(0, s - 1)
                if s % 2 == 0 and s // 2 <= PRE:
                    bias_step(s // 2 - 1)
                if s % 2 and s // 2 <= PRE:
                    down_step(s // 2 - 1)
            dve.wait_ge(s_const, 7)
            ksum_mask(0)
            dve.wait_ge(s_part, 2)
            with v.Fori(0, BATCH - 1) as b:
                xT_lo(b + 1, 0, xT_banks[0])
                reciprocal(b)
                for s in range(SLOTS):
                    if s < TILES:
                        k_bias(b + 1, s)
                    for a in spreads(s - 1)[1:]:
                        qn_lo(b, a)
                    if s == 0:
                        recip_split(b, 0)
                    for a in spreads(s)[:1]:
                        normalise_q(b, a)
                    if s == FIRST:
                        m_lo(b)
                    if 1 <= s <= TILES:
                        k_lo(b + 1, s - 1)
                    for a in spreads(s)[1:]:
                        normalise_q(b, a)
                    if s == FIRST + 1:
                        xT_lo(b + 1, 1, xT_banks[1])
                    if s == PART_SLOT:
                        recip_split(b, 1)
                    if s == TURN_SLOT:
                        layer_norm_1(b, 0, pd[:, :])
                layer_norm_1_end(b, 0)
                ksum_mask(b + 1)
                layer_norm_1(b, 1, pd[:, :])
                bias_step(PRE + PER_TURN * b)
                layer_norm_1_end(b, 1)
                for n in range(1, PER_TURN):
                    bias_step(PRE + PER_TURN * b + n)
            last_b = BATCH - 1

            def tokens(c):
                return x1T[:, c * CH:(c + 1) * CH] if isinstance(c, int) else x1T[:, bass.ds(c * CH, CH)]

            def ffn_x_lo(c, r):
                dve.wait_ge(s_fxh, c + 1)
                lo(xT_l[:, r * CH:(r + 1) * CH], tokens(c), xT_h[:, r * CH:(r + 1) * CH], s_fxl)

            def hidden_lo(c, r):
                for i in range(HID_POOL, HT):
                    dve.wait_ge(s_gh, 2 * (c + 1))
                    lo(tile_of(hid_l[r], i), tile_of(hid[r], i), tile_of(hid_h[r], i), s_gld)

            def residual(c):
                dve.wait_ge(s_dp, c + 1)
                v.scalar_tensor_tensor(yT, pa[:, 0:CH], bdn_col[:, :], tokens(c), ALU.add, ALU.add).then_inc(s_y, 1)

            def layer_norm_2(c):
                dve.wait_ge(s_yt, c + 1)
                for i in range(QUADS):
                    v.bn_stats(stats2[:, i, :], pd[:, i * 128:(i + 1) * 128]).then_inc(s_st2, 1)
                dve.wait_ge(s_st2, QUADS * (c + 1))
                v.memset(scratch[:, :], 0.0)
                for i in range(QUADS):
                    v.bn_aggr(mean_var2[:, i, :], stats2[:, i, :]).then_inc(s_mv2, 1)

            def layer_norm_2_end(c):
                dve.wait_ge(s_rs2, c + 1)
                if not isinstance(c, int) or c:
                    dve.wait_ge(s_out, 16 * c)
                for i in range(QUADS):
                    ins = v.tensor_scalar(y_out[:, i, :], pd[:, i * 128:(i + 1) * 128],
                                          mean_var2[:, i, 0:1], rstd2[:, i:i + 1], ALU.subtract, ALU.mult)
                ins.then_inc(s_yo, 1)

            dve.wait_ge(s_bT, 1)
            v.tensor_tensor(bup_col[:, :], bup_raw[:, :], pz[:, 0:HT], ALU.add).then_inc(s_bc, 1)
            v.tensor_tensor(bdn_col[:, :], bcon_col[:, :], bdn_raw[:, :], ALU.add).then_inc(s_bc, 1)
            reciprocal(last_b)
            dve.wait_ge(s_wuh, 1)
            lo(wup_l[:, :], y_up[:, :], wup_h[:, :], s_wul)
            recip_split(last_b, 0)
            ffn_x_lo(0, 0)
            m_lo(last_b)
            dve.wait_ge(s_wdh, 1)
            lo(wdn_l[:, :, :].rearrange("p a c -> p (a c)"), pz[:, CH:],
               wdn_h[:, :, :].rearrange("p a c -> p (a c)"), s_wdl)
            ffn_x_lo(1, 1)
            for s in range(FIRST, SLOTS):
                for a in spreads(s - 1)[1:]:
                    qn_lo(last_b, a)
                for a in spreads(s):
                    normalise_q(last_b, a)
                if s == PART_SLOT:
                    recip_split(last_b, 1)
                    hidden_lo(0, 0)
                if s == 4:
                    ffn_x_lo(2, 0)
                if s == 6:
                    hidden_lo(1, 1)
                if s == 7:
                    ffn_x_lo(3, 1)
                    add_x(last_b, 0, pd[:, :])
                    norm_stats_1(last_b, 0)
                if s == 8:
                    residual(0)
                    layer_norm_1_end(last_b, 0)
            layer_norm_1(last_b, 1, pq[:, 0:CH])
            layer_norm_2(0)
            layer_norm_1_end(last_b, 1)
            hidden_lo(2, 0)
            residual(1)
            layer_norm_2_end(0)
            with v.Fori(1, ALLCH // 2 - 1) as i:
                for r in range(2):
                    c = 2 * i + r
                    ffn_x_lo(c + 2, r)
                    layer_norm_2(c - 1)
                    hidden_lo(c + 1, 1 - r)
                    residual(c)
                    layer_norm_2_end(c - 1)
            layer_norm_2(ALLCH - 3)
            hidden_lo(ALLCH - 1, 1)
            residual(ALLCH - 2)
            layer_norm_2_end(ALLCH - 3)
            layer_norm_2(ALLCH - 2)
            residual(ALLCH - 1)
            layer_norm_2_end(ALLCH - 2)
            layer_norm_2(ALLCH - 1)
            layer_norm_2_end(ALLCH - 1)


_INS = ['L0_attn_x', 'L0_attn_W_qkv', 'L0_attn_W_f', 'L0_attn_b_f', 'L0_attn_W_out', 'L0_attn_b_out',
        'L0_ffn_W_exp', 'L0_ffn_b_exp', 'L0_ffn_up_weights', 'L0_ffn_up_bias', 'L0_ffn_down_weights',
        'L0_ffn_W_con', 'L0_ffn_b_con', 'L0_ffn_down_bias']


def kernel(**inputs):
    import numpy as _np
    import concourse.bacc as _bacc
    from concourse import mybir as _mybir
    from concourse.bass_utils import run_bass_kernel_spmd as _run

    nc = _bacc.Bacc("TRN2", target_bir_lowering=False, num_devices=1)
    arrays, args = {}, []
    for name in _INS:
        a = _np.ascontiguousarray(inputs[name])
        arrays[f"in_{name}_dram"] = a
        args.append(nc.dram_tensor(f"in_{name}_dram", a.shape, _mybir.dt.from_np(a.dtype), kind="ExternalInput").ap())
    shape = inputs['L0_attn_x'].shape
    args.append(nc.dram_tensor("out_0_dram", shape, _mybir.dt.from_np(_np.dtype('float32')), kind="ExternalOutput").ap())
    postln_linear_attention_butterfly_ffn_kernel(nc, *args)
    r = _run(nc, [arrays], core_ids=[0])
    return r.results[0]["out_0_dram"]
```

```python
import concourse.bass as bass
from concourse import mybir
from contextlib import ExitStack


def postln_linear_attention_butterfly_ffn_kernel(
    nc: bass.Bass,
    x: bass.AP,
    W_qkv: bass.AP,
    W_f: bass.AP,
    b_f: bass.AP,
    W_out: bass.AP,
    b_out: bass.AP,
    W_exp: bass.AP,
    b_exp: bass.AP,
    up_weights: bass.AP,
    up_bias: bass.AP,
    down_weights: bass.AP,
    W_con: bass.AP,
    b_con: bass.AP,
    down_bias: bass.AP,
    out: bass.AP,
):
    fp32 = mybir.dt.float32
    fp32r = mybir.dt.float32r
    ALU = mybir.AluOpType
    ACT = mybir.ActivationFunctionType

    BATCH, N, C = x.shape
    D = W_f.shape[0]
    HD = W_out.shape[0]
    HID = W_exp.shape[1]
    STAGES = up_weights.shape[0]
    PAIRS = HD // 128
    TILES = N // 128
    CH = 512
    CHUNKS = N // CH
    STEPS = CHUNKS * PAIRS
    QUADS = CH // 128
    QT = N // 4
    HT = HID // 128
    ALLCH = BATCH * CHUNKS
    NORM_EPS = 1e-6
    LN_EPS = 1e-5

    xs_view = x.rearrange("b (t p) c -> b p t c", p=128)
    out_view = out.rearrange("b (h t p) c -> (b h) p t c", p=128, h=CHUNKS)

    ctx = ExitStack()
    with ctx:
        def sb(name, shape, dt=fp32):
            return ctx.enter_context(nc.sbuf_tensor(name, shape, dt))

        def pb(name, shape):
            return ctx.enter_context(nc.psum_tensor(name, shape, fp32))

        def sem(name):
            return ctx.enter_context(nc.semaphore(name))

        wq_h = sb("wq_h", [128, PAIRS, 128], fp32r)
        wq_l = sb("wq_l", [128, PAIRS, 128], fp32r)
        wk_h = sb("wk_h", [128, HD], fp32r)
        wk_l = sb("wk_l", [128, HD], fp32r)
        vo = sb("vo", [128, 2 * PAIRS, 128])
        wup_h = sb("wup_h", [128, HID], fp32r)
        wup_l = sb("wup_l", [128, HID], fp32r)
        wdn_h = sb("wdn_h", [128, HT, 128], fp32r)
        wdn_l = sb("wdn_l", [128, HT, 128], fp32r)
        wf_diag = sb("wf_diag", [128, 128])
        ident = sb("ident", [128, 128])
        ones = sb("ones", [128, 1])
        head_mask = sb("head_mask", [128, PAIRS, 32])
        row_head = sb("row_head", [128, 16])
        row_part = sb("row_part", [128, 1])
        select = sb("select", [128, 16, D], fp32r)
        part_b = sb("part_b", [128, 1])
        bf_col = sb("bf_col", [128, 1])
        bf_row = sb("bf_row", [128, D])
        bf_h = sb("bf_h", [128, D], fp32r)
        bf_rows = sb("bf_rows", [128, CH], fp32r)
        ones_r = sb("ones_r", [128, 128], fp32r)
        bout_col = sb("bout_col", [128, 1])
        bup_raw = sb("bup_raw", [128, HT])
        bup_col = sb("bup_col", [128, HT])
        bcon_col = sb("bcon_col", [128, 1])
        bdn_raw = sb("bdn_raw", [128, 1])
        bdn_col = sb("bdn_col", [128, 1])
        ln_eps = sb("ln_eps", [128, 1])
        scratch = sb("scratch", [128, 1])
        warm = sb("warm", [128, 1])
        minus_half = sb("minus_half", [128, 1])
        xs = sb("xs", [128, TILES, C])
        x_res = sb("x_res", [128, TILES, C])
        x_h = sb("x_h", [128, TILES, C], fp32r)
        x_l = sb("x_l", [128, TILES, C], fp32r)
        xT_h = sb("xT_h", [128, N], fp32r)
        xT_l = sb("xT_l", [128, N], fp32r)
        q = sb("q", [128, PAIRS, N])
        k = sb("k", [128, 2, HD])
        k_h = sb("k_h", [128, 2, HD], fp32r)
        k_l = sb("k_l", [128, 2, HD], fp32r)
        k_total = sb("k_total", [128, HD])
        kx = sb("kx", [128, HD])
        ksum_cols = sb("ksum_cols", [128, PAIRS, 32])
        m_h = sb("m_h", [128, PAIRS, C], fp32r)
        m_l = sb("m_l", [128, PAIRS, C], fp32r)
        recip = sb("recip", [128, QT])
        recip_h = sb("recip_h", [128, QT], fp32r)
        recip_parts = sb("recip_parts", [128, N], fp32r)
        qn = sb("qn", [128, 2, CH])
        qn_h = sb("qn_h", [128, 4, CH], fp32r)
        qn_l = sb("qn_l", [128, 4, CH], fp32r)
        attnT = sb("attnT", [128, CH])
        x1 = sb("x1", [128, QUADS, C])
        x1T = sb("x1T", [128, BATCH * N])
        stats = sb("stats", [128, QUADS, 6])
        mean_var = sb("mean_var", [128, QUADS, 2])
        var_eps = sb("var_eps", [128, QUADS])
        rstd = sb("rstd", [128, QUADS])
        y_up = sb("y_up", [128, HID])
        y_bias = sb("y_bias", [1, HID])
        y_dn = sb("y_dn", [128, HID])
        coef_up = sb("coef_up", [128, 2 * HID])
        coef_dn = sb("coef_dn", [128, 2 * HID])
        term = sb("term", [128, 2, HID])
        bias_term = sb("bias_term", [1, 2, HID])
        coef_scratch = nc.dram_tensor("coef_scratch", [2, STAGES, 2 * HID], fp32, kind="Internal").ap()
        stats2 = sb("stats2", [128, QUADS, 6])
        mean_var2 = sb("mean_var2", [128, QUADS, 2])
        var_eps2 = sb("var_eps2", [128, QUADS])
        rstd2 = sb("rstd2", [128, QUADS])

        q_flat = q[:, :, :].rearrange("p a n -> p (a n)")
        wqkv_raw = q_flat[:, 0:3 * HD]
        wout_diag = q_flat[:, 3 * HD:5 * HD].rearrange("p (a h c) -> p a h c", a=PAIRS, h=2)
        wT = q_flat[:, 5 * HD:8 * HD]
        wcon_raw = attnT[:, :].rearrange("p (a c) -> p a c", a=HT)
        term_dve = [attnT[:, :], x1[:, :, :].rearrange("p t c -> p (t c)")]
        hid = [[k[:, 0, :], k[:, 1, :]], [kx[:, :], k_total[:, :]]]
        hid_h = [[k_h[:, 0, :], k_h[:, 1, :]],
                 [x_h[:, :, :].rearrange("p t c -> p (t c)"), x_l[:, :, :].rearrange("p t c -> p (t c)")]]
        hid_l = [[k_l[:, 0, :], k_l[:, 1, :]],
                 [wk_h[:, :], wk_l[:, :]]]

        def tile_of(pairs, i):
            return pairs[i // 2][:, (i % 2) * CH:(i % 2 + 1) * CH]

        def norm_buffers(c):
            if isinstance(c, int) and c == ALLCH - 1:
                return stats, mean_var, var_eps, rstd
            return stats2, mean_var2, var_eps2, rstd2

        yT = y_up[:, :]
        yT_last = y_dn[:, :]
        y_out = [term[:, r, :].rearrange("p (t c) -> p t c", t=QUADS) for r in range(2)]

        pz = pb("pz", [128, 2 * CH])
        pa = pb("pa", [128, 2 * CH])
        pq = pb("pq", [128, 2 * CH])
        pc = pb("pc", [128, CH])
        pd = pb("pd", [128, CH])
        ring = [pz[:, 0:CH], pz[:, CH:2 * CH], pq[:, 0:CH], pq[:, CH:2 * CH]]
        early_ring = [pz[:, 0:CH], pz[:, CH:2 * CH], pa[:, CH:2 * CH]]
        xT_banks = [pz[:, 0:CH], pd[:, :]]

        s_wk = [sem(f"k_weights_half_{n}_loaded") for n in range(2)]
        s_wq = sem("q_weights_loaded")
        s_wv = sem("v_weights_loaded")
        s_wf = sem("wf_loaded")
        s_wout = sem("wout_loaded")
        s_bf = sem("bf_loaded")
        s_bias = sem("biases_loaded")
        s_xs = sem("xs_loaded")
        s_xres = sem("xres_loaded")
        s_wffn = sem("ffn_weights_loaded")
        s_order = sem("coefs_reordered")
        s_cu = sem("coef_up_loaded")
        s_cd = sem("coef_dn_loaded")
        s_zero = sem("zeroed")
        s_wfz = sem("wf_zeroed")
        s_const = sem("constants_made")
        s_row = sem("row_heads_done")
        s_part = sem("part_b_done")
        s_ones = sem("ones_rounded")
        s_bfh = sem("bf_hi")
        s_bfl = sem("bf_lo")
        s_sel = sem("select_rounded")
        s_wT = sem("wT_transposed")
        s_wTa = sem("wT_copied_act")
        s_wTd = sem("wT_copied_dve")
        s_fold = sem("folded")
        s_wh = sem("folded_hi")
        s_wl = sem("folded_lo")
        s_voa = sem("vo_copied_act")
        s_vod = sem("vo_copied_dve")
        s_xTp = sem("xT_transposed")
        s_xTh = sem("xT_hi")
        s_xTl = sem("xT_lo")
        s_xh = sem("x_hi")
        s_xl = sem("x_lo")
        s_kp = sem("k_projected")
        s_kb = sem("k_biased")
        s_k = sem("k_relu")
        s_k0 = sem("k_relu_first_half")
        s_kh = sem("k_hi")
        s_kl = sem("k_lo")
        s_ks = sem("k_summed")
        s_kxt = sem("kx_tile_added")
        s_kx = sem("kx_copied")
        s_qp = sem("q_projected")
        s_q = sem("q_relu")
        s_kcol = sem("ksum_columns")
        s_kcm = sem("ksum_masked")
        s_m = sem("m_done")
        s_mh = sem("m_hi")
        s_ml = sem("m_lo")
        s_np = sem("norm_done")
        s_ne = sem("norm_plus_eps")
        s_r = sem("recip_done")
        s_rh = sem("recip_hi")
        s_rp = sem("recip_parts_done")
        s_rb = sem("recip_spread")
        s_qn = sem("qn_done")
        s_qnh = sem("qn_hi")
        s_qnlp = sem("qn_lo_pool")
        s_qnld = sem("qn_lo_dve")
        s_at = sem("attn_step_added")
        s_atc = sem("attn_copied")
        s_att = sem("attn_transposed")
        s_x1p = sem("x1_pre_done")
        s_st = sem("stats_done")
        s_mv = sem("mean_var_done")
        s_ve = sem("var_eps_done")
        s_rs = sem("rstd_done")
        s_x1 = sem("x1_done")
        s_x1t = sem("x1_transposed")
        s_x1c = sem("x1T_copied")
        s_up = sem("up_butterfly")
        s_ub = sem("up_bias_butterfly")
        s_dn = sem("down_butterfly")
        s_wct = sem("wcon_transposed")
        s_wcc = sem("wconT_copied")
        s_bT = sem("b_up_transposed")
        s_bc = sem("ffn_biases_done")
        s_wdt = sem("wdn_transposed")
        s_wuh = sem("wup_hi")
        s_wul = sem("wup_lo")
        s_wdh = sem("wdn_hi")
        s_wdl = sem("wdn_lo")
        s_fxh = sem("ffn_x_hi")
        s_fxl = sem("ffn_x_lo")
        s_h = sem("hidden_projected")
        s_g = sem("hidden_gelu")
        s_gh = sem("hidden_hi")
        s_glp = sem("hidden_lo_pool")
        s_gld = sem("hidden_lo_dve")
        s_dp = sem("down_projected")
        s_y = sem("yT_done")
        s_yt = sem("y_transposed")
        s_st2 = sem("stats2_done")
        s_mv2 = sem("mean_var2_done")
        s_ve2 = sem("var_eps2_done")
        s_rs2 = sem("rstd2_done")
        s_yo = sem("y_normalised")
        s_out = sem("out_stored")
        s_last = sem("last_out_stored")

        HALF_STEPS = STEPS // 2
        HID_POOL = HT - 1

        def wait_qn_lo(eng, b, a):
            eng.wait_ge(s_qnld if a % 2 else s_qnlp, b * HALF_STEPS + a // 2 + 1)

        FIRST = 1
        SLOTS = FIRST + PAIRS + 1
        PER_SLOT = 3
        EARLY_Q = PER_SLOT * (SLOTS - TILES)

        def spreads(s):
            return [2 * (s - FIRST), 2 * (s - FIRST) + 1] if FIRST <= s < FIRST + PAIRS else []

        def adds(s):
            return [2 * (s - FIRST - 1), 2 * (s - FIRST - 1) + 1] if FIRST < s <= FIRST + PAIRS else []

        def early_q(s):
            return range(PER_SLOT * (s - TILES), PER_SLOT * (s - TILES + 1)) if s >= TILES else []

        COPY_SLOT = FIRST + 5
        TURN_SLOT = TILES
        PART_SLOT = FIRST + 2
        PRE = 3
        PER_TURN = (STAGES - PRE) // (BATCH - 1)

        PE_BIASED = 2
        MAPS_FIRST = 3

        def bias_on_pe(b, s):
            return not isinstance(b, int) and s < PE_BIASED

        def biased_before(b, s):
            if isinstance(b, int):
                return 2 * s
            return 2 * TILES + (b - 1) * 2 * (TILES - PE_BIASED) + 2 * (s - PE_BIASED)

        def q_bank(b, i):
            if isinstance(b, int):
                return ring[2 + i % 2]
            return ring[i % 2] if i < EARLY_Q else ring[i % 4]

        def first_q(s):
            return range(2 * (s - 2), min(2 * (s - 1), STEPS - 3))

        LAST_UP = {1: [0, 1], 2: [2, 3], 3: [4, 5], 4: [6], 5: [7], 8: [8], 9: [9]}
        LAST_DOWN = {6: [0, 1], 7: [2, 3]}

        block = ctx.enter_context(nc.Block())

        @block.sync
        def _(sp):
            def column(dst, src):
                sp.dma_start(dst, src.rearrange("(p o) -> p o", o=1)).then_inc(s_bias, 16)

            def weights(part, done):
                cols = slice(part * HD, (part + 1) * HD)
                sp.dma_start(wqkv_raw[:, cols], W_qkv[:, cols]).then_inc(done, 16)

            for half in range(2):
                cols = slice(HD + half * CH, HD + (half + 1) * CH)
                sp.dma_start(wqkv_raw[:, cols], W_qkv[:, cols]).then_inc(s_wk[half], 16)
            sp.dma_start(xs[:, :, :], xs_view[0, :, :, :]).then_inc(s_xs, 16)
            sp.dma_start(bf_row[:, :], b_f.rearrange("(o n) -> o n", o=1).to_broadcast([128, D])).then_inc(s_bf, 16)
            weights(0, s_wq)
            for h in range(2):
                sp.dma_start(bf_col[h * D:(h + 1) * D, :], b_f.rearrange("(p o) -> p o", o=1)).then_inc(s_bf, 16)
            weights(2, s_wv)
            sp.wait_ge(s_zero, 1)
            wo = W_out.rearrange("(a h e) c -> h e a c", h=2, e=D)
            for h in range(2):
                sp.dma_start(wout_diag[h * D:(h + 1) * D, :, h, :], wo[h, :, :, :]).then_inc(s_wout, 16)
            sp.dma_start(y_up[:, :], W_exp).then_inc(s_wffn, 16)
            sp.dma_start(y_bias[:, :], b_exp.rearrange("(a n) -> a n", a=1)).then_inc(s_wffn, 16)
            sp.dma_start(wcon_raw, W_con.rearrange("(a p) c -> p a c", p=128)).then_inc(s_wffn, 16)

            def reorder(way, st):
                w = [up_weights, down_weights][way][st, :, :, :]
                src = w.rearrange("(hi lo) i j -> lo hi (i j)", lo=1 << st)
                dst = coef_scratch[way, st, :].rearrange("(lo hi f) -> lo hi f", lo=1 << st, f=4)
                sp.dma_start(dst, src).then_inc(s_order, 16)

            def load_up(n):
                if n:
                    sp.wait_ge(s_up, 3 * n)
                    sp.wait_ge(s_ub, 3 * n)
                row = coef_scratch[0, n, :].rearrange("(o n) -> o n", o=1)
                sp.dma_start(coef_up[:, :], row.to_broadcast([128, 2 * HID])).then_inc(s_cu, 16)

            def load_down(n):
                if n:
                    sp.wait_ge(s_dn, 3 * n)
                row = coef_scratch[1, STAGES - 1 - n, :].rearrange("(o n) -> o n", o=1)
                sp.dma_start(coef_dn[:, :], row.to_broadcast([128, 2 * HID])).then_inc(s_cd, 16)

            def reorder_steps(first, end):
                for n in range(first, end):
                    reorder(0, n)
                    reorder(1, STAGES - 1 - n)
                sp.wait_ge(s_order, 32 * end)

            reorder_steps(0, 1)
            load_up(0)
            load_down(0)
            reorder_steps(1, STAGES)
            load_up(1)
            load_down(1)
            column(bout_col[:, :], b_out)
            column(bcon_col[:, :], b_con)
            column(bdn_raw[:, :], down_bias)
            for i in range(HT):
                column(bup_raw[:, i:i + 1], up_bias[i * 128:(i + 1) * 128])
            sp.dma_start(x_res[:, :, :], xs_view[0, :, :, :]).then_inc(s_xres, 16)

            def load_xs(b):
                sp.wait_ge(s_xTp, CHUNKS * b)
                sp.wait_ge(s_xh, b)
                sp.wait_ge(s_xl, b)
                sp.dma_start(xs[:, :, :], xs_view[b, :, :, :]).then_inc(s_xs, 16)

            load_xs(1)
            for n in range(2, PRE + 1):
                load_up(n)
                load_down(n)
            for b in range(BATCH - 1):
                if b + 2 < BATCH:
                    load_xs(b + 2)
                for n in range(PRE + PER_TURN * b + 1, PRE + PER_TURN * (b + 1) + 1):
                    if n < STAGES:
                        load_down(n)
                        load_up(n)
                    if n == PRE + PER_TURN * b + 1:
                        sp.wait_ge(s_x1p, CHUNKS * (b + 1))
                        sp.dma_start(x_res[:, :, :], xs_view[b + 1, :, :, :]).then_inc(s_xres, 16)
            for c in range(ALLCH):
                sp.wait_ge(s_yo, c + 1)
                if 0 < c < ALLCH - 1:
                    sp.wait_ge(s_out, 16 * c)
                sp.dma_start(out_view[c, :, :, :], y_out[c % 2]).then_inc(s_out if c < ALLCH - 1 else s_last, 16)
            sp.wait_ge(s_out, 16 * (ALLCH - 1))
            sp.wait_ge(s_last, 16)

        @block.gpsimd
        def _(pool):
            g = nc.gpsimd
            g.memset(wf_diag[:, :], 0.0).then_inc(s_wfz, 1)
            g.memset(ident[:, :], 0.0).then_inc(s_const, 1)
            pool.wait_ge(s_const, 1)
            g.affine_select(out=ident[:, :], in_=ident[:, :], compare_op=ALU.not_equal, fill=1.0, base=0,
                            pattern=[[-1, 128]], channel_multiplier=1).then_inc(s_const, 1)
            g.memset(ones[:, :], 1.0)
            g.memset(ln_eps[:, :], LN_EPS)
            g.memset(minus_half[:, :], -0.5)
            g.memset(head_mask[:, :, :], 0.0).then_inc(s_const, 1)
            pool.wait_ge(s_const, 3)
            for part in range(2):
                for half in range(2):
                    rows = head_mask[half * D:(half + 1) * D, :, :]
                    g.affine_select(out=rows, in_=rows, compare_op=ALU.not_equal, fill=1.0,
                                    base=-half - 16 * part, pattern=[[-2, PAIRS], [1, 32]],
                                    channel_multiplier=0).then_inc(s_const, 1)
                    pool.wait_ge(s_const, 4 + 2 * part + half)

            def up_part(n, j):
                w = coef_up[:, :].rearrange("p (j i f) -> p i j f", i=2, f=2)
                y = y_up[:, :].rearrange("p (o j f) -> p o j f", o=1, f=2)
                if j < 2:
                    if j == 0:
                        pool.wait_ge(s_cu, 16 * (n + 1))
                    g.tensor_tensor(term[:, j, :].rearrange("p (i j) -> p i j", i=2), w[:, :, :, j],
                                    y[:, :, :, j].to_broadcast([128, 2, HID // 2]), ALU.mult).then_inc(s_up, 1)
                else:
                    pool.wait_ge(s_up, 3 * n + 2)
                    g.tensor_tensor(y_up[:, :], term[:, 0, :], term[:, 1, :], ALU.add).then_inc(s_up, 1)
                    pool.wait_ge(s_up, 3 * n + 3)

            def up_step(n):
                for j in range(3):
                    up_part(n, j)

            def down_step(n):
                w = coef_dn[:, :].rearrange("p (j i f) -> p i j f", i=2, f=2)
                y = y_dn[:, :].rearrange("p (i j o) -> p i j o", i=2, o=1)
                pool.wait_ge(s_cd, 16 * (n + 1))
                pool.wait_ge(s_dn, 3 * n)
                for i in range(2):
                    g.tensor_tensor(term[:, i, :].rearrange("p (j f) -> p j f", f=2), w[:, i, :, :],
                                    y[:, i, :, :].to_broadcast([128, HID // 2, 2]), ALU.mult).then_inc(s_dn, 1)
                pool.wait_ge(s_dn, 3 * n + 2)
                g.tensor_tensor(y_dn[:, :], term[:, 0, :], term[:, 1, :], ALU.add).then_inc(s_dn, 1)
                pool.wait_ge(s_dn, 3 * n + 3)

            def x_lo(b):
                pool.wait_ge(s_xh, b + 1)
                g.tensor_tensor(x_l[:, :, :], xs[:, :, :], x_h[:, :, :].bitcast(fp32), ALU.subtract).then_inc(s_xl, 1)

            def k_sum_start(b):
                pool.wait_ge(s_k, b * TILES + 1)
                pool.wait_ge(s_kcol, b)
                g.tensor_tensor(k_total[:, :], k[:, 0, :], ones[:, :].to_broadcast([128, HD]), ALU.mult).then_inc(s_ks, 1)

            def k_sum(b, s):
                pool.wait_ge(s_k, b * TILES + s + 1)
                pool.wait_ge(s_ks, b * TILES + s)
                g.tensor_tensor(k_total[:, :], k_total[:, :], k[:, s % 2, :], ALU.add).then_inc(s_ks, 1)

            def qn_lo(b, a):
                if a % 2:
                    return
                pool.wait_ge(s_qnh, b * STEPS + a + 1)
                g.tensor_tensor(qn_l[:, a % 4, :], qn[:, a % 2, :], qn_h[:, a % 4, :].bitcast(fp32),
                                ALU.subtract).then_inc(s_qnlp, 1)

            def ln_rstd(c, ve, rs, mv, s_in, s_mid, s_done):
                pool.wait_ge(s_in, QUADS * (c + 1))
                g.tensor_tensor(ve, mv, ln_eps[:, :].to_broadcast([128, QUADS]), ALU.add).then_inc(s_mid, 1)
                pool.wait_ge(s_mid, c + 1)
                g.tensor_tensor(rs, ve, minus_half[:, :].to_broadcast([128, QUADS]), ALU.pow).then_inc(s_done, 1)

            def rstd_1(c):
                ln_rstd(c, var_eps[:, :], rstd[:, :], mean_var[:, :, 1], s_mv, s_ve, s_rs)

            def rstd_2(c):
                _, mv, ve, rs = norm_buffers(c)
                ln_rstd(c, ve[:, :], rs[:, :], mv[:, :, 1], s_mv2, s_ve2, s_rs2)

            def hidden_lo(c, r, tiles):
                for i in tiles:
                    pool.wait_ge(s_gh, 2 * c + i // 2 + 1)
                    g.tensor_tensor(tile_of(hid_l[r], i), tile_of(hid[r], i), tile_of(hid_h[r], i).bitcast(fp32),
                                    ALU.subtract).then_inc(s_glp, 1)

            pool.wait_ge(s_wffn, 48)
            x_lo(0)
            up_step(0)
            parts = [(n, j) for n in range(1, PRE) for j in range(3)]
            for s in range(1, TILES):
                k_sum(0, s)
                if s >= 2:
                    up_part(*parts[s - 2])
            with pool.Fori(0, BATCH - 1) as b:
                x_lo(b + 1)
                n = PRE + PER_TURN * b
                for s in range(SLOTS):
                    for a in spreads(s):
                        qn_lo(b, a)
                    if s == 0:
                        k_sum_start(b + 1)
                    if 0 < s < TILES:
                        k_sum(b + 1, s)
                    if s == TURN_SLOT:
                        down_step(n)
                rstd_1(CHUNKS * b)
                up_step(n)
                rstd_1(CHUNKS * b + 1)
                for m in range(1, PER_TURN):
                    down_step(n + m)
                    up_step(n + m)
            pool.wait_ge(s_wuh, 1)
            g.tensor_tensor(wup_l[:, :], y_up[:, :], wup_h[:, :].bitcast(fp32), ALU.subtract).then_inc(s_wul, 1)
            for s in range(FIRST, SLOTS):
                for a in spreads(s):
                    qn_lo(BATCH - 1, a)
                if s == TURN_SLOT:
                    rstd_1(ALLCH - 2)
                if s == 2:
                    hidden_lo(0, 0, [0, 1])
                if s == 3:
                    hidden_lo(0, 0, [2])
                if s == 4:
                    hidden_lo(1, 1, [0])
                if s == 5:
                    hidden_lo(1, 1, [1])
                if s == 6:
                    hidden_lo(1, 1, [2])
            hidden_lo(2, 0, [0])
            rstd_1(ALLCH - 1)
            hidden_lo(2, 0, [1])
            rstd_2(0)
            hidden_lo(2, 0, [2])

            def turn(c, r):
                hidden_lo(c + 1, 1 - r, [0])
                rstd_2(c - 1)
                hidden_lo(c + 1, 1 - r, range(1, HID_POOL))

            with pool.Fori(1, ALLCH // 2 - 1) as i:
                for r in range(2):
                    turn(2 * i + r, r)
            hidden_lo(ALLCH - 1, 1, [0])
            rstd_2(ALLCH - 3)
            hidden_lo(ALLCH - 1, 1, [2])
            rstd_2(ALLCH - 2)
            rstd_2(ALLCH - 1)

        @block.tensor
        def _(pe):
            t = nc.tensor

            def product(dst, pairs, start, stop):
                for n, (lhsT, rhs) in enumerate(pairs):
                    last = t.matmul(dst, lhsT, rhs, start=start and n == 0, stop=stop and n == len(pairs) - 1)
                return last

            def split(dst, lhs, rhs, start=True, stop=True):
                (lh, ll), (rh, rl) = lhs, rhs
                return product(dst, [(lh, rh), (lh, rl), (ll, rh)], start, stop)

            def transpose_tiles(dst, src):
                for i in range(QUADS):
                    last = t.transpose(dst[:, i * 128:(i + 1) * 128], src(i), ident[:, :])
                return last

            def transpose_weights(grp, dst):
                pe.wait_ge([s_wq, s_wq, *s_wk, s_wv, s_wv][grp], 16)
                transpose_tiles(dst, lambda i: wqkv_raw[:, (grp * 4 + i) * 128:(grp * 4 + i + 1) * 128])\
                    .then_inc(s_wT, 1)

            def fold_wf(grp, dst):
                for i in range(4):
                    col = (grp * 4 + i) * 128
                    last = t.matmul(dst[:, i * 128:(i + 1) * 128], wT[:, col:col + 128], wf_diag[:, :],
                                    start=True, stop=True)
                last.then_inc(s_fold, 1)

            def transpose_x(n, banks):
                pe.wait_ge(s_xs, 16 * (n + 1))
                for half in range(2):
                    transpose_tiles(banks[half], lambda i: xs[:, 4 * half + i, :]).then_inc(s_xTp, 1)

            def project_k(b, s):
                if s % QUADS == 0:
                    pe.wait_ge(s_xTh, CHUNKS * b + s // QUADS + 1)
                    pe.wait_ge(s_xTl, CHUNKS * b + s // QUADS + 1)
                tok = slice(s * 128, (s + 1) * 128)
                for half in range(2):
                    if s and bias_on_pe(b, s - 1) and half == 0:
                        pe.wait_ge(s_k0, (b - 1) * PE_BIASED + s)
                    elif s and bias_on_pe(b, s - 1):
                        pe.wait_ge(s_k, b * TILES + s)
                    elif s:
                        pe.wait_ge(s_kb, biased_before(b, s - 1) + half + 1)
                    cols = slice(half * CH, (half + 1) * CH)
                    operands = (xT_h[:, tok], xT_l[:, tok]), (wk_h[:, cols], wk_l[:, cols])
                    if bias_on_pe(b, s):
                        split(pz[:, cols], *operands, stop=False)
                        t.matmul(pz[:, cols], ones_r[:, :], bf_rows[:, :], start=False, stop=True).then_inc(s_kp, 1)
                    else:
                        split(pz[:, cols], *operands).then_inc(s_kp, 1)

            def add_kx(b, s):
                pe.wait_ge(s_kh, b * TILES + s + 1)
                pe.wait_ge(s_kl, b * TILES + s + 1)
                if s == 0:
                    pe.wait_ge(s_xh, b + 1)
                    pe.wait_ge(s_xl, b + 1)
                    if not isinstance(b, int):
                        pe.wait_ge(s_ml, b)
                for half in range(2):
                    cols = slice(half * CH, (half + 1) * CH)
                    last = split(pa[:, cols], (x_h[:, s, :], x_l[:, s, :]),
                                 (k_h[:, s % 2, cols], k_l[:, s % 2, cols]), s == 0, s == TILES - 1)
                last.then_inc(s_kxt, 1)

            def project_q(b, i):
                p, c = i // CHUNKS, i % CHUNKS
                if isinstance(b, int):
                    if i == 0:
                        pe.wait_ge(s_voa, 2)
                        pe.wait_ge(s_vod, 2)
                    elif i >= 2:
                        pe.wait_ge(s_q, i - 1)
                elif i == 0:
                    pe.wait_ge(s_kb, biased_before(b, TILES))
                elif i == EARLY_Q:
                    pe.wait_ge(s_qn, b * STEPS)
                elif 2 <= i < EARLY_Q:
                    pe.wait_ge(s_q, b * STEPS + i - 1)
                elif i >= EARLY_Q + 2:
                    pe.wait_ge(s_q, b * STEPS + i - 3)
                cols = slice(c * CH, (c + 1) * CH)
                split(q_bank(b, i), (wq_h[:, p, :], wq_l[:, p, :]), (xT_h[:, cols], xT_l[:, cols])).then_inc(s_qp, 1)

            def ksum(b):
                pe.wait_ge(s_kx, b + 1)
                pe.wait_ge(s_ks, TILES * (b + 1))
                for p in range(PAIRS):
                    last = t.matmul(pa[:, p:p + 1], k_total[:, p * 128:(p + 1) * 128], ones[:, :],
                                    start=True, stop=True)
                last.then_inc(s_kcol, 1)

            def add_norm(b, p):
                if p == 0:
                    pe.wait_ge(s_kcm, b + 1)
                    if not isinstance(b, int):
                        pe.wait_ge(s_atc, CHUNKS * b)
                pe.wait_ge(s_q, b * STEPS + CHUNKS * (p + 1))
                for j in range(4):
                    last = t.matmul(pc[32 * j:32 * j + 32, 0:QT], ksum_cols[:, p, :],
                                    q[:, p, j * QT:(j + 1) * QT], start=p == 0, stop=p == PAIRS - 1)
                if p == PAIRS - 1:
                    last.then_inc(s_np, 1)

            def head_maps(b, pairs):
                for p in pairs:
                    for h in range(2):
                        last = t.matmul(pa[h * D:(h + 1) * D, p * 128:(p + 1) * 128],
                                        kx[:, (2 * p + h) * D:(2 * p + h + 1) * D], vo[:, 2 * p + h, :],
                                        start=True, stop=True)
                if PAIRS - 1 in pairs:
                    last.then_inc(s_m, 1)

            def spread(b, a):
                c, p = a // PAIRS, a % PAIRS
                if a == 0:
                    pe.wait_ge(s_sel, 1)
                if p == 0:
                    pe.wait_ge(s_rp, 4 * b + 2 * c + 2)
                if a >= 2:
                    pe.wait_ge(s_qn, b * STEPS + a - 1)
                sel = select[:, 2 * p:2 * p + 2, :].rearrange("p h m -> p (h m)")
                t.matmul(pq[:, (a % 2) * CH:(a % 2 + 1) * CH], sel, recip_parts[:, c * CH:(c + 1) * CH],
                         start=True, stop=True).then_inc(s_rb, 1)

            def add_attn(b, a):
                c, p = a // PAIRS, a % PAIRS
                if a == 0:
                    pe.wait_ge(s_ml, b + 1)
                if a == PAIRS:
                    pe.wait_ge(s_atc, CHUNKS * b + 1)
                pe.wait_ge(s_qnh, b * STEPS + a + 1)
                wait_qn_lo(pe, b, a)
                split(pc[:, :], (m_h[:, p, :], m_l[:, p, :]), (qn_h[:, a % 4, :], qn_l[:, a % 4, :]),
                      p == 0, p == PAIRS - 1).then_inc(s_at, 1)

            def transpose_attn(c, dst):
                pe.wait_ge(s_atc, c + 1)
                transpose_tiles(dst, lambda i: attnT[:, i * 128:(i + 1) * 128]).then_inc(s_att, 1)

            def transpose_x1(c, dst):
                pe.wait_ge(s_x1, c + 1)
                transpose_tiles(dst, lambda i: x1[:, i, :]).then_inc(s_x1t, 1)

            pe.wait_ge(s_const, 2)
            transpose_weights(2, pz[:, 0:CH])
            transpose_weights(3, pz[:, CH:])
            transpose_x(0, [pa[:, 0:CH], pa[:, CH:]])
            pe.wait_ge(s_wf, 32)
            pe.wait_ge(s_wTa, 1)
            fold_wf(2, pc[:, :])
            pe.wait_ge(s_wTd, 1)
            fold_wf(3, pd[:, :])
            transpose_weights(0, pq[:, 0:CH])
            transpose_weights(1, pq[:, CH:])
            pe.wait_ge(s_wh, 2)
            pe.wait_ge(s_wl, 2)
            project_k(0, 0)
            pe.wait_ge(s_wTa, 2)
            fold_wf(0, pc[:, :])
            pe.wait_ge(s_wTd, 2)
            fold_wf(1, pd[:, :])
            transpose_weights(4, pq[:, 0:CH])
            transpose_weights(5, pq[:, CH:])
            project_k(0, 1)
            pe.wait_ge(s_wTa, 3)
            pe.wait_ge(s_wTd, 3)
            pe.wait_ge(s_wout, 32)
            for n, dst in enumerate([pq[:, 0:CH], pq[:, CH:], pc[:, :], pd[:, :]]):
                if n == 2:
                    pe.wait_ge(s_wh, 4)
                    pe.wait_ge(s_wl, 4)
                for i in range(2):
                    pair = 2 * n + i
                    col = 2 * HD + pair * 128
                    last = t.matmul(dst[:, i * 256:(i + 1) * 256], wT[:, col:col + 128],
                                    wout_diag[:, pair, :, :].rearrange("p h c -> p (h c)"), start=True, stop=True)
                last.then_inc(s_fold, 1)
            for s in range(2, TILES + 2):
                if s < TILES:
                    project_k(0, s)
                for i in first_q(s)[:1]:
                    project_q(0, i)
                add_kx(0, s - 2)
                if s == 2:
                    pe.wait_ge(s_wffn, 48)
                    transpose_tiles(pd, lambda i: wcon_raw[:, i, :]).then_inc(s_wct, 1)
                for i in first_q(s)[1:]:
                    project_q(0, i)
            project_q(0, STEPS - 3)
            project_q(0, STEPS - 2)
            ksum(0)
            project_q(0, STEPS - 1)
            for p in range(PAIRS - 1):
                add_norm(0, p)
            pe.wait_ge(s_wcc, 1)
            pe.wait_ge(s_ones, 1)

            with t.Fori(0, BATCH - 1) as b:
                pe.wait_ge(s_q, b * STEPS + STEPS - 2)
                transpose_x(b + 1, xT_banks)
                add_norm(b, PAIRS - 1)
                head_maps(b, range(MAPS_FIRST))
                pe.wait_ge(s_bfl, 1)
                project_k(b + 1, 0)
                head_maps(b, range(MAPS_FIRST, PAIRS))
                for s in range(SLOTS):
                    if s == FIRST:
                        for a in spreads(s):
                            spread(b, a)
                    if s == FIRST + 1:
                        spread(b, spreads(s)[0])
                    if 0 < s < TILES:
                        project_k(b + 1, s)
                    if s == TURN_SLOT:
                        transpose_attn(CHUNKS * b, pd)
                    if s > FIRST + 1:
                        for a in spreads(s)[:1]:
                            spread(b, a)
                    if s > FIRST:
                        add_kx(b + 1, s - 2)
                        for a in spreads(s)[1:]:
                            spread(b, a)
                    if s <= TILES:
                        for a in adds(s):
                            add_attn(b, a)
                    for i in early_q(s)[:1]:
                        project_q(b + 1, i)
                    if s > TILES:
                        for a in adds(s)[:1]:
                            add_attn(b, a)
                    for i in early_q(s)[1:2]:
                        project_q(b + 1, i)
                    if s > TILES:
                        for a in adds(s)[1:]:
                            add_attn(b, a)
                    for i in early_q(s)[2:]:
                        project_q(b + 1, i)
                for i in range(EARLY_Q, STEPS):
                    project_q(b + 1, i)
                    n = i - EARLY_Q
                    if n == 0:
                        transpose_x1(CHUNKS * b, pd)
                    if n == 1:
                        ksum(b + 1)
                    if n == 2:
                        pe.wait_ge(s_x1c, CHUNKS * b + 1)
                        transpose_attn(CHUNKS * b + 1, pd)
                    if n >= 3:
                        add_norm(b + 1, n - 3)
                    if i == STEPS - 2:
                        transpose_x1(CHUNKS * b + 1, pd)
                pe.wait_ge(s_x1c, CHUNKS * (b + 1))
            last_b = BATCH - 1
            add_norm(last_b, PAIRS - 1)
            head_maps(last_b, range(PAIRS))
            pe.wait_ge(s_ub, 3 * STAGES)
            for i in range(HT):
                last = t.matmul(pz[:, i:i + 1], y_bias[:, i * 128:(i + 1) * 128], ones[0:1, :],
                                start=True, stop=True)
            last.then_inc(s_bT, 1)
            pe.wait_ge(s_dn, 3 * STAGES)
            transpose_tiles(pd, lambda i: y_dn[:, i * 128:(i + 1) * 128]).then_inc(s_wdt, 1)

            def up_tile(c, r, i, bank):
                if i == 0:
                    pe.wait_ge(s_fxh, c + 1)
                    pe.wait_ge(s_fxl, c + 1)
                cols = slice(i * 128, (i + 1) * 128)
                tok = slice(r * CH, (r + 1) * CH)
                split(bank, (wup_h[:, cols], wup_l[:, cols]), (xT_h[:, tok], xT_l[:, tok])).then_inc(s_h, 1)

            def up(c, r):
                for i in range(HT):
                    pe.wait_ge(s_g, HT * (c - 1) + i + 1)
                    up_tile(c, r, i, ring[i])

            def early_up(u):
                n = len(early_ring)
                if u == 0:
                    pe.wait_ge(s_bc, 2)
                    pe.wait_ge(s_wuh, 1)
                    pe.wait_ge(s_wul, 1)
                if u == 2:
                    pe.wait_ge(s_mh, BATCH)
                    pe.wait_ge(s_ml, BATCH)
                if u >= n:
                    pe.wait_ge(s_g, u - n + 1)
                up_tile(u // HT, u // HT % 2, u % HT, early_ring[u % n])

            def down_tile(c, r, i):
                last_one = isinstance(c, int) and c == ALLCH - 1
                bank = pa[:, CH:] if last_one else pa[:, 0:CH]
                if i == 0 and (not isinstance(c, int) or c) and not last_one:
                    pe.wait_ge(s_y, c)
                if last_one and i % 2:
                    pe.wait_ge(s_gld, c + i // 2 + 1)
                elif last_one:
                    pe.wait_ge(s_glp, HID_POOL * c + i // 2 + 1)
                elif i < HID_POOL:
                    pe.wait_ge(s_glp, HID_POOL * c + i + 1)
                else:
                    pe.wait_ge(s_gld, c + 1)
                last = split(bank, (wdn_h[:, i, :], wdn_l[:, i, :]),
                             (tile_of(hid_h[r], i), tile_of(hid_l[r], i)), i == 0, i == HT - 1)
                if i == HT - 1:
                    last.then_inc(s_dp, 1)

            def down(c, r):
                for i in range(HT):
                    down_tile(c, r, i)

            def transpose_y(c, bank=pd, src=yT):
                pe.wait_ge(s_y, c + 1)
                if bank is pd and (not isinstance(c, int) or c):
                    pe.wait_ge(s_yo, c)
                transpose_tiles(bank, lambda i: src[:, i * 128:(i + 1) * 128]).then_inc(s_yt, 1)

            for s in range(FIRST, SLOTS):
                ups = LAST_UP.get(s, [])
                for a in spreads(s):
                    spread(last_b, a)
                for u in ups[:1]:
                    early_up(u)
                for i in LAST_DOWN.get(s, [])[:1]:
                    down_tile(0, 0, i)
                if s == COPY_SLOT:
                    pe.wait_ge(s_wdh, 1)
                    pe.wait_ge(s_wdl, 1)
                    transpose_attn(ALLCH - 2, pd)
                for a in adds(s)[:1]:
                    add_attn(last_b, a)
                for u in ups[1:]:
                    early_up(u)
                for i in LAST_DOWN.get(s, [])[1:]:
                    down_tile(0, 0, i)
                for a in adds(s)[1:]:
                    add_attn(last_b, a)
            early_up(10)
            pe.wait_ge(s_qn, BATCH * STEPS)
            transpose_attn(ALLCH - 1, pq[:, 0:CH])
            transpose_x1(ALLCH - 2, pc)
            early_up(11)
            down_tile(1, 1, 0)
            down_tile(1, 1, 1)
            transpose_y(0)
            down_tile(1, 1, 2)
            down_tile(1, 1, 3)
            pe.wait_ge(s_x1c, ALLCH - 1)
            transpose_x1(ALLCH - 1, pc)
            pe.wait_ge(s_g, HT * 3 - 2)
            with t.Fori(1, ALLCH // 2 - 1) as i:
                for r in range(2):
                    c = 2 * i + r
                    up(c + 1, 1 - r)
                    transpose_y(c - 1)
                    down(c, r)
            up(ALLCH - 1, 1)
            transpose_y(ALLCH - 3)
            down(ALLCH - 2, 0)
            for i in range(HT):
                down_tile(ALLCH - 1, 1, i)
                if i == 1:
                    transpose_y(ALLCH - 2, pc)
            transpose_y(ALLCH - 1, pz, yT_last)

        @block.scalar
        def _(act):
            a_ = nc.scalar
            act.wait_ge(s_wfz, 1)
            for h in range(2):
                act.dma_start(wf_diag[h * D:(h + 1) * D, h * D:(h + 1) * D], W_f).then_inc(s_wf, 16)
            a_.activation(warm[0:D, :], wf_diag[0:D, D:D + 1], ACT.Copy)

            def hi(dst, src, done):
                a_.activation(dst, src, ACT.Copy).then_inc(done, 1)

            def wT_copy(n, grp, bank):
                act.wait_ge(s_wT, n)
                a_.activation(wT[:, grp * CH:(grp + 1) * CH], bank, ACT.Copy).then_inc(s_wTa, 1)

            def xT_hi(b, c, bank):
                act.wait_ge(s_xTp, CHUNKS * b + c + 1)
                hi(xT_h[:, c * CH:(c + 1) * CH], bank, s_xTh)

            def x_hi(b):
                hi(x_h[:, :, :], xs[:, :, :], s_xh)

            def k_relu(b, s):
                kt = k[:, s % 2, :]
                if bias_on_pe(b, s):
                    act.wait_ge(s_ks, b * TILES + max(0, s - 1))
                    act.wait_ge(s_kl, b * TILES + max(0, s - 1))
                    for half, done in enumerate([s_k0, s_k]):
                        cols = slice(half * CH, (half + 1) * CH)
                        act.wait_ge(s_kp, b * 2 * TILES + 2 * s + half + 1)
                        a_.activation(kt[:, cols], pz[:, cols], ACT.Relu).then_inc(done, 1)
                else:
                    act.wait_ge(s_kb, biased_before(b, s) + 2)
                    a_.activation(kt, kt, ACT.Relu).then_inc(s_k, 1)

            def k_sum_start(b):
                act.wait_ge(s_k, b * TILES + 1)
                a_.activation(k_total[:, :], k[:, 0, :], ACT.Copy).then_inc(s_ks, 1)

            def k_hi(b, s):
                if s >= 2:
                    act.wait_ge(s_kxt, b * TILES + s - 1)
                act.wait_ge(s_k, b * TILES + s + 1)
                hi(k_h[:, s % 2, :], k[:, s % 2, :], s_kh)

            def kx_copy(b):
                act.wait_ge(s_kxt, TILES * (b + 1))
                a_.activation(kx[:, :], pa[:, :], ACT.Copy).then_inc(s_kx, 1)

            def q_relu(b, i):
                p, c = i // CHUNKS, i % CHUNKS
                act.wait_ge(s_qp, b * STEPS + i + 1)
                if not isinstance(b, int):
                    act.wait_ge(s_qn, (b - 1) * STEPS + c * PAIRS + p + 1)
                a_.activation(q[:, p, c * CH:(c + 1) * CH], q_bank(b, i), ACT.Relu, bias=bf_col[:, :])\
                    .then_inc(s_q, 1)

            def qn_hi(b, a):
                act.wait_ge(s_qn, b * STEPS + a + 1)
                if a >= 4:
                    act.wait_ge(s_at, b * STEPS + a - 3)
                hi(qn_h[:, a % 4, :], qn[:, a % 2, :], s_qnh)

            def attn_copy(c):
                act.wait_ge(s_at, PAIRS * (c + 1))
                a_.activation(attnT[:, :], pc[:, :], ACT.Identity, bias=bout_col[:, :]).then_inc(s_atc, 1)

            def tokens(c):
                return x1T[:, c * CH:(c + 1) * CH] if isinstance(c, int) else x1T[:, bass.ds(c * CH, CH)]

            def x1T_copy(c, bank):
                act.wait_ge(s_x1t, c + 1)
                a_.activation(tokens(c), bank, ACT.Copy).then_inc(s_x1c, 1)

            def m_hi(b):
                act.wait_ge(s_m, b + 1)
                hi(m_h[:, :, :].rearrange("p a c -> p (a c)"), pa[:, :], s_mh)

            def norm_eps(b):
                act.wait_ge(s_np, b + 1)
                a_.activation(recip[:, :], pc[:, 0:QT], ACT.Copy, bias=NORM_EPS).then_inc(s_ne, 1)

            def recip_hi(b):
                act.wait_ge(s_r, b + 1)
                hi(recip_h[:, :], recip[:, :], s_rh)

            wT_copy(1, 2, pz[:, 0:CH])
            xT_hi(0, 0, pa[:, 0:CH])
            xT_hi(0, 1, pa[:, CH:])
            for half, bank in enumerate([pc, pd]):
                act.wait_ge(s_fold, half + 1)
                hi(wk_h[:, half * CH:(half + 1) * CH], bank[:, :], s_wh)
            wT_copy(3, 0, pq[:, 0:CH])
            x_hi(0)
            act.wait_ge(s_bf, 48)
            k_relu(0, 0)
            wq_flat = wq_h[:, :, :].rearrange("p a m -> p (a m)")
            for half, bank in enumerate([pc, pd]):
                act.wait_ge(s_fold, half + 3)
                hi(wq_flat[:, half * CH:(half + 1) * CH], bank[:, :], s_wh)
            wT_copy(5, 4, pq[:, 0:CH])
            k_hi(0, 0)
            k_sum_start(0)
            k_relu(0, 1)
            vo_flat = vo[:, :, :].rearrange("p a m -> p (a m)")
            for n, bank in [(0, pq[:, 0:CH]), (2, pc[:, :])]:
                act.wait_ge(s_fold, 5 + n)
                a_.activation(vo_flat[:, n * CH:(n + 1) * CH], bank, ACT.Copy).then_inc(s_voa, 1)
            k_hi(0, 1)
            act.wait_ge(s_fold, 8)
            for s in range(2, TILES + 2):
                if s < TILES:
                    k_relu(0, s)
                for i in first_q(s)[:1]:
                    q_relu(0, i)
                if s < TILES:
                    k_hi(0, s)
                if s == 2:
                    act.wait_ge(s_wct, 1)
                    a_.activation(y_dn[:, :], pd[:, :], ACT.Copy).then_inc(s_wcc, 1)
                for i in first_q(s)[1:]:
                    q_relu(0, i)
            kx_copy(0)
            for i in range(STEPS - 3, STEPS):
                q_relu(0, i)
            act.wait_ge(s_const, 3)
            hi(ones_r[:, :], ones[:, :].to_broadcast([128, 128]), s_ones)
            hi(bf_h[:, :], bf_row[:, :], s_bfh)
            a_.activation(bf_rows[:, :].rearrange("p (a c) -> p a c", c=128),
                          ident[:, :].rearrange("p (o c) -> p o c", o=1).to_broadcast([128, CH // 128, 128]),
                          ACT.Copy, scale=0.0).then_inc(s_bfh, 1)
            act.wait_ge(s_bfh, 2)
            hi(bf_rows[0:1, :].rearrange("p (h d) -> p h d", d=D),
               bf_row[0:1, :].rearrange("p (o d) -> p o d", o=1).to_broadcast([1, CH // D, D]), s_bfh)
            act.wait_ge(s_row, 2)
            hi(select[:, :, :], row_head[:, :].rearrange("p (h o) -> p h o", o=1)
               .to_broadcast([128, 16, D]), s_sel)
            a_.activation(part_b[:, :], row_part[:, :], ACT.Copy, scale=-1.0).then_inc(s_part, 1)
            a_.activation(recip_parts[:, :].rearrange("p (a c) -> p a c", c=128),
                          ident[:, :].rearrange("p (o c) -> p o c", o=1).to_broadcast([128, N // 128, 128]),
                          ACT.Copy, scale=0.0).then_inc(s_part, 1)
            act.wait_ge(s_bias, 16 * (3 + HT))
            with a_.Fori(0, BATCH - 1) as b:
                xT_hi(b + 1, 0, xT_banks[0])
                norm_eps(b)
                xT_hi(b + 1, 1, xT_banks[1])
                x_hi(b + 1)
                recip_hi(b)
                for s in range(SLOTS):
                    if s == COPY_SLOT:
                        attn_copy(CHUNKS * b)
                    if s < TILES:
                        k_relu(b + 1, s)
                    if s == 0:
                        m_hi(b)
                    for a in spreads(s)[:1]:
                        qn_hi(b, a)
                    if s < TILES:
                        k_hi(b + 1, s)
                    for i in early_q(s)[:1]:
                        q_relu(b + 1, i)
                    for a in spreads(s)[1:]:
                        qn_hi(b, a)
                    for i in early_q(s)[1:]:
                        q_relu(b + 1, i)
                kx_copy(b + 1)
                attn_copy(CHUNKS * b + 1)
                for i in range(EARLY_Q, STEPS):
                    q_relu(b + 1, i)
                    if i == EARLY_Q:
                        x1T_copy(CHUNKS * b, pd[:, :])
                    if i == STEPS - 2:
                        x1T_copy(CHUNKS * b + 1, pd[:, :])
            last_b = BATCH - 1

            def gelu_tile(c, r, i, bank):
                act.wait_ge(s_h, HT * c + i + 1)
                if i == 0 and (not isinstance(c, int) or c >= 2):
                    act.wait_ge(s_glp, HID_POOL * (c - 1))
                    act.wait_ge(s_gld, c - 1)
                a_.activation(tile_of(hid[r], i), bank, ACT.Gelu, bias=bup_col[:, i:i + 1]).then_inc(s_g, 1)
                if i % 2:
                    act.wait_ge(s_g, HT * c + i + 1)
                    if i == 1 and (not isinstance(c, int) or c >= 2):
                        act.wait_ge(s_dp, c - 1)
                    hi(hid_h[r][i // 2], hid[r][i // 2], s_gh)

            def gelu(c, r):
                for i in range(HT):
                    gelu_tile(c, r, i, ring[i])

            def early_gelu(u):
                gelu_tile(u // HT, u // HT % 2, u % HT, early_ring[u % len(early_ring)])

            norm_eps(last_b)
            act.wait_ge(s_up, 3 * STAGES)
            hi(wup_h[:, :], y_up[:, :], s_wuh)
            recip_hi(last_b)
            m_hi(last_b)
            act.wait_ge(s_wdt, 1)
            hi(wdn_h[:, :, :].rearrange("p a c -> p (a c)"), pd[:, :], s_wdh)
            a_.activation(warm[0:D, :], wf_diag[0:D, D:D + 1], ACT.Gelu)
            act.wait_ge(s_bc, 2)
            for s in range(FIRST, SLOTS):
                for a in spreads(s):
                    qn_hi(last_b, a)
                if s == COPY_SLOT - 1:
                    attn_copy(ALLCH - 2)
                for u in LAST_UP.get(s, []):
                    early_gelu(u)
            attn_copy(ALLCH - 1)
            early_gelu(10)
            x1T_copy(ALLCH - 2, pc[:, :])
            early_gelu(11)
            x1T_copy(ALLCH - 1, pc[:, :])
            with a_.Fori(1, ALLCH // 2 - 1) as i:
                for r in range(2):
                    gelu(2 * i + r + 1, 1 - r)
            gelu(ALLCH - 1, 1)

        @block.vector
        def _(dve):
            v = nc.vector

            def lo(dst, src, high, done):
                v.tensor_tensor(dst, src, high.bitcast(fp32), ALU.subtract).then_inc(done, 1)

            def wT_copy(n, grp, bank):
                dve.wait_ge(s_wT, n)
                v.tensor_copy(wT[:, grp * CH:(grp + 1) * CH], bank).then_inc(s_wTd, 1)

            def xT_lo(b, c, bank):
                dve.wait_ge(s_xTh, CHUNKS * b + c + 1)
                cols = slice(c * CH, (c + 1) * CH)
                lo(xT_l[:, cols], bank, xT_h[:, cols], s_xTl)

            def k_bias(b, s):
                if bias_on_pe(b, s):
                    return
                for half in range(2):
                    dve.wait_ge(s_kp, b * 2 * TILES + 2 * s + half + 1)
                    if half == 0 and s >= 2:
                        dve.wait_ge(s_ks, b * TILES + s - 1)
                        dve.wait_ge(s_kl, b * TILES + s - 1)
                    if half == 0 and s < 2 and not isinstance(b, int):
                        dve.wait_ge(s_ks, b * TILES)
                        dve.wait_ge(s_kl, b * TILES)
                    cols = slice(half * CH, (half + 1) * CH)
                    v.tensor_tensor(k[:, s % 2, cols].rearrange("p (h d) -> p h d", d=D),
                                    pz[:, cols].rearrange("p (h d) -> p h d", d=D),
                                    bf_row[:, :].rearrange("p (o d) -> p o d", o=1).to_broadcast([128, CH // D, D]),
                                    ALU.add).then_inc(s_kb, 1)

            def k_lo(b, s):
                dve.wait_ge(s_kh, b * TILES + s + 1)
                lo(k_l[:, s % 2, :], k[:, s % 2, :], k_h[:, s % 2, :], s_kl)

            def normalise_q(b, a):
                c, p = a // PAIRS, a % PAIRS
                dve.wait_ge(s_rb, b * STEPS + a + 1)
                if a >= 2:
                    wait_qn_lo(dve, b, a - 2)
                v.tensor_tensor(qn[:, a % 2, :], q[:, p, c * CH:(c + 1) * CH], pq[:, (a % 2) * CH:(a % 2 + 1) * CH],
                                ALU.mult).then_inc(s_qn, 1)

            def qn_lo(b, a):
                dve.wait_ge(s_qnh, b * STEPS + a + 1)
                lo(qn_l[:, a % 4, :], qn[:, a % 2, :], qn_h[:, a % 4, :], s_qnld)

            def add_x(b, c, bank):
                n = CHUNKS * b + c
                dve.wait_ge(s_att, n + 1)
                dve.wait_ge(s_xres, 16 * (b + 1))
                if c:
                    dve.wait_ge(s_x1t, n)
                v.tensor_tensor(x1[:, :, :], bank.rearrange("p (t c) -> p t c", t=QUADS),
                                x_res[:, c * QUADS:(c + 1) * QUADS, :], ALU.add).then_inc(s_x1p, 1)

            def norm_stats_1(b, c):
                n = CHUNKS * b + c
                dve.wait_ge(s_x1p, n + 1)
                for i in range(QUADS):
                    v.bn_stats(stats[:, i, :], x1[:, i, :]).then_inc(s_st, 1)
                dve.wait_ge(s_st, QUADS * (n + 1))
                v.memset(scratch[:, :], 0.0)
                for i in range(QUADS):
                    v.bn_aggr(mean_var[:, i, :], stats[:, i, :]).then_inc(s_mv, 1)

            def layer_norm_1(b, c, bank):
                add_x(b, c, bank)
                norm_stats_1(b, c)

            def layer_norm_1_end(b, c):
                dve.wait_ge(s_rs, CHUNKS * b + c + 1)
                for i in range(QUADS):
                    ins = v.tensor_scalar(x1[:, i, :], x1[:, i, :], mean_var[:, i, 0:1], rstd[:, i:i + 1],
                                          ALU.subtract, ALU.mult)
                ins.then_inc(s_x1, 1)

            def bias_step(n):
                w = coef_up[0:1, :].rearrange("p (j i f) -> p i j f", i=2, f=2)
                y = y_bias[:, :].rearrange("p (o j f) -> p o j f", o=1, f=2)
                dve.wait_ge(s_cu, 16 * (n + 1))
                for f in range(2):
                    v.tensor_tensor(bias_term[:, f, :].rearrange("p (i j) -> p i j", i=2), w[:, :, :, f],
                                    y[:, :, :, f].to_broadcast([1, 2, HID // 2]), ALU.mult).then_inc(s_ub, 1)
                dve.wait_ge(s_ub, 3 * n + 2)
                v.tensor_tensor(y_bias[:, :], bias_term[:, 0, :], bias_term[:, 1, :], ALU.add).then_inc(s_ub, 1)
                dve.wait_ge(s_ub, 3 * n + 3)

            def down_step(n):
                w = coef_dn[:, :].rearrange("p (j i f) -> p i j f", i=2, f=2)
                y = y_dn[:, :].rearrange("p (i j o) -> p i j o", i=2, o=1)
                dve.wait_ge(s_wcc, 1)
                dve.wait_ge(s_cd, 16 * (n + 1))
                for i in range(2):
                    v.tensor_tensor(term_dve[i].rearrange("p (j f) -> p j f", f=2), w[:, i, :, :],
                                    y[:, i, :, :].to_broadcast([128, HID // 2, 2]), ALU.mult).then_inc(s_dn, 1)
                dve.wait_ge(s_dn, 3 * n + 2)
                v.tensor_tensor(y_dn[:, :], term_dve[0], term_dve[1], ALU.add).then_inc(s_dn, 1)
                dve.wait_ge(s_dn, 3 * n + 3)

            def m_lo(b):
                dve.wait_ge(s_mh, b + 1)
                lo(m_l[:, :, :].rearrange("p a c -> p (a c)"), pa[:, :],
                   m_h[:, :, :].rearrange("p a c -> p (a c)"), s_ml)

            def ksum_mask(b):
                dve.wait_ge(s_kcol, b + 1)
                v.tensor_tensor(ksum_cols[:, :, :], head_mask[:, :, :],
                                pa[:, 0:PAIRS].rearrange("p (a o) -> p a o", o=1).to_broadcast([128, PAIRS, 32]),
                                ALU.mult).then_inc(s_kcm, 1)

            def reciprocal(b):
                dve.wait_ge(s_ne, b + 1)
                v.reciprocal(recip[:, :], recip[:, :]).then_inc(s_r, 1)

            def recip_split(b, c):
                dve.wait_ge(s_rh, b + 1)
                for j in range(2 * c, 2 * c + 2):
                    rows = slice(32 * j, 32 * j + 32)
                    v.scalar_tensor_tensor(recip_parts[rows, j * QT:(j + 1) * QT], recip_h[rows, :].bitcast(fp32),
                                           part_b[rows, :], recip[rows, :], ALU.mult, ALU.add).then_inc(s_rp, 1)

            v.memset(wout_diag, 0.0).then_inc(s_zero, 1)
            wT_copy(2, 3, pz[:, CH:])
            xT_lo(0, 0, pa[:, 0:CH])
            for half, bank in enumerate([pc, pd]):
                cols = slice(half * CH, (half + 1) * CH)
                dve.wait_ge(s_wh, half + 1)
                lo(wk_l[:, cols], bank[:, :], wk_h[:, cols], s_wl)
            wT_copy(4, 1, pq[:, CH:])
            dve.wait_ge(s_bf, 48)
            k_bias(0, 0)
            xT_lo(0, 1, pa[:, CH:])
            wT_copy(6, 5, pq[:, CH:])
            wq_lf = wq_l[:, :, :].rearrange("p a m -> p (a m)")
            wq_hf = wq_h[:, :, :].rearrange("p a m -> p (a m)")
            for half, bank in enumerate([pc, pd]):
                cols = slice(half * CH, (half + 1) * CH)
                dve.wait_ge(s_wh, 3 + half)
                lo(wq_lf[:, cols], bank[:, :], wq_hf[:, cols], s_wl)
            k_bias(0, 1)
            vo_flat = vo[:, :, :].rearrange("p a m -> p (a m)")
            for n, bank in [(1, pq[:, CH:]), (3, pd[:, :])]:
                dve.wait_ge(s_fold, 5 + n)
                v.tensor_copy(vo_flat[:, n * CH:(n + 1) * CH], bank).then_inc(s_vod, 1)
            k_lo(0, 0)
            dve.wait_ge(s_const, 2)
            v.reduce_sum(row_head[:, :], ident[:, :].rearrange("p (k i) -> p i k", i=16),
                         axis=mybir.AxisListType.X).then_inc(s_row, 1)
            part_cols = ident[:, :].rearrange("p (k b i) -> p b k i", b=2, i=16)[:, 1, :, :]
            v.reduce_sum(row_part[:, :], part_cols, axis=mybir.AxisListType.XY).then_inc(s_row, 1)
            dve.wait_ge(s_wffn, 48)
            for s in range(2, TILES + 1):
                if s < TILES:
                    k_bias(0, s)
                k_lo(0, s - 1)
                if s % 2 == 0 and s // 2 < PRE:
                    bias_step(s // 2 - 1)
                if s % 2 and s // 2 < PRE:
                    down_step(s // 2 - 1)
            bias_step(PRE - 1)
            down_step(PRE - 1)
            dve.wait_ge(s_const, 7)
            ksum_mask(0)
            dve.wait_ge(s_part, 2)
            dve.wait_ge(s_bfh, 3)
            low_row = bf_rows[32:33, :].rearrange("p (h d) -> p h d", d=D)
            b_row, b_high = (r[32:33, :].rearrange("p (o d) -> p o d", o=1).to_broadcast([1, CH // D, D])
                             for r in (bf_row, bf_h.bitcast(fp32)))
            v.tensor_tensor(low_row, b_row, b_high, ALU.subtract).then_inc(s_bfl, 1)
            with v.Fori(0, BATCH - 1) as b:
                xT_lo(b + 1, 0, xT_banks[0])
                reciprocal(b)
                for s in range(SLOTS):
                    if s == FIRST:
                        recip_split(b, 0)
                        xT_lo(b + 1, 1, xT_banks[1])
                        normalise_q(b, 0)
                    if s < TILES:
                        k_bias(b + 1, s)
                    if s == FIRST:
                        m_lo(b)
                    for a in spreads(s - 1)[1:]:
                        qn_lo(b, a)
                    if s > FIRST:
                        for a in spreads(s)[:1]:
                            normalise_q(b, a)
                    if 1 <= s <= TILES:
                        k_lo(b + 1, s - 1)
                    for a in spreads(s)[1:]:
                        normalise_q(b, a)
                    if s == PART_SLOT:
                        recip_split(b, 1)
                    if s == TURN_SLOT:
                        layer_norm_1(b, 0, pd[:, :])
                layer_norm_1_end(b, 0)
                bias_step(PRE + PER_TURN * b)
                ksum_mask(b + 1)
                layer_norm_1(b, 1, pd[:, :])
                layer_norm_1_end(b, 1)
                for n in range(1, PER_TURN):
                    bias_step(PRE + PER_TURN * b + n)
            last_b = BATCH - 1

            def tokens(c):
                return x1T[:, c * CH:(c + 1) * CH] if isinstance(c, int) else x1T[:, bass.ds(c * CH, CH)]

            def split_x1(c, r):
                cols = slice(r * CH, (r + 1) * CH)
                dve.wait_ge(s_x1c, c + 1)
                if not isinstance(c, int) or c >= 2:
                    dve.wait_ge(s_h, HT * (c - 1))
                else:
                    dve.wait_ge(s_qp, BATCH * STEPS)
                v.tensor_copy(xT_h[:, cols], tokens(c)).then_inc(s_fxh, 1)
                dve.wait_ge(s_fxh, c + 1)
                lo(xT_l[:, cols], tokens(c), xT_h[:, cols], s_fxl)

            def hidden_lo_tile(c, r, i):
                dve.wait_ge(s_gh, 2 * c + i // 2 + 1)
                lo(tile_of(hid_l[r], i), tile_of(hid[r], i), tile_of(hid_h[r], i), s_gld)

            def hidden_lo(c, r):
                hidden_lo_tile(c, r, HT - 1)

            def residual(c, bank=pa[:, 0:CH], dst=yT):
                dve.wait_ge(s_dp, c + 1)
                v.scalar_tensor_tensor(dst, bank, bdn_col[:, :], tokens(c), ALU.add, ALU.add).then_inc(s_y, 1)

            def layer_norm_2(c, bank=pd):
                st, mv, _, _ = norm_buffers(c)
                dve.wait_ge(s_yt, c + 1)
                for i in range(QUADS):
                    v.bn_stats(st[:, i, :], bank[:, i * 128:(i + 1) * 128]).then_inc(s_st2, 1)
                dve.wait_ge(s_st2, QUADS * (c + 1))
                v.memset(scratch[:, :], 0.0)
                for i in range(QUADS):
                    v.bn_aggr(mv[:, i, :], st[:, i, :]).then_inc(s_mv2, 1)

            def layer_norm_2_end(c, r, bank=pd):
                _, mv, _, rs = norm_buffers(c)
                dve.wait_ge(s_rs2, c + 1)
                if not isinstance(c, int):
                    dve.wait_ge(s_out, 16 * c)
                elif c >= 2:
                    dve.wait_ge(s_out, 16 * (c - 1))
                for i in range(QUADS):
                    ins = v.tensor_scalar(y_out[r][:, i, :], bank[:, i * 128:(i + 1) * 128],
                                          mv[:, i, 0:1], rs[:, i:i + 1], ALU.subtract, ALU.mult)
                ins.then_inc(s_yo, 1)

            split_x1(0, 0)
            reciprocal(last_b)
            split_x1(1, 1)
            v.tensor_tensor(bdn_col[:, :], bcon_col[:, :], bdn_raw[:, :], ALU.add).then_inc(s_bc, 1)
            recip_split(last_b, 0)
            dve.wait_ge(s_bT, 1)
            v.tensor_tensor(bup_col[:, :], bup_raw[:, :], pz[:, 0:HT], ALU.add).then_inc(s_bc, 1)
            for s in range(FIRST, SLOTS):
                for a in spreads(s - 1)[1:]:
                    qn_lo(last_b, a)
                for a in spreads(s):
                    normalise_q(last_b, a)
                if s == FIRST:
                    m_lo(last_b)
                if s == FIRST + 1:
                    dve.wait_ge(s_wdh, 1)
                    lo(wdn_l[:, :, :].rearrange("p a c -> p (a c)"), pd[:, :],
                       wdn_h[:, :, :].rearrange("p a c -> p (a c)"), s_wdl)
                if s == PART_SLOT:
                    recip_split(last_b, 1)
                    hidden_lo(0, 0)
                if s == 4:
                    split_x1(2, 0)
                if s == 6:
                    hidden_lo(1, 1)
                if s == 7:
                    add_x(last_b, 0, pd[:, :])
                if s == 8:
                    norm_stats_1(last_b, 0)
            residual(0)
            layer_norm_1_end(last_b, 0)
            split_x1(3, 1)
            layer_norm_1(last_b, 1, pq[:, 0:CH])
            layer_norm_2(0)
            layer_norm_1_end(last_b, 1)
            hidden_lo(2, 0)
            residual(1)
            layer_norm_2_end(0, 0)
            with v.Fori(1, ALLCH // 2 - 1) as i:
                for r in range(2):
                    c = 2 * i + r
                    split_x1(c + 2, r)
                    layer_norm_2(c - 1)
                    hidden_lo(c + 1, 1 - r)
                    residual(c)
                    layer_norm_2_end(c - 1, 1 - r)
            layer_norm_2(ALLCH - 3)
            hidden_lo_tile(ALLCH - 1, 1, 1)
            hidden_lo_tile(ALLCH - 1, 1, 3)
            residual(ALLCH - 2)
            layer_norm_2_end(ALLCH - 3, 1)
            layer_norm_2(ALLCH - 2, pc)
            residual(ALLCH - 1, pa[:, CH:], yT_last)
            layer_norm_2(ALLCH - 1, pz)
            layer_norm_2_end(ALLCH - 2, 0, pc)
            layer_norm_2_end(ALLCH - 1, 1, pz)


_INS = ['L0_attn_x', 'L0_attn_W_qkv', 'L0_attn_W_f', 'L0_attn_b_f', 'L0_attn_W_out', 'L0_attn_b_out',
        'L0_ffn_W_exp', 'L0_ffn_b_exp', 'L0_ffn_up_weights', 'L0_ffn_up_bias', 'L0_ffn_down_weights',
        'L0_ffn_W_con', 'L0_ffn_b_con', 'L0_ffn_down_bias']


def kernel(**inputs):
    import numpy as _np
    import concourse.bacc as _bacc
    from concourse import mybir as _mybir
    from concourse.bass_utils import run_bass_kernel_spmd as _run

    nc = _bacc.Bacc("TRN2", target_bir_lowering=False, num_devices=1)
    arrays, args = {}, []
    for name in _INS:
        a = _np.ascontiguousarray(inputs[name])
        arrays[f"in_{name}_dram"] = a
        args.append(nc.dram_tensor(f"in_{name}_dram", a.shape, _mybir.dt.from_np(a.dtype), kind="ExternalInput").ap())
    shape = inputs['L0_attn_x'].shape
    args.append(nc.dram_tensor("out_0_dram", shape, _mybir.dt.from_np(_np.dtype('float32')), kind="ExternalOutput").ap())
    postln_linear_attention_butterfly_ffn_kernel(nc, *args)
    r = _run(nc, [arrays], core_ids=[0])
    return r.results[0]["out_0_dram"]
```
